# Optimizing a Trainium2 kernel written in Bass

```python
import numpy as np
import jax
import jax.numpy as jnp

def _softmax(x, axis=-1):
    return jax.nn.softmax(x, axis=axis)

def _gelu(x):
    return jax.nn.gelu(x, approximate=True)

def _silu(x):
    return jax.nn.silu(x)

def _sigmoid(x):
    return jax.nn.sigmoid(x)

def _layernorm(x, axis=-1, eps=1e-05):
    m = jnp.mean(x, axis=axis, keepdims=True)
    v = jnp.var(x, axis=axis, keepdims=True)
    return (x - m) / jnp.sqrt(v + eps)

def _scatter_add(tgt, idx, src, axis=0):
    return tgt.at[idx].add(src)

def _segment_sum(src, seg, n):
    return jax.ops.segment_sum(src, seg, n)
kernel_name = 'mk_conv_attn_hybrid_d4_conv_nhwc256_r4_23a715'

def setup_inputs(seed: int=0):
    np.random.seed(seed)
    _w = jnp.asarray

    def _rec_inputs():
        import jax
        import jax.numpy as jnp
        _gk = jax.random.key(seed)
        x = -0.0002928 + 1 * jax.random.normal(jax.random.fold_in(_gk, 1), (4, 16, 16, 64), jnp.float32)
        return x
    x = _rec_inputs()

    def _L0_conv_setup():
        import jax, jax.numpy as jnp
        import numpy as np
        B, H, W, C = (4, 16, 16, 64)
        D = C // 8
        key = jax.random.key(seed)
        ks = jax.random.split(key, 5)
        scale = lambda fan_in: 1.0 / np.sqrt(fan_in)
        return {'x': jax.random.normal(ks[0], (B, H, W, C), dtype=jnp.float32), 'wq': jax.random.normal(ks[1], (C, D), dtype=jnp.float32) * scale(C), 'bq': jnp.zeros((D,), dtype=jnp.float32), 'wk': jax.random.normal(ks[2], (C, D), dtype=jnp.float32) * scale(C), 'bk': jnp.zeros((D,), dtype=jnp.float32), 'wv': jax.random.normal(ks[3], (C, C), dtype=jnp.float32) * scale(C), 'bv': jnp.zeros((C,), dtype=jnp.float32), 'wo': jax.random.normal(ks[4], (C, C), dtype=jnp.float32) * scale(C), 'bo': jnp.zeros((C,), dtype=jnp.float32)}
    _L0_conv_all = _L0_conv_setup()
    _L0_conv_in = {k: v for k, v in _L0_conv_all.items() if k in ('wq', 'bq', 'wk', 'bk', 'wv', 'bv', 'wo', 'bo')}
    del _L0_conv_all

    def _L1_conv_setup():
        import jax, jax.numpy as jnp
        import numpy as np

        def _window_start(L, k):
            ns = k // 2
            i = jnp.arange(L)
            return jnp.maximum(i - ns, 0) + jnp.where(i + ns >= L, L - i - ns - 1, 0)

        def _neighborhood_attention(hidden_states, wq, bq, wk, bk, wv, bv, rpb):
            B, H, W, dim = hidden_states.shape
            heads = rpb.shape[0]
            k = (rpb.shape[1] + 1) // 2
            hd = dim // heads

            def proj(w, b):
                y = hidden_states @ w.T + b
                return y.reshape(B, H, W, heads, hd).transpose(0, 3, 1, 2, 4)
            q = proj(wq, bq) / jnp.sqrt(jnp.float32(hd))
            kl = proj(wk, bk)
            vl = proj(wv, bv)
            off = jnp.arange(k)
            ki = _window_start(H, k)[:, None] + off[None, :]
            kj = _window_start(W, k)[:, None] + off[None, :]

            def gather_nbhd(x):
                g = x[:, :, ki[:, :, None, None], kj[None, None, :, :], :]
                return g.transpose(0, 1, 2, 4, 3, 5, 6).reshape(B, heads, H, W, k * k, hd)
            kn = gather_nbhd(kl)
            vn = gather_nbhd(vl)
            pbi = ki - jnp.arange(H)[:, None] + (k - 1)
            pbj = kj - jnp.arange(W)[:, None] + (k - 1)
            bias = rpb[:, pbi[:, :, None, None], pbj[None, None, :, :]]
            bias = bias.transpose(0, 1, 3, 2, 4).reshape(heads, H, W, k * k)
            scores = jnp.einsum('bnijd,bnijkd->bnijk', q, kn) + bias[None]
            probs = jax.nn.softmax(scores, axis=-1)
            ctx = jnp.einsum('bnijk,bnijkd->bnijd', probs, vn)
            return ctx.transpose(0, 2, 3, 1, 4).reshape(B, H, W, dim)
        key = jax.random.key(seed)
        ks = jax.random.split(key, 5)
        B, H, W, dim = (2, 56, 56, 64)
        heads, k = (8, 7)
        s = 0.02
        return {'hidden_states': jax.random.normal(ks[0], (B, H, W, dim), jnp.float32), 'wq': jax.random.normal(ks[1], (dim, dim), jnp.float32) * s, 'bq': jnp.zeros((dim,), jnp.float32), 'wk': jax.random.normal(ks[2], (dim, dim), jnp.float32) * s, 'bk': jnp.zeros((dim,), jnp.float32), 'wv': jax.random.normal(ks[3], (dim, dim), jnp.float32) * s, 'bv': jnp.zeros((dim,), jnp.float32), 'rpb': jax.random.normal(ks[4], (heads, 2 * k - 1, 2 * k - 1), jnp.float32) * s}
    _L1_conv_all = _L1_conv_setup()
    _L1_conv_in = {k: v for k, v in _L1_conv_all.items() if k in ('wq', 'bq', 'wk', 'bk', 'wv', 'bv', 'rpb')}
    del _L1_conv_all

    def _L2_attn_setup():
        import jax, jax.numpy as jnp
        import numpy as np
        key = jax.random.key(seed)
        inputs = jax.random.normal(key, (8, 512, 64), dtype=jnp.float32)
        return {'inputs': inputs}
    _L2_attn_all = _L2_attn_setup()
    _L2_attn_in = {k: v for k, v in _L2_attn_all.items() if k in ()}
    del _L2_attn_all

    def _L2_ffn_setup():
        import math
        import jax, jax.numpy as jnp
        import numpy as np
        CAPACITY_FACTOR = 1.25
        TOP_K = 2
        LN_EPS = 1e-05

        def _layer_norm(x, gamma, beta):
            mu = jnp.mean(x, axis=-1, keepdims=True)
            var = jnp.var(x, axis=-1, keepdims=True)
            return (x - mu) * jax.lax.rsqrt(var + LN_EPS) * gamma + beta
        key = jax.random.key(seed)
        ks = jax.random.split(key, 4)
        B, S, D, F, E = (8, 1024, 64, 128, 8)
        x = jax.random.normal(ks[0], (B, S, D), dtype=jnp.float32)
        Wr = jax.random.normal(ks[1], (D, E), dtype=jnp.float32) / np.sqrt(D)
        br = jnp.zeros((E,), jnp.float32)
        W1 = jax.random.normal(ks[2], (E, D, F), dtype=jnp.float32) / np.sqrt(D)
        b1 = jnp.zeros((E, F), jnp.float32)
        W2 = jax.random.normal(ks[3], (E, F, D), dtype=jnp.float32) / np.sqrt(F)
        b2 = jnp.zeros((E, D), jnp.float32)
        gamma = jnp.ones((D,), jnp.float32)
        beta = jnp.zeros((D,), jnp.float32)
        return {'x': x, 'Wr': Wr, 'br': br, 'W1': W1, 'b1': b1, 'W2': W2, 'b2': b2, 'gamma': gamma, 'beta': beta}
    _L2_ffn_all = _L2_ffn_setup()
    _L2_ffn_in = {k: v for k, v in _L2_ffn_all.items() if k in ('Wr', 'br', 'W1', 'b1', 'W2', 'b2', 'gamma', 'beta')}
    del _L2_ffn_all

    def _L3_attn_setup():
        import jax, jax.numpy as jnp
        import numpy as np
        F_DIM = 64
        key = jax.random.key(seed)
        ks = jax.random.split(key, 8)
        B, S, F = (8, 512, F_DIM)
        scale = 1.0 / np.sqrt(F)
        return {'x': jax.random.normal(ks[0], (B, S, F), dtype=jnp.float32), 'att_w': jax.random.normal(ks[1], (3 * F,), dtype=jnp.float32) * scale, 'z_w': jax.random.normal(ks[2], (F, 2 * F), dtype=jnp.float32) * scale, 'z_b': jax.random.normal(ks[3], (F,), dtype=jnp.float32) * 0.01, 'r_w': jax.random.normal(ks[4], (F, 2 * F), dtype=jnp.float32) * scale, 'r_b': jax.random.normal(ks[5], (F,), dtype=jnp.float32) * 0.01, 'f_w': jax.random.normal(ks[6], (F, 2 * F), dtype=jnp.float32) * scale, 'f_b': jax.random.normal(ks[7], (F,), dtype=jnp.float32) * 0.01}
    _L3_attn_all = _L3_attn_setup()
    _L3_attn_in = {k: v for k, v in _L3_attn_all.items() if k in ('att_w', 'z_w', 'z_b', 'r_w', 'r_b', 'f_w', 'f_b')}
    del _L3_attn_all

    def _L3_ffn_setup():
        import math
        import jax, jax.numpy as jnp
        import numpy as np
        CAPACITY_FACTOR = 1.25
        key = jax.random.key(seed)
        ks = jax.random.split(key, 5)
        B, L, D, F, E = (8, 2048, 64, 256, 8)
        h = jax.random.normal(ks[0], (B, L, D), dtype=jnp.float32)
        gate_w = jax.random.normal(ks[1], (D, E), dtype=jnp.float32) * 0.02
        gate_b = jnp.zeros((E,), dtype=jnp.float32)
        w1 = jax.random.normal(ks[2], (E, D, F), dtype=jnp.float32) * (1.0 / math.sqrt(D))
        b1 = jnp.zeros((E, F), dtype=jnp.float32)
        w2 = jax.random.normal(ks[3], (E, F, D), dtype=jnp.float32) * (1.0 / math.sqrt(F))
        b2 = jnp.zeros((E, D), dtype=jnp.float32)
        return {'h': h, 'gate_w': gate_w, 'gate_b': gate_b, 'w1': w1, 'b1': b1, 'w2': w2, 'b2': b2}
    _L3_ffn_all = _L3_ffn_setup()
    _L3_ffn_in = {k: v for k, v in _L3_ffn_all.items() if k in ('gate_w', 'gate_b', 'w1', 'b1', 'w2', 'b2')}
    del _L3_ffn_all
    return {'x': x, 'L0_conv_wq': _L0_conv_in['wq'], 'L0_conv_bq': _L0_conv_in['bq'], 'L0_conv_wk': _L0_conv_in['wk'], 'L0_conv_bk': _L0_conv_in['bk'], 'L0_conv_wv': _L0_conv_in['wv'], 'L0_conv_bv': _L0_conv_in['bv'], 'L0_conv_wo': _L0_conv_in['wo'], 'L0_conv_bo': _L0_conv_in['bo'], 'L1_conv_wq': _L1_conv_in['wq'], 'L1_conv_bq': _L1_conv_in['bq'], 'L1_conv_wk': _L1_conv_in['wk'], 'L1_conv_bk': _L1_conv_in['bk'], 'L1_conv_wv': _L1_conv_in['wv'], 'L1_conv_bv': _L1_conv_in['bv'], 'L1_conv_rpb': _L1_conv_in['rpb'], 'L2_ffn_Wr': _L2_ffn_in['Wr'], 'L2_ffn_br': _L2_ffn_in['br'], 'L2_ffn_W1': _L2_ffn_in['W1'], 'L2_ffn_b1': _L2_ffn_in['b1'], 'L2_ffn_W2': _L2_ffn_in['W2'], 'L2_ffn_b2': _L2_ffn_in['b2'], 'L2_ffn_gamma': _L2_ffn_in['gamma'], 'L2_ffn_beta': _L2_ffn_in['beta'], 'L3_attn_att_w': _L3_attn_in['att_w'], 'L3_attn_z_w': _L3_attn_in['z_w'], 'L3_attn_z_b': _L3_attn_in['z_b'], 'L3_attn_r_w': _L3_attn_in['r_w'], 'L3_attn_r_b': _L3_attn_in['r_b'], 'L3_attn_f_w': _L3_attn_in['f_w'], 'L3_attn_f_b': _L3_attn_in['f_b'], 'L3_ffn_gate_w': _L3_ffn_in['gate_w'], 'L3_ffn_gate_b': _L3_ffn_in['gate_b'], 'L3_ffn_w1': _L3_ffn_in['w1'], 'L3_ffn_b1': _L3_ffn_in['b1'], 'L3_ffn_w2': _L3_ffn_in['w2'], 'L3_ffn_b2': _L3_ffn_in['b2']}

def reference(x, L0_conv_wq, L0_conv_bq, L0_conv_wk, L0_conv_bk, L0_conv_wv, L0_conv_bv, L0_conv_wo, L0_conv_bo, L1_conv_wq, L1_conv_bq, L1_conv_wk, L1_conv_bk, L1_conv_wv, L1_conv_bv, L1_conv_rpb, L2_ffn_Wr, L2_ffn_br, L2_ffn_W1, L2_ffn_b1, L2_ffn_W2, L2_ffn_b2, L2_ffn_gamma, L2_ffn_beta, L3_attn_att_w, L3_attn_z_w, L3_attn_z_b, L3_attn_r_w, L3_attn_r_b, L3_attn_f_w, L3_attn_f_b, L3_ffn_gate_w, L3_ffn_gate_b, L3_ffn_w1, L3_ffn_b1, L3_ffn_w2, L3_ffn_b2):
    import jax
    import jax.numpy as jnp

    def _L0_conv_ref(x, wq, bq, wk, bk, wv, bv, wo, bo):
        import jax, jax.numpy as jnp
        import numpy as np
        B, H, W, C = (4, 16, 16, 64)
        D = C // 8
        b, h, w, c = x.shape
        n = h * w
        xt = x.reshape(b, n, c)
        q = xt @ wq + bq
        k = xt @ wk + bk
        v = xt @ wv + bv
        scores = jnp.einsum('bnd,bmd->bnm', q, k) / jnp.sqrt(jnp.float32(k.shape[-1]))
        attn = jax.nn.softmax(scores, axis=-1)
        attended = jnp.einsum('bnm,bmc->bnc', attn, v)
        out = attended @ wo + bo
        return x + out.reshape(b, h, w, c)

    def _L1_conv_ref(hidden_states, wq, bq, wk, bk, wv, bv, rpb):
        import jax, jax.numpy as jnp
        import numpy as np

        def _window_start(L, k):
            ns = k // 2
            i = jnp.arange(L)
            return jnp.maximum(i - ns, 0) + jnp.where(i + ns >= L, L - i - ns - 1, 0)

        def _neighborhood_attention(hidden_states, wq, bq, wk, bk, wv, bv, rpb):
            B, H, W, dim = hidden_states.shape
            heads = rpb.shape[0]
            k = (rpb.shape[1] + 1) // 2
            hd = dim // heads

            def proj(w, b):
                y = hidden_states @ w.T + b
                return y.reshape(B, H, W, heads, hd).transpose(0, 3, 1, 2, 4)
            q = proj(wq, bq) / jnp.sqrt(jnp.float32(hd))
            kl = proj(wk, bk)
            vl = proj(wv, bv)
            off = jnp.arange(k)
            ki = _window_start(H, k)[:, None] + off[None, :]
            kj = _window_start(W, k)[:, None] + off[None, :]

            def gather_nbhd(x):
                g = x[:, :, ki[:, :, None, None], kj[None, None, :, :], :]
                return g.transpose(0, 1, 2, 4, 3, 5, 6).reshape(B, heads, H, W, k * k, hd)
            kn = gather_nbhd(kl)
            vn = gather_nbhd(vl)
            pbi = ki - jnp.arange(H)[:, None] + (k - 1)
            pbj = kj - jnp.arange(W)[:, None] + (k - 1)
            bias = rpb[:, pbi[:, :, None, None], pbj[None, None, :, :]]
            bias = bias.transpose(0, 1, 3, 2, 4).reshape(heads, H, W, k * k)
            scores = jnp.einsum('bnijd,bnijkd->bnijk', q, kn) + bias[None]
            probs = jax.nn.softmax(scores, axis=-1)
            ctx = jnp.einsum('bnijk,bnijkd->bnijd', probs, vn)
            return ctx.transpose(0, 2, 3, 1, 4).reshape(B, H, W, dim)
        return _neighborhood_attention(hidden_states, wq, bq, wk, bk, wv, bv, rpb)

    def _L2_attn_ref(inputs):
        import jax, jax.numpy as jnp
        import numpy as np
        d_k = jnp.asarray(inputs.shape[-1], dtype=inputs.dtype)
        scores = jnp.einsum('bnd,bmd->bnm', inputs, inputs) / jnp.sqrt(d_k)
        weights = jax.nn.softmax(scores, axis=-1)
        context = jnp.einsum('bnm,bmd->bnd', weights, inputs)
        return context

    def _L2_ffn_ref(x, Wr, br, W1, b1, W2, b2, gamma, beta):
        import math
        import jax, jax.numpy as jnp
        import numpy as np
        CAPACITY_FACTOR = 1.25
        TOP_K = 2
        LN_EPS = 1e-05

        def _layer_norm(x, gamma, beta):
            mu = jnp.mean(x, axis=-1, keepdims=True)
            var = jnp.var(x, axis=-1, keepdims=True)
            return (x - mu) * jax.lax.rsqrt(var + LN_EPS) * gamma + beta
        B, S, D = x.shape
        E = Wr.shape[1]
        N = B * S
        K = TOP_K
        logits = jnp.mean(x, axis=1) @ Wr + br
        routing_weights = jax.nn.softmax(logits, axis=-1)
        capacity = float(math.ceil(N * CAPACITY_FACTOR / E))
        expected_loads = routing_weights.sum(axis=0) * (N / B)
        scale = jnp.where(expected_loads > capacity, capacity / expected_loads, 1.0)
        routing_weights = jax.nn.softmax(routing_weights * scale, axis=-1)
        rw_tok = jnp.broadcast_to(routing_weights[:, None, :], (B, S, E)).reshape(N, E)
        top_w, top_i = jax.lax.top_k(rw_tok, K)
        top_w = jax.nn.softmax(top_w, axis=-1)
        xf = x.reshape(N, D)
        h = jax.nn.gelu(jnp.einsum('nd,edf->enf', xf, W1) + b1[:, None, :], approximate=False)
        y = jnp.einsum('enf,efd->end', h, W2) + b2[:, None, :]
        w_dense = jnp.zeros((N, E), x.dtype).at[jnp.arange(N)[:, None], top_i].add(top_w)
        out = jnp.einsum('ne,end->nd', w_dense, y).reshape(B, S, D)
        out = _layer_norm(out + x, gamma, beta)
        return out

    def _L3_attn_ref(x, att_w, z_w, z_b, r_w, r_b, f_w, f_b):
        import jax, jax.numpy as jnp
        import numpy as np
        F_DIM = 64
        F = x.shape[-1]
        wa, wb, wc = (att_w[:F], att_w[F:2 * F], att_w[2 * F:])
        a = jnp.einsum('bif,f->bi', x, wa)
        b = jnp.einsum('bjf,f->bj', x, wb)
        c = jnp.einsum('bif,bjf->bij', x * wc, x)
        scores = a[:, :, None] + b[:, None, :] + c
        attn_weight = jax.nn.softmax(scores, axis=2)
        attn = jnp.einsum('bij,bjf->bif', attn_weight, x)
        cat = jnp.concatenate([x, attn], axis=-1)
        z = jnp.tanh(jnp.einsum('bsg,fg->bsf', cat, z_w) + z_b)
        r = jax.nn.sigmoid(jnp.einsum('bsg,fg->bsf', cat, r_w) + r_b)
        f = jax.nn.sigmoid(jnp.einsum('bsg,fg->bsf', cat, f_w) + f_b)
        return r * x + f * z

    def _L3_ffn_ref(h, gate_w, gate_b, w1, b1, w2, b2):
        import math
        import jax, jax.numpy as jnp
        import numpy as np
        CAPACITY_FACTOR = 1.25
        B, L, D = h.shape
        E = gate_w.shape[1]
        T = B * L
        C = max(1, math.ceil(CAPACITY_FACTOR * T / E))
        x = h.reshape(T, D)
        logits = x @ gate_w + gate_b
        probs = jax.nn.softmax(logits, axis=-1)
        idx = jnp.argmax(probs, axis=-1)
        prb = jnp.take_along_axis(probs, idx[:, None], axis=1)[:, 0]
        one_hot = jax.nn.one_hot(idx, E, dtype=jnp.float32)
        pos = (jnp.cumsum(one_hot, axis=0) * one_hot).sum(-1).astype(jnp.int32) - 1
        kept = pos < C
        pos_safe = jnp.where(kept, pos, C)
        buf = jnp.zeros((E, C, D), dtype=h.dtype).at[idx, pos_safe].set(x, mode='drop')
        hmid = jax.nn.relu(jnp.einsum('ecd,edf->ecf', buf, w1) + b1[:, None, :])
        ybuf = jnp.einsum('ecf,efd->ecd', hmid, w2) + b2[:, None, :]
        pos_g = jnp.minimum(pos, C - 1)
        y_tok = ybuf[idx, pos_g] * (prb * kept)[:, None]
        y = y_tok.reshape(B, L, D)
        y = jnp.nan_to_num(y, nan=0.0, posinf=10000.0, neginf=-10000.0)
        return y

    def _gn(v, G=32, eps=1e-05):
        B_, H_, W_, C_ = v.shape
        g = v.reshape(B_, H_, W_, G, C_ // G)
        m = jnp.mean(g, axis=(1, 2, 4), keepdims=True)
        s = jnp.var(g, axis=(1, 2, 4), keepdims=True)
        return ((g - m) / jnp.sqrt(s + eps)).reshape(v.shape)

    def _ln_c(v, eps=1e-06):
        m = jnp.mean(v, axis=-1, keepdims=True)
        s = jnp.var(v, axis=-1, keepdims=True)
        return (v - m) / jnp.sqrt(s + eps)

    def _ln_t(v, eps=1e-05):
        m = jnp.mean(v, axis=-1, keepdims=True)
        s = jnp.var(v, axis=-1, keepdims=True)
        return (v - m) / jnp.sqrt(s + eps)

    def _to_tokens(v):
        B_, H_, W_, C_ = v.shape
        return v.reshape(B_, H_ * W_, C_)

    def _from_tokens(t, like):
        return t.reshape(like.shape)
    x = _L0_conv_ref(x, L0_conv_wq, L0_conv_bq, L0_conv_wk, L0_conv_bk, L0_conv_wv, L0_conv_bv, L0_conv_wo, L0_conv_bo)
    x = x + _L1_conv_ref(_gn(x), L1_conv_wq, L1_conv_bq, L1_conv_wk, L1_conv_bk, L1_conv_wv, L1_conv_bv, L1_conv_rpb)
    t = _to_tokens(x)
    t = t + _L2_attn_ref(_ln_t(t))
    t = t + _L2_ffn_ref(_ln_t(t), L2_ffn_Wr, L2_ffn_br, L2_ffn_W1, L2_ffn_b1, L2_ffn_W2, L2_ffn_b2, L2_ffn_gamma, L2_ffn_beta)
    t = t + _L3_attn_ref(_ln_t(t), L3_attn_att_w, L3_attn_z_w, L3_attn_z_b, L3_attn_r_w, L3_attn_r_b, L3_attn_f_w, L3_attn_f_b)
    t = t + _L3_ffn_ref(_ln_t(t), L3_ffn_gate_w, L3_ffn_gate_b, L3_ffn_w1, L3_ffn_b1, L3_ffn_w2, L3_ffn_b2)
    x = _from_tokens(t, x)
    return x

_drawn_inputs = setup_inputs


def setup_inputs(seed=0):
    import zlib

    import numpy as np

    out = dict(_drawn_inputs(seed))
    spreads = {'L0_conv_bq': (0.0, 0.375),
     'L0_conv_bk': (0.0, 2.0),
     'L0_conv_bv': (0.0, 0.1),
     'L0_conv_bo': (0.0, 0.1),
     'L1_conv_bq': (0.0, 0.8),
     'L1_conv_bk': (0.0, 2.0),
     'L1_conv_bv': (0.0, 0.1),
     'L2_ffn_br': (0.0, 0.1),
     'L2_ffn_b1': (0.0, 0.468),
     'L2_ffn_b2': (0.0, 0.308),
     'L2_ffn_gamma': (1.0, 0.2),
     'L2_ffn_beta': (0.0, 0.1),
     'L3_ffn_gate_b': (0.0, 0.29),
     'L3_ffn_b1': (0.0, 2.0),
     'L3_ffn_b2': (0.0, 2.0)}
    factors = {'L1_conv_wq': 8.0,
     'L1_conv_wk': 8.0,
     'L1_conv_rpb': 64.0,
     'L3_attn_z_b': 42.622,
     'L3_attn_r_b': 64.0,
     'L3_attn_f_b': 64.0,
     'L3_ffn_w1': 3.333}
    for name, (base, spread) in spreads.items():
        noise = np.random.default_rng([zlib.crc32(name.encode()), seed]).standard_normal(out[name].shape)
        drawn = base * np.exp(spread * noise) if base else spread * noise
        out[name] = jnp.asarray(drawn.astype(out[name].dtype))
    for name, factor in factors.items():
        out[name] = (out[name] * factor).astype(out[name].dtype)
    return out
```

```python
from contextlib import ExitStack

import numpy as np
import concourse.bass as bass
from concourse import mybir

P = 128
B, HW, C = 4, 16, 64
N = HW * HW
TB = N // P
T = B * TB
C1 = C + 1
D0 = C // 8
NH, HD, WIN = 8, 8, 7
SPAN = (P // HW + WIN // 2) * HW
OFF = (0, N - SPAN)
NT = 9
KS = NT * HD
VW = 32
MASKED = -1e30
E2, F2, TOPK = 8, 128, 2
CAP2 = float(-(-B * N * 5 // (4 * E2)))
E3, F3 = 8, 256
CAP3 = -(-B * N * 5 // (4 * E3))
SLOTS = E3 * CAP3
LN_EPS = 1e-5
FLT_MAX = 3.4028234663852886e38

F32, F32R, BF16, I32, U32 = (mybir.dt.float32, mybir.dt.float32r, mybir.dt.bfloat16,
                             mybir.dt.int32, mybir.dt.uint32)
ALU = mybir.AluOpType
ACT = mybir.ActivationFunctionType
AX = mybir.AxisListType


def window_start(i):
    return min(max(i - WIN // 2, 0), HW - WIN)


def columns(*pairs):
    at, where = 0, {}
    for name, width in pairs:
        where[name] = slice(at, at + width)
        at += width
    return where, at


CST, CST_W = columns(("ident", P), ("prefix", P), ("pair", C), ("rev", T * E3), ("scale", 1),
                     ("first", T * E3), ("slot", 10))
W0, W0_W = columns(("wvT", C1), ("wo", C), ("wqk1", 2 * C), ("wv1", C))
WA, WA_W = columns(("w1", E2 * F2), ("wr", E2), ("b2", E2), ("y3", C1), ("gx", 3 * C), ("ga", 3 * C),
                   ("gate", E3), ("fb2", E3))


def hybrid_kernel(nc, x, w8, w0, wa, w3, w2a, w2b, cst, bias_q, bias_k, lnw, out):
    ctx = ExitStack()
    with ctx:
        def sb(name, shape, dt=F32):
            return ctx.enter_context(nc.sbuf_tensor(name, shape, dt))

        sems = {}

        def sem(name):
            if name not in sems:
                sems[name] = ctx.enter_context(nc.semaphore(name))
            return sems[name]

        bank = [ctx.enter_context(nc.psum_tensor(f"bank{i}", [P, 512], F32)) for i in range(8)]

        q_parts = nc.dram_tensor("q_parts", (B, 3, HD, NH, N), BF16, kind="Internal").ap()
        k_parts = nc.dram_tensor("k_parts", (B, HD, 3, NH, N), BF16, kind="Internal").ap()

        W8 = sb("W8", [D0, 2 * C1])
        W0s = sb("W0s", [C1, W0_W])
        Cs = sb("Cs", [P, CST_W])
        identb = sb("identb", [P, P], BF16)
        onesb = sb("onesb", [P, P], BF16)
        bias_mem = sb("bias_mem", [P, 2 * NH * TB * SPAN])
        mid_mem = sb("mid_mem", [P, 7232])
        half_mem = sb("half_mem", [P, 4992])
        stack_mem = sb("stack_mem", [P, B * NH * N])
        taken = {}

        def view(mem, *shape):
            at = taken.get(id(mem), 0)
            size = int(np.prod(shape[1:]))
            taken[id(mem)] = at + size
            v = mem[0:shape[0], at:at + size]
            if len(shape) == 3:
                return v.rearrange("p (a b) -> p a b", a=shape[1])
            return v.rearrange("p (a b c) -> p a b c", a=shape[1], b=shape[2]) if len(shape) == 4 else v

        def view16(mem, *shape):
            at = taken.get(id(mem), 0)
            size = int(np.prod(shape[1:])) // 2
            taken[id(mem)] = at + size
            v = mem[0:shape[0], at:at + size].bitcast(BF16)
            if len(shape) == 3:
                return v.rearrange("p (a b) -> p a b", a=shape[1])
            return v.rearrange("p (a b c) -> p a b c", a=shape[1], b=shape[2]) if len(shape) == 4 else v

        biasQb = view16(half_mem, P, NH, TB * SPAN)
        biasQ = view(bias_mem, P, NH, TB * SPAN)
        biasK = view(bias_mem, P, NH, TB * SPAN)
        mhalf = sb("mhalf", [P, T])
        ident = Cs[:, CST["ident"]]

        X = sb("X", [P, T, C1])
        XT = sb("XT", [C1, B * N])
        A0 = sb("A0", [C1, C1])
        Wvo = sb("Wvo", [C1, C])
        G0 = sb("G0", [C1, B * N])
        S_P = sb("S_P", [P, B, TB, N])
        S_PT = sb("S_PT", [P, B, TB, N])
        nmax = sb("nmax", [P, T])
        den = sb("den", [P, T])
        rden = sb("rden", [P, T])
        CT = sb("CT", [C1, B * N])
        X1 = sb("X1", [P, T, C])

        gn_st = sb("gn_st", [C, B, 6])
        gn_mv = sb("gn_mv", [C, B, 3])
        gn_g = sb("gn_g", [C, B, 3])
        gn_v = sb("gn_v", [C, B])
        gn_sq = sb("gn_sq", [C, B])
        gn_r = sb("gn_r", [C, B])
        gn_nb = sb("gn_nb", [C, B])
        XN1 = sb("XN1", [C1, B * N])
        QK = view(mid_mem, P, B * N)
        qkr = view(mid_mem, P, B * N)
        part = [view16(half_mem, P, B * N) for i in range(3)]
        words = B * NH * N // 2
        QS, KSt = [stack_mem[0:KS, k * words:(k + 1) * words].bitcast(BF16)
                   .rearrange("r (b h n) -> r b h n", b=B, h=NH) for k in range(2)]
        V1 = view(mid_mem, P, T, NH, VW)
        nm1 = sb("nm1", [P, B, NH, TB], BF16)
        diag1 = view16(half_mem, P, 2, NH, TB * P)
        U1 = view(mid_mem, P, 3, TB * SPAN)
        P1 = view(mid_mem, P, 3, TB * SPAN)
        CT1 = view(mid_mem, P, 2, 512)
        rz1 = sb("rz1", [P, 2, TB * 2, 4])
        ctx1 = sb("ctx1", [P, 2, TB * 2, 4, HD])
        X2 = sb("X2", [P, T, C])

        taken.clear()
        LN = "abucd"
        LN_STEPS = [("a", TB * b, TB) for b in range(B)] + \
                   [(s, h * T // 2, T // 2) for s in "bucd" for h in range(2)]
        ln_st = {s: sb("ln_st" + s, [P, T, 6]) for s in LN}
        ln_mv = {s: sb("ln_mv" + s, [P, T, 2]) for s in LN}
        ln_ve = {s: sb("ln_ve" + s, [P, T]) for s in LN}
        ln_rs = {s: sb("ln_rs" + s, [P, T]) for s in LN}
        XN = {s: sb("XN" + s, [P, T, C1]) for s in "abc"}
        XF = {s: sb("XF" + s, [C1, B * N]) for s in "ab"}
        XN["u"], XN["d"] = XN["a"], XN["b"]
        XF["c"], XF["d"] = XF["a"], XF["b"]
        LHSa = XT
        LHSc = G0
        CTa = XN1[0:C, :]
        CTc = CT
        nmaxa = sb("nmaxa", [P, T])
        dena = sb("dena", [P, T])
        rdena = sb("rdena", [P, T])
        nmaxc = sb("nmaxc", [P, T])
        denc = sb("denc", [P, T])
        rdenc = sb("rdenc", [P, T])
        X3 = sb("X3", [P, T, C])
        WAs = sb("WAs", [C1, WA_W])
        W2A = view(half_mem, P, E2, C)
        msum = sb("msum", [C, B])
        mean2 = sb("mean2", [C1, B])
        lg = sb("lg", [B, 8, E2])
        col = sb("col", [B, 10])
        top_i = sb("top_i", [B, 8], U32)
        spread = sb("spread", [B, 2, B, TOPK])
        loads1 = sb("loads1", [B, B])
        ones4 = sb("ones4", [B, P])
        tw = sb("tw", [P, B * TOPK])
        slot_e = sb("slot_e", [1, B * TOPK], I32)
        W1sel = view(stack_mem, C1, B * TOPK, F2)
        W2sel = view(stack_mem, P, B * TOPK, C)
        b2sel = sb("b2sel", [C, B, TOPK])
        H2 = view(bias_mem, P, B, TOPK * N)
        UT = view(half_mem, C, B * N)
        U = view(mid_mem, P, T, C)
        gb = sb("gb", [P, 2, C])
        X3b = view(mid_mem, P, T, C)
        un = view(stack_mem, P, T, C)
        X4 = view(half_mem, P, T, C)
        th = view(stack_mem, P, T, 3 * C)
        gm = view(stack_mem, P, T, 2 * C)
        gs = sb("gs", [P, T, C])
        X5 = view(bias_mem, P, T, C)
        W3s = view(mid_mem, C1, E3, F3)
        W2B = view(mid_mem, P, E3, 2, C)
        mx3 = sb("mx3", [P, T])
        d3 = sb("d3", [P, T, E3])
        ex3 = sb("ex3", [P, T, E3])
        prb = sb("prb", [P, T])
        se3 = sb("se3", [P, T])
        rv3 = sb("rv3", [P, T, E3])
        mr3 = sb("mr3", [P, T])
        oh3 = sb("oh3", [P, T, E3])
        ohb = sb("ohb", [P, T, E3], BF16)
        prefixb = sb("prefixb", [P, P], BF16)
        sel3 = sb("sel3", [P, 2, T, E3])
        cf3 = sb("cf3", [P, 2, T])
        kept = sb("kept", [P, T])
        gate3 = sb("gate3", [P, T])
        sid = sb("sid", [P, T])
        iota_f = view(half_mem, P, SLOTS)
        XH = sb("XH", [P, T, C], F32R)
        XL = sb("XL", [P, T, C], F32R)
        G3 = sb("G3", [P, 2, SLOTS], F32R)
        XB = view(stack_mem, C1, SLOTS)
        H3 = view(bias_mem, P, 3, 2, CAP3)
        YT = view(stack_mem, C, SLOTS)
        YH = sb("YH", [P, SLOTS // P, C], F32R)
        YL = sb("YL", [P, SLOTS // P, C], F32R)
        onesf = sb("onesf", [P, P])
        SD = view(bias_mem, P, T, P)
        SB = view(bias_mem, P, T * P)
        GT = sb("GT", [P, 2, T * P], F32R)
        ZT = view(mid_mem, C, B * N)
        y3 = view(mid_mem, P, T, C)
        sat3 = view(mid_mem, P, T, C)
        nan3 = view(mid_mem, P, T, C)
        fin3 = sb("fin3", [P, T, C], I32)
        Y6 = view(mid_mem, P, T, C)

        def through(s):
            return B if s == "c" else 0

        block = ctx.enter_context(nc.Block())

        x_t = x.rearrange("b (q p) c -> b p q c", p=P)
        o_t = out.rearrange("b (q p) c -> b p q c", p=P)

        def final(sp):
            for b in range(B):
                sp.wait_ge(sem("y6"), b + 1)
                sp.dma_start(o_t[b], Y6[:, TB * b:TB * b + TB, :]).then_inc(sem("out_stored"), 16)
            sp.wait_ge(sem("out_stored"), 16 * B)

        @block.sync
        def _(sp):
            sp.dma_start(X[:, 0:TB, 0:C], x_t[0]).then_inc(sem("x_landed0"), 16)
            sp.dma_start(Cs[:, :], cst).then_inc(sem("cst_landed"), 16)
            for b in range(1, B):
                sp.dma_start(X[:, TB * b:TB * b + TB, 0:C], x_t[b]).then_inc(sem(f"x_landed{b}"), 16)
            sp.dma_start(biasQ[:, :, :], bias_q).then_inc(sem("biasQ_landed"), 16)
            sp.dma_start(biasK[:, :, :], bias_k).then_inc(sem("biasK_landed"), 16)
            sp.dma_start(WAs[:, :], wa).then_inc(sem("wa_landed"), 16)
            for b in range(B):
                cols = slice(b * N, b * N + N)
                for i in range(3):
                    sp.wait_ge(sem("qk_part"), 3 * b + i + 1)
                    sp.dma_start(q_parts[b, i].rearrange("d h n -> h d n"), part[i][0:C, cols]) \
                        .then_inc(sem(f"q_parts_stored{b}"), 16)
                    sp.dma_start(k_parts[b, :, i].rearrange("d h n -> h d n"), part[i][C:2 * C, cols]) \
                        .then_inc(sem(f"k_parts_stored{b}"), 16)
                sp.wait_ge(sem(f"q_parts_stored{b}"), 48)
                for i in range(3):
                    sp.dma_start(QS[24 * i:24 * i + 24, b, :, :].rearrange("r h n -> r (h n)"),
                                 q_parts[b, i].rearrange("d h n -> d (h n)").unsqueeze(1)
                                 .to_broadcast([HD, 3, NH * N])).then_inc(sem(f"stack_landed{b}"), 16)
                sp.wait_ge(sem(f"k_parts_stored{b}"), 48)
                for i in range(3):
                    sp.dma_start(KSt[24 * i:24 * i + 24, b, :, :].rearrange("r h n -> r (h n)"),
                                 k_parts[b].rearrange("d j h n -> (d j) (h n)")).then_inc(sem(f"stack_landed{b}"), 16)
            sp.wait_ge(sem("x2_done"), B)
            sp.dma_start(W2A[:, :, :], w2a).then_inc(sem("w2a_landed"), 16)
            sp.dma_start(gb[:, :, :], lnw.unsqueeze(0).to_broadcast([P, 2, C])).then_inc(sem("gb_landed"), 16)
            sp.dma_start(W3s[:, :, :], w3).then_inc(sem("w3_landed"), 16)
            sp.dma_start(W2B[:, :, :, :], w2b).then_inc(sem("w2b_landed"), 16)
            final(sp)

        @block.gpsimd
        def _(pool):
            pool.memset(XT[C:C1, :], 1.0).then_inc(sem("ones_xt"), 1)
            pool.wait_ge(sem("ones_xt"), 1)
            pool.memset(X[:, :, C:C1], 1.0).then_inc(sem("ones_x"), 1)
            pool.wait_ge(sem("ones_x"), 1)
            pool.memset(XN1[C:C1, :], 1.0).then_inc(sem("pool_const"), 1)
            pool.wait_ge(sem("pool_const"), 1)
            pool.memset(mhalf[:, :], -0.5).then_inc(sem("pool_const"), 1)
            pool.memset(onesb[:, :], 1.0).then_inc(sem("pool_const"), 1)
            pool.memset(V1[:, :, :, HD:VW], 0.0).then_inc(sem("v1_zero"), 1)
            pool.wait_ge(sem("v1_zero"), 1)
            pool.memset(V1[:, :, :, HD:HD + 1], 1.0).then_inc(sem("pool_const"), 1)
            pool.wait_ge(sem("cst_landed"), 16)
            pool.tensor_copy(identb[:, :], ident).then_inc(sem("identb"), 1)
            pool.wait_ge(sem("biasQ_landed"), 16)
            pool.tensor_copy(biasQb[:, :, :], biasQ[:, :, :]).then_inc(sem("biasQb"), 1)
            for k, (tile, value) in enumerate([
                    (XN["c"][:, :, C:C1], 1.0), (onesf[:, :], 1.0), (XF["a"][C:C1, :], 1.0),
                    (XF["b"][C:C1, :], 1.0),
                    (mean2[C:C1, :], 1.0), (ones4[:, :], 1.0), (loads1[:, :], float(N))]):
                if k:
                    pool.wait_ge(sem("later_const"), k)
                pool.memset(tile, value).then_inc(sem("later_const"), 1)
            pool.tensor_copy(prefixb[:, :], Cs[:, CST["prefix"]]).then_inc(sem("prefixb"), 1)
            pool.wait_ge(sem("gn_var"), 1)
            pool.tensor_tensor(gn_r[:, :], gn_v[:, :], mhalf[0:C, 0:B], ALU.pow).then_inc(sem("gn_rstd"), 1)
            def rstd(s, half=0):
                n = LN_STEPS.index((s, half * T // 2, T // 2) if s != "a" else (s, TB * half, TB))
                t = slice(LN_STEPS[n][1], LN_STEPS[n][1] + LN_STEPS[n][2])
                pool.wait_ge(sem("ln_mv"), n + 1)
                pool.tensor_scalar(ln_ve[s][:, t], ln_mv[s][:, t, 1], LN_EPS, None, ALU.add).then_inc(sem("ln_ve"), 1)
                pool.wait_ge(sem("ln_ve"), n + 1)
                pool.tensor_tensor(ln_rs[s][:, t], ln_ve[s][:, t], mhalf[:, t], ALU.pow).then_inc(sem("ln_rs"), 1)

            for b in range(B):
                for h in range(NH):
                    pool.wait_ge(sem("nm1"), b * NH + h + 1)
                    if b >= 2:
                        pool.wait_ge(sem("s1"), (b - 2) * NH + h + 1)
                    pool.tensor_tensor(
                        diag1[:, b % 2, h, :].rearrange("p (q k) -> p q k", q=TB),
                        identb[:, :].unsqueeze(1).to_broadcast([P, TB, P]),
                        nm1[:, b, h, :].unsqueeze(2).to_broadcast([P, TB, P]), ALU.mult) \
                        .then_inc(sem("diag1"), 1)
                    if h == 4 and b >= 2:
                        rstd("a", b - 2)
            for b in range(2, B):
                rstd("a", b)
            pool.wait_ge(sem("x2_done"), B)
            pool.iota(iota_f[:, :], [[1, SLOTS]], base=0, channel_multiplier=0,
                      allow_small_or_imprecise_dtypes=True).then_inc(sem("iota_f"), 1)
            for half in range(2):
                rstd("b", half)
            pool.wait_ge(sem("gb_landed"), 16)
            pool.tensor_tensor(X3b[:, :, :], X3[:, :, :], gb[:, 1, :].unsqueeze(1).to_broadcast([P, T, C]), ALU.add) \
                .then_inc(sem("x3b"), 1)
            for half in range(2):
                rstd("u", half)
            for half in range(2):
                rstd("c", half)
            pool.wait_ge(sem("x5"), B)
            pool.memset(XB[C:C1, :], 1.0).then_inc(sem("xb_ones"), 1)
            pool.wait_ge(sem("xb_ones"), 1)
            for half in range(2):
                rstd("d", half)

        @block.tensor
        def _(pe):
            pe.wait_ge(sem("w8_landed"), 16)
            pe.matmul(bank[6][0:C1, 0:C1], W8[:, 0:C1], W8[:, C1:2 * C1], start=True, stop=True) \
                .then_inc(sem("a0"), 1)
            pe.wait_ge(sem("w0_landed"), 16)
            pe.matmul(bank[7][0:C1, 0:C], W0s[:, W0["wvT"]], W0s[:, W0["wo"]], start=True, stop=True) \
                .then_inc(sem("wvo"), 1)
            pe.wait_ge(sem("cst_landed"), 16)

            def transposes(b, src, ready, count, done):
                pe.wait_ge(sem(ready), count)
                for q in range(TB):
                    last = pe.transpose(bank[b][0:C, q * P:q * P + P], src[:, TB * b + q, 0:C], ident)
                last.then_inc(sem(done), 1)

            def scores(b, lhs, rhs):
                for q in range(TB):
                    last = pe.matmul(bank[4 + b % 2][:, q * N:q * N + N], lhs[:, b * N + q * P:b * N + q * P + P],
                                     rhs[:, b * N:b * N + N], start=True, stop=True)
                return last

            def transpose_p(b):
                for k in range(TB):
                    for q in range(TB):
                        last = pe.transpose(bank[6 + b % 2][:, k * N + q * P:k * N + q * P + P],
                                            S_P[:, b, q, k * P:k * P + P], ident)
                return last

            def attend(b, values, width):
                for k in range(TB):
                    last = pe.matmul(bank[2 + b % 2][0:width, 0:N], values[:, TB * b + k, 0:width],
                                     S_PT[:, b, k, :], start=(k == 0), stop=(k == TB - 1))
                return last

            for b in range(B):
                pe.wait_ge(sem("x_landed" + str(b)), 16)
                if b == 0:
                    pass
                for q in range(TB):
                    last = pe.transpose(bank[b % 2][0:C, q * P:q * P + P] if b < 2 else
                                        bank[b][0:C, q * P:q * P + P], X[:, TB * b + q, 0:C], ident)
                last.then_inc(sem("xt_p"), 1)
            for b in range(B):
                pe.wait_ge(sem("xt"), b + 1)
                if b == 0:
                    pe.wait_ge(sem("ones_xt"), 1)
                    pe.wait_ge(sem("a0_s"), 1)
                if b >= 2:
                    pe.wait_ge(sem("xt"), 4)
                pe.matmul(bank[b][0:C1, 0:N], A0[:, :], XT[:, b * N:b * N + N], start=True, stop=True) \
                    .then_inc(sem("g0_p"), 1)
            for i in range(B + 3):
                if i < B:
                    pe.wait_ge(sem("g0"), i + 1)
                    if i >= 2:
                        pe.wait_ge(sem("exp0"), 2 * (i - 1))
                    scores(i, G0, XT).then_inc(sem("s0"), 1)
                if 0 <= i - 1 < B:
                    b = i - 1
                    pe.wait_ge(sem("exp0"), 2 * b + 2)
                    if b == 0:
                        pe.wait_ge(sem("a0_s"), 1)
                        pe.wait_ge(sem("wvo_s"), 1)
                    if b >= 2:
                        pe.wait_ge(sem("pt0"), b - 1)
                    transpose_p(b).then_inc(sem("pt0_p"), 1)
                if 0 <= i - 2 < B:
                    b = i - 2
                    pe.wait_ge(sem("pt0"), b + 1)
                    if b == 0:
                        pe.wait_ge(sem("ones_x"), 1)
                        pe.wait_ge(sem("g0"), 4)
                    if b >= 2:
                        pe.wait_ge(sem("ct0"), b - 1)
                    attend(b, X, C1).then_inc(sem("ct0_p"), 1)
                if 0 <= i - 3 < B:
                    b = i - 3
                    pe.wait_ge(sem("ct0"), b + 1)
                    if b >= 2:
                        pe.wait_ge(sem("x1"), b - 1)
                    for q in range(TB):
                        last = pe.matmul(bank[b % 2][:, q * C:q * C + C], CT[:, b * N + q * P:b * N + q * P + P],
                                         Wvo[:, :], start=True, stop=True)
                    last.then_inc(sem("o0"), 1)

            for b in range(B):
                pe.wait_ge(sem("x1"), b + 1)
                for q in range(TB):
                    last = pe.transpose(bank[4 + b][0:C, q * P:q * P + P], X1[:, TB * b + q, :], ident)
                last.then_inc(sem("x1t_p"), 1)
            pe.wait_ge(sem("gn_mv"), 1)
            pe.matmul(bank[0][0:C, 0:3 * B], Cs[0:C, CST["pair"]], gn_mv[:, :, :].rearrange("c b k -> c (b k)"),
                      start=True, stop=True).then_inc(sem("gn_pair"), 1)
            for b in range(B):
                pe.wait_ge(sem("xn1"), b + 1)
                if b == 0:
                    pe.wait_ge(sem("pool_const"), 4)
                pe.matmul(bank[b][:, 0:N], W0s[:, W0["wqk1"]], XN1[:, b * N:b * N + N], start=True, stop=True) \
                    .then_inc(sem("qk_p"), 1)
            pe.wait_ge(sem("xn1"), B)
            for t in range(T):
                last = pe.matmul(bank[4][:, t * C:t * C + C], XN1[:, t * P:t * P + P], W0s[:, W0["wv1"]],
                                 start=True, stop=True)
            last.then_inc(sem("v1_p"), 1)

            def max_scores(b, h):
                n = b * NH + h
                if h == 0:
                    pe.wait_ge(sem(f"stack_landed{b}"), 6 * 16)
                    if b == 0:
                        pe.wait_ge(sem("biasQb"), 1)
                        pe.wait_ge(sem("identb"), 1)
                        pe.wait_ge(sem("qkf"), B)
                if n >= 2:
                    pe.wait_ge(sem("nm1"), n - 1)
                for q in range(TB):
                    dst = bank[n % 2][:, q * SPAN:q * SPAN + SPAN]
                    pe.matmul(dst, QS[:, b, h, q * P:q * P + P], KSt[:, b, h, OFF[q]:OFF[q] + SPAN],
                              start=True, stop=False)
                    last = pe.matmul(dst, identb[:, :], biasQb[:, h, q * SPAN:q * SPAN + SPAN],
                                     start=False, stop=True)
                last.then_inc(sem("mx1"), 1)

            def exact_scores(b, h):
                n = b * NH + h
                pe.wait_ge(sem("diag1"), n + 1)
                if n >= 2:
                    pe.wait_ge(sem("u1"), n - 1)
                for k in range(TB):
                    dst = bank[2 + n % 2][:, k * SPAN:k * SPAN + SPAN]
                    pe.matmul(dst, KSt[:, b, h, k * P:k * P + P], QS[:, b, h, OFF[k]:OFF[k] + SPAN],
                              start=True, stop=False)
                    last = pe.matmul(dst, onesb[:, :], diag1[:, b % 2, h, OFF[k]:OFF[k] + SPAN],
                                     start=False, stop=True)
                last.then_inc(sem("s1"), 1)

            def attend1(b, h):
                n = b * NH + h
                pe.wait_ge(sem("p1"), n + 1)
                if n == 0:
                    pe.wait_ge(sem("v1"), 1)
                if h == 0 and b >= 2:
                    pe.wait_ge(sem("ct1"), b - 1)
                g, c0 = h % 4, (h // 4) * N
                for k in range(TB):
                    last = pe.matmul(bank[4 + b % 2][32 * g:32 * g + VW, c0 + OFF[k]:c0 + OFF[k] + SPAN],
                                     V1[:, TB * b + k, h, :], P1[:, n % 3, k * SPAN:k * SPAN + SPAN],
                                     start=(k == 0), stop=(k == TB - 1), skip_group_check=True)
                last.then_inc(sem("av1"), 1)

            def turn1(b):
                pe.wait_ge(sem("ct1"), b + 1)
                if b >= 1:
                    pe.wait_ge(sem("ctx1"), b)
                for q in range(TB):
                    for g in range(2):
                        j = q * 2 + g
                        last = pe.transpose(bank[6][:, j * P:j * P + P],
                                            CT1[:, b % 2, g * N + q * P:g * N + q * P + P], ident)
                last.then_inc(sem("turn1"), 1)

            LAG = 2
            for h in range(NH):
                max_scores(0, h)
            for n in range(B * NH + LAG):
                b, h = divmod(n, NH)
                if b < B:
                    if b + 1 < B:
                        max_scores(b + 1, h)
                    exact_scores(b, h)
                m = n - LAG
                if m >= 0:
                    attend1(m // NH, m % NH)
                    if m % NH == 3 and m // NH >= 1:
                        turn1(m // NH - 1)

            def features(s, b, i):
                pe.wait_ge(sem(s + "_xn"), b + 1)
                for q in range(TB):
                    last = pe.transpose(bank[i][0:C, q * P:q * P + P], XN[s][:, TB * b + q, 0:C], ident)
                last.then_inc(sem(s + "_xf_p"), 1)

            def self_attention(s, lhs, width, hand_on, middle=None):
                for i in range(B + 5):
                    if s == "a" and i == 2:
                        turn1(B - 1)
                    if 0 <= i - 2 < B:
                        b = i - 2
                        pe.wait_ge(sem("c_lhs" if middle else "a_xf"), b + 1)
                        if b == 0:
                            pe.wait_ge(sem("later_const"), 7)
                        if b >= 2:
                            pe.wait_ge(sem("att_exp"), 2 * through(s) + 2 * (b - 1))
                        scores(b, lhs, XF[s]).then_inc(sem("att_s"), 1)
                    if i < B:
                        if i >= 2:
                            pe.wait_ge(sem(s + "_xf"), i - 1)
                        elif s == "a":
                            pe.wait_ge(sem("nm1"), B * NH - 1 + i)
                        features(s, i, i % 2)
                    if middle and 0 <= i - 1 < B:
                        middle(i - 1)
                    if 0 <= i - 3 < B:
                        b = i - 3
                        pe.wait_ge(sem("c_pn" if s == "c" else "att_exp"), 2 * b + 2)
                        if b >= 2:
                            pe.wait_ge(sem("att_pt"), through(s) + b - 1)
                        transpose_p(b).then_inc(sem("att_pt_p"), 1)
                    if 0 <= i - 4 < B:
                        b = i - 4
                        pe.wait_ge(sem("att_pt"), through(s) + b + 1)
                        if b >= 2:
                            pe.wait_ge(sem("att_ct"), through(s) + b - 1)
                        attend(b, XN[s], width).then_inc(sem("att_ct_p"), 1)
                    if 0 <= i - 5:
                        hand_on(i - 5)

            def hand_on_a(b):
                pe.wait_ge(sem("att_ct"), b + 1)
                if b == 0:
                    pe.wait_ge(sem("a_xf"), B)
                if b >= 2:
                    pe.wait_ge(sem("x3"), b - 1)
                for q in range(TB):
                    last = pe.transpose(bank[b % 2][:, q * C:q * C + C], CTa[:, b * N + q * P:b * N + q * P + P],
                                        ident[0:C, 0:C])
                last.then_inc(sem("a_turned"), 1)

            self_attention("a", XF["a"], C, hand_on_a)

            for b in range(B):
                if b < 2:
                    pe.wait_ge(sem("x3"), b + 3)
                features("b", b, b)
            pe.wait_ge(sem("mean2"), 1)
            pe.wait_ge(sem("wa_landed"), 16)
            pe.matmul(bank[4][0:B, 0:E2], mean2[:, :], WAs[:, WA["wr"]], start=True, stop=True).then_inc(sem("r_logits"), 1)
            pe.wait_ge(sem("r_rw"), 1)
            pe.matmul(bank[5][0:B, 0:E2], loads1[:, :], lg[:, 1, :], start=True, stop=True).then_inc(sem("r_loads"), 1)
            pe.wait_ge(sem("r_spread"), 2)
            pe.matmul(bank[6][:, 0:2 * B * TOPK], ones4[:, :], spread[:, :, :, :].rearrange("p a b k -> p (a b k)"),
                      start=True, stop=True).then_inc(sem("r_bcast"), 1)
            for i in range(B + 2):
                if i < B:
                    b = i
                    pe.wait_ge(sem("w1sel"), TOPK * (b + 1))
                    pe.wait_ge(sem("b_xf"), B)
                    for k in range(TOPK):
                        last = pe.matmul(bank[b][:, k * N:k * N + N], W1sel[:, TOPK * b + k, :],
                                         XF["b"][:, b * N:b * N + N], start=True, stop=True)
                    last.then_inc(sem("up2"), 1)
                if 0 <= i - 1 < B:
                    b = i - 1
                    pe.wait_ge(sem("gelu"), b + 1)
                    pe.wait_ge(sem("w2sel"), TOPK * (b + 1))
                    if b == 0:
                        pe.wait_ge(sem("r_spread_read"), 2)
                    if b >= 2:
                        pe.wait_ge(sem("ut"), b - 1)
                    for k in range(TOPK):
                        last = pe.matmul(bank[4 + b % 2][0:C, 0:N], W2sel[:, TOPK * b + k, :],
                                         H2[:, b, k * N:k * N + N], start=(k == 0), stop=(k == TOPK - 1))
                    last.then_inc(sem("down2"), 1)
                if 0 <= i - 2 < B:
                    b = i - 2
                    pe.wait_ge(sem("ut"), b + 1)
                    if b >= 2:
                        pe.wait_ge(sem("u"), b - 1)
                    for q in range(TB):
                        last = pe.transpose(bank[6 + b % 2][:, q * C:q * C + C], UT[:, b * N + q * P:b * N + q * P + P],
                                            ident[0:C, 0:C])
                    last.then_inc(sem("u_turned"), 1)

            def middle_c(b):
                pe.wait_ge(sem("c_xf"), b + 1)
                if b >= 2:
                    pe.wait_ge(sem("c_lhs"), b - 1)
                pe.matmul(bank[2 + b % 2][0:C1, 0:N], WAs[:, WA["y3"]], XF["c"][:, b * N:b * N + N],
                          start=True, stop=True).then_inc(sem("c_lhs_p"), 1)

            def hand_on_c(b):
                pe.wait_ge(sem("att_ct"), B + b + 1)
                if b == 0:
                    pe.wait_ge(sem("c_xf"), B)
                if b >= 2:
                    pe.wait_ge(sem("tanh"), 2 * (b - 1))
                for q in range(TB):
                    c = slice(b * N + q * P, b * N + q * P + P)
                    dst = bank[b % 2][:, q * 3 * C:(q + 1) * 3 * C]
                    pe.matmul(dst, XF["c"][:, c], WAs[:, WA["gx"]], start=True, stop=False)
                    last = pe.matmul(dst, CTc[:, c], WAs[:, WA["ga"]], start=False, stop=True)
                last.then_inc(sem("gates"), 1)

            pe.wait_ge(sem("gelu"), B)
            self_attention("c", LHSc, C1, hand_on_c, middle_c)

            for b in range(B):
                if b < 2:
                    pe.wait_ge(sem("tanh"), 2 * (b + 3))
                features("d", b, b)
            for b in range(B):
                pe.wait_ge(sem("d_xf"), b + 1)
                for q in range(TB):
                    t = TB * b + q
                    last = pe.matmul(bank[4][:, t * E3:t * E3 + E3], XF["d"][:, t * P:t * P + P],
                                     WAs[:, WA["gate"]], start=True, stop=True)
            last.then_inc(sem("logits3"), 1)
            pe.wait_ge(sem("ohb"), 1)
            pe.wait_ge(sem("prefixb"), 1)
            flat = ohb[:, :, :].rearrange("p t e -> p (t e)")
            last = pe.matmul(bank[5][:, 0:T * E3], prefixb[:, :], flat, start=True, stop=False, skip_group_check=True)
            for back in range(1, T):
                last = pe.matmul(bank[5][:, back * E3:T * E3], onesb[:, :], flat[:, 0:(T - back) * E3],
                                 start=False, stop=(back == T - 1), skip_group_check=True)
            last.then_inc(sem("counts"), 1)
            chunks = [(0, 512), (512, 512), (1024, 256)]
            for t in range(T):
                pe.wait_ge(sem("g3"), t + 1)
                if t == 0:
                    pe.wait_ge(sem("xl"), 1)
                for h, part3 in enumerate((XH, XL)):
                    for c, (at, width) in enumerate(chunks):
                        last = pe.matmul(bank[c][0:C, 0:width], part3[:, t, :], G3[:, t % 2, at:at + width],
                                         start=(t == 0 and h == 0), stop=(t == T - 1 and h == 1))
                last.then_inc(sem("gathered"), 1)
            pe.wait_ge(sem("sd"), 1)
            for h in range(2):
                last = pe.matmul(bank[6 + h][:, :], onesf[:, :],
                                 SD[:, 4 * h:4 * h + 4, :].rearrange("p t q -> p (t q)"), start=True, stop=True)
            last.then_inc(sem("sb_p"), 1)
            for e in range(E3 + 1):
                if e < E3:
                    pe.wait_ge(sem("xb"), 3)
                    pe.wait_ge(sem("xb_ones"), 1)
                    if e == 0:
                        pe.wait_ge(sem("w3_landed"), 16)
                    if e >= 2:
                        pe.wait_ge(sem("h3"), e - 1)
                    for k in range(2):
                        last = pe.matmul(bank[3 + e % 2][:, k * CAP3:k * CAP3 + CAP3], W3s[:, e, k * P:k * P + P],
                                         XB[:, e * CAP3:e * CAP3 + CAP3], start=True, stop=True)
                    last.then_inc(sem("up3"), 1)
                if e >= 1:
                    f = e - 1
                    pe.wait_ge(sem("h3"), f + 1)
                    if f == 0:
                        pe.wait_ge(sem("w2b_landed"), 16)
                    if f >= 2:
                        pe.wait_ge(sem("yt"), f - 1)
                    dst = bank[5 if f % 2 else 0]
                    for k in range(2):
                        last = pe.matmul(dst[0:C, 0:CAP3], W2B[:, f, k, :], H3[:, f % 3, k, :],
                                         start=(k == 0), stop=(k == 1))
                    last.then_inc(sem("down3"), 1)
            pe.wait_ge(sem("yt"), E3)
            for j in range(SLOTS // P):
                last = pe.transpose(bank[1 + j // 8][:, j % 8 * C:j % 8 * C + C], YT[:, j * P:j * P + P], ident[0:C, 0:C])
            last.then_inc(sem("y_turned"), 1)
            pe.wait_ge(sem("yl"), 2)
            pe.wait_ge(sem("sb"), 2)
            for j in range(SLOTS // P):
                pe.wait_ge(sem("gt"), j + 1)
                for h, part3 in enumerate((YH, YL)):
                    for c in range(2):
                        last = pe.matmul(bank[6 + c][0:C, :], part3[:, j, :], GT[:, j % 2, c * 512:c * 512 + 512],
                                         start=(j == 0 and h == 0), stop=(j == SLOTS // P - 1 and h == 1))
                last.then_inc(sem("scattered"), 1)
            for b in range(B):
                pe.wait_ge(sem("zt"), b // 2 + 1)
                for q in range(TB):
                    t = TB * b + q
                    last = pe.transpose(bank[b][:, q * C:q * C + C], ZT[:, t * P:t * P + P], ident[0:C, 0:C])
                last.then_inc(sem("z_turned"), 1)

        @block.scalar
        def _(act):
            act.dma_start(W8[:, :], w8).then_inc(sem("w8_landed"), 16)
            act.dma_start(W0s[:, :], w0).then_inc(sem("w0_landed"), 16)
            act.wait_ge(sem("a0"), 1)
            act.activation(A0[:, :], bank[6][0:C1, 0:C1], ACT.Copy, scale=float(D0) ** -0.5) \
                .then_inc(sem("a0_s"), 1)
            for b in range(B):
                act.wait_ge(sem("g0_p"), b + 1)
                act.activation(G0[:, b * N:b * N + N], bank[b][0:C1, 0:N], ACT.Copy).then_inc(sem("g0"), 1)
            for i in range(B + 1):
                if i < B:
                    act.wait_ge(sem("nm0"), i + 1)
                    for q in range(TB):
                        t = TB * i + q
                        act.activation(S_P[:, i, q, :], bank[4 + i % 2][:, q * N:q * N + N], ACT.Exp,
                                       bias=nmax[:, t:t + 1], accum_out=den[:, t:t + 1]).then_inc(sem("exp0"), 1)
                if i >= 1:
                    b = i - 1
                    act.wait_ge(sem("ct0_p"), b + 1)
                    act.activation(CT[:, b * N:b * N + N], bank[2 + b % 2][0:C1, 0:N], ACT.Copy) \
                        .then_inc(sem("ct0"), 1)
            for b in range(B):
                act.wait_ge(sem("qk_p"), b + 1)
                act.activation(QK[:, b * N:b * N + N], bank[b][:, 0:N], ACT.Copy,
                               scale=Cs[:, CST["scale"]]).then_inc(sem("qkf"), 1)
            act.wait_ge(sem("v1_p"), 1)
            act.activation(V1[:, :, :, 0:HD],
                           bank[4][:, :].rearrange("p (t h d) -> p t h d", t=T, h=NH), ACT.Copy).then_inc(sem("v1"), 1)
            for n in range(B * NH + 3):
                b, h = divmod(n, NH)
                if b < B:
                    act.wait_ge(sem("u1"), n + 1)
                    if n >= 3:
                        act.wait_ge(sem("av1"), n - 2)
                    act.activation(P1[:, n % 3, :], U1[:, n % 3, :], ACT.Exp).then_inc(sem("p1"), 1)
                m = n - 3
                if m >= 0 and m % NH == NH - 1:
                    b = m // NH
                    act.wait_ge(sem("av1"), (b + 1) * NH)
                    if b >= 2:
                        act.wait_ge(sem("turn1"), b - 1)
                    act.activation(CT1[:, b % 2, :], bank[4 + b % 2][:, :], ACT.Copy).then_inc(sem("ct1"), 1)


            def attention_act(s, nm, dn, ct, width):
                for i in range(B + 6):
                    if 0 <= i - 2 < B:
                        b = i - 2
                        act.wait_ge(sem("att_nm"), through(s) + b + 1)
                        for q in range(TB):
                            t = TB * b + q
                            act.activation(S_P[:, b, q, :], bank[4 + b % 2][:, q * N:q * N + N], ACT.Exp,
                                           bias=nm[:, t:t + 1], scale=float(C) ** -0.5 if s == "a" else 1.0,
                                           accum_out=dn[:, t:t + 1]).then_inc(sem("att_exp"), 1)
                    if i < B:
                        act.wait_ge(sem(s + "_xf_p"), i + 1)
                        act.activation(XF[s][0:C, i * N:i * N + N], bank[i % 2][0:C, 0:N], ACT.Copy) \
                            .then_inc(sem(s + "_xf"), 1)
                    if s == "c" and 0 <= i - 1 < B:
                        b = i - 1
                        act.wait_ge(sem("c_lhs_p"), b + 1)
                        act.activation(LHSc[:, b * N:b * N + N], bank[2 + b % 2][0:C1, 0:N], ACT.Copy) \
                            .then_inc(sem("c_lhs"), 1)
                    if 0 <= i - 4 < B:
                        b = i - 4
                        act.wait_ge(sem("att_ct_p"), through(s) + b + 1)
                        act.activation(ct[:, b * N:b * N + N], bank[2 + b % 2][0:width, 0:N], ACT.Copy) \
                            .then_inc(sem("att_ct"), 1)
                    if s == "c" and 0 <= i - 5 < B:
                        b = i - 5
                        act.wait_ge(sem("gates"), b + 1)
                        g = bank[b % 2][:, 0:TB * 3 * C].rearrange("p (q f) -> p q f", q=TB)
                        t = slice(TB * b, TB * b + TB)
                        act.activation(th[:, t, 0:C], g[:, :, 0:C], ACT.Tanh).then_inc(sem("tanh"), 1)
                        act.activation(th[:, t, C:3 * C], g[:, :, C:3 * C], ACT.Tanh, scale=0.5).then_inc(sem("tanh"), 1)

            attention_act("a", nmaxa, dena, CTa, C)
            for b in range(B):
                act.wait_ge(sem("b_xf_p"), b + 1)
                act.activation(XF["b"][0:C, b * N:b * N + N], bank[b][0:C, 0:N], ACT.Copy, accum_out=msum[:, b:b + 1]) \
                    .then_inc(sem("b_xf"), 1)
            act.wait_ge(sem("r_nm"), 1)
            act.activation(lg[:, 0, :], bank[4][0:B, 0:E2], ACT.Exp, bias=col[:, 0:1], accum_out=col[:, 1:2]) \
                .then_inc(sem("r_exp"), 1)
            act.wait_ge(sem("r_nm"), 2)
            act.activation(lg[:, 4, :], lg[:, 3, :], ACT.Exp, bias=col[:, 3:4], accum_out=col[:, 4:5]) \
                .then_inc(sem("r_exp"), 1)
            act.wait_ge(sem("r_nm"), 3)
            act.activation(lg[:, 7, 0:TOPK], lg[:, 6, 0:TOPK], ACT.Exp, bias=col[:, 6:7], accum_out=col[:, 7:8]) \
                .then_inc(sem("r_exp"), 1)
            act.wait_ge(sem("slot_e"), 1)
            for i in range(B * TOPK):
                e = act.value_load(slot_e[0:1, i:i + 1], min_val=0, max_val=E2 - 1)
                act.activation(W1sel[:, i, :], WAs[:, bass.ds(e * F2, F2)], ACT.Copy).then_inc(sem("w1sel"), 1)
            for b in range(B):
                act.wait_ge(sem("up2"), b + 1)
                act.activation(H2[:, b, :], bank[b][:, :], ACT.Gelu).then_inc(sem("gelu"), 1)
            attention_act("c", nmaxc, denc, CTc, C1)
            for b in range(B):
                act.wait_ge(sem("d_xf_p"), b + 1)
                act.activation(XF["d"][0:C, b * N:b * N + N], bank[b][0:C, 0:N], ACT.Copy).then_inc(sem("d_xf"), 1)
            act.wait_ge(sem("d3"), 1)
            act.activation(ex3[:, :, :], d3[:, :, :], ACT.Exp).then_inc(sem("ex3"), 1)
            act.wait_ge(sem("sb_p"), 1)
            for h in range(2):
                act.activation(SB[:, h * 512:h * 512 + 512], bank[6 + h][:, :], ACT.Copy).then_inc(sem("sb"), 1)
            act.wait_ge(sem("gathered"), T)
            for c, (at, width) in enumerate([(0, 512), (512, 512), (1024, 256)]):
                act.activation(XB[0:C, at:at + width], bank[c][0:C, 0:width], ACT.Copy).then_inc(sem("xb"), 1)
            for e in range(E3 + 1):
                if e < E3:
                    act.wait_ge(sem("up3"), e + 1)
                    if e >= 3:
                        act.wait_ge(sem("down3"), e - 2)
                    act.activation(H3[:, e % 3, :, :].rearrange("p k s -> p (k s)"),
                                   bank[3 + e % 2][:, 0:2 * CAP3], ACT.Relu).then_inc(sem("h3"), 1)
                if e >= 1:
                    f = e - 1
                    act.wait_ge(sem("down3"), f + 1)
                    act.activation(YT[:, f * CAP3:f * CAP3 + CAP3], bank[5 if f % 2 else 0][0:C, 0:CAP3], ACT.Identity,
                                   bias=WAs[0:C, WA["fb2"]][:, f:f + 1]).then_inc(sem("yt"), 1)
            act.wait_ge(sem("y_turned"), 1)
            act.activation(YH[:, 0:8, :].rearrange("p j c -> p (j c)"), bank[1][:, :], ACT.Copy).then_inc(sem("yh"), 1)
            act.activation(YH[:, 8:10, :].rearrange("p j c -> p (j c)"), bank[2][:, 0:2 * C], ACT.Copy).then_inc(sem("yh"), 1)
            act.wait_ge(sem("scattered"), SLOTS // P)
            for h in range(2):
                act.activation(ZT[:, h * 512:h * 512 + 512], bank[6 + h][0:C, :], ACT.Copy).then_inc(sem("zt"), 1)

        @block.vector
        def _(dve):
            steps = [0]

            def counted(ins):
                steps[0] += 1
                ins.then_inc(sem("vector_step"), 1)
                return steps[0]

            def then(ins):
                dve.wait_ge(sem("vector_step"), counted(ins))

            for b in range(B):
                dve.wait_ge(sem("xt_p"), b + 1)
                dve.tensor_copy(XT[0:C, b * N:b * N + N], bank[b][0:C, 0:N]).then_inc(sem("xt"), 1)
            dve.wait_ge(sem("wvo"), 1)
            dve.tensor_copy(Wvo[:, :], bank[7][0:C1, 0:C]).then_inc(sem("wvo_s"), 1)
            for i in range(B + 3):
                if i < B:
                    dve.wait_ge(sem("s0"), i + 1)
                    dve.tensor_reduce(nmax[:, TB * i:TB * i + TB],
                                      bank[4 + i % 2][:, :].rearrange("p (q k) -> p q k", q=TB),
                                      AX.X, ALU.max, negate=True).then_inc(sem("nm0"), 1)
                if 0 <= i - 1 < B:
                    b = i - 1
                    dve.wait_ge(sem("pt0_p"), b + 1)
                    dve.tensor_copy(S_PT[:, b, :, :].rearrange("p k q -> p (k q)"), bank[6 + b % 2][:, :]) \
                        .then_inc(sem("pt0"), 1)
                    dve.wait_ge(sem("exp0"), 2 * b + 2)
                    dve.reciprocal(rden[:, TB * b:TB * b + TB], den[:, TB * b:TB * b + TB]).then_inc(sem("rd0"), 1)
                if 0 <= i - 3 < B:
                    b = i - 3
                    dve.wait_ge(sem("o0"), b + 1)
                    dve.wait_ge(sem("rd0"), b + 1)
                    for q in range(TB):
                        t = TB * b + q
                        last = dve.scalar_tensor_tensor(
                            out=X1[:, t, :], in0=bank[b % 2][:, q * C:q * C + C], scalar=rden[:, t:t + 1],
                            in1=X[:, t, 0:C], op0=ALU.mult, op1=ALU.add)
                    last.then_inc(sem("x1"), 1)
            stats = []
            for b in range(B):
                dve.wait_ge(sem("x1t_p"), b + 1)
                stats.append(counted(dve.bn_stats(gn_st[:, b, :], bank[4 + b][0:C, 0:N])))
            for b in range(B):
                dve.wait_ge(sem("vector_step"), stats[b])
                last = counted(dve.bn_aggr(gn_mv[:, b, 0:2], gn_st[:, b, :]))
            dve.wait_ge(sem("vector_step"), last)
            dve.tensor_tensor(gn_mv[:, :, 2], gn_mv[:, :, 0], gn_mv[:, :, 0], ALU.mult).then_inc(sem("gn_mv"), 1)
            dve.wait_ge(sem("gn_pair"), 1)
            then(dve.tensor_copy(gn_g[:, :, :].rearrange("c b k -> c (b k)"), bank[0][0:C, 0:3 * B]))
            then(dve.tensor_tensor(gn_sq[:, :], gn_g[:, :, 0], gn_g[:, :, 0], ALU.mult))
            then(dve.scalar_tensor_tensor(out=gn_v[:, :], in0=gn_g[:, :, 1], scalar=LN_EPS, in1=gn_g[:, :, 2],
                                          op0=ALU.add, op1=ALU.add))
            dve.tensor_tensor(gn_v[:, :], gn_v[:, :], gn_sq[:, :], ALU.subtract).then_inc(sem("gn_var"), 1)
            dve.wait_ge(sem("gn_rstd"), 1)
            then(dve.scalar_tensor_tensor(out=gn_nb[:, :], in0=gn_g[:, :, 0], scalar=-1.0, in1=gn_r[:, :],
                                          op0=ALU.mult, op1=ALU.mult))
            for b in range(B):
                dve.tensor_scalar(XN1[0:C, b * N:b * N + N], bank[4 + b][0:C, 0:N], gn_r[:, b:b + 1],
                                  gn_nb[:, b:b + 1], ALU.mult, ALU.add).then_inc(sem("xn1"), 1)
            for b in range(B):
                c = slice(b * N, b * N + N)
                dve.wait_ge(sem("qkf"), b + 1)
                dve.tensor_copy(part[0][:, c], QK[:, c]).then_inc(sem("qk_part"), 1)
                dve.wait_ge(sem("qk_part"), 3 * b + 1)
                then(dve.tensor_tensor(qkr[:, c], QK[:, c], part[0][:, c], ALU.subtract))
                dve.tensor_copy(part[1][:, c], qkr[:, c]).then_inc(sem("qk_part"), 1)
                dve.wait_ge(sem("qk_part"), 3 * b + 2)
                dve.tensor_tensor(part[2][:, c], qkr[:, c], part[1][:, c], ALU.subtract).then_inc(sem("qk_part"), 1)

            def maxima(n):
                dve.wait_ge(sem("mx1"), n + 1)
                dve.tensor_reduce(nm1[:, n // NH, n % NH, :],
                                  bank[n % 2][:, 0:TB * SPAN].rearrange("p (q k) -> p q k", q=TB),
                                  AX.X, ALU.max, negate=True).then_inc(sem("nm1"), 1)

            def biased(n):
                dve.wait_ge(sem("s1"), n + 1)
                if n == 0:
                    dve.wait_ge(sem("biasK_landed"), 16)
                if n >= 3:
                    dve.wait_ge(sem("p1"), n - 2)
                dve.tensor_tensor(U1[:, n % 3, :], bank[2 + n % 2][:, 0:TB * SPAN], biasK[:, n % NH, :], ALU.add) \
                    .then_inc(sem("u1"), 1)

            def finish1(b):
                dve.wait_ge(sem("turn1"), b + 1)
                v = bank[6][:, :].rearrange("p (j g w) -> p j g w", j=2 * TB, g=4)
                then(dve.reciprocal(rz1[:, b % 2, :, :], v[:, :, :, HD]))
                dve.tensor_tensor(ctx1[:, b % 2, :, :, :], v[:, :, :, 0:HD],
                                  rz1[:, b % 2, :, :].unsqueeze(3).to_broadcast([P, 2 * TB, 4, HD]), ALU.mult) \
                    .then_inc(sem("ctx1"), 1)
                dve.wait_ge(sem("ctx1"), b + 1)
                dve.tensor_tensor(X2[:, TB * b:TB * b + TB, :].rearrange("p q c -> p (q c)"),
                                  ctx1[:, b % 2, :, :, :].rearrange("p j g d -> p (j g d)"),
                                  X1[:, TB * b:TB * b + TB, :].rearrange("p q c -> p (q c)"), ALU.add) \
                    .then_inc(sem("x2_done"), 1)

            def stats(s, src, ready, count, k):
                n = LN_STEPS.index((s, k * T // 2, T // 2) if s != "a" else (s, TB * k, TB))
                first, blocks = LN_STEPS[n][1:]
                dve.wait_ge(sem(ready), count)
                for t in range(first, first + blocks):
                    last = dve.bn_stats(ln_st[s][:, t, :], src[:, t, :])
                then(last)
                for t in range(first, first + blocks):
                    last = dve.bn_aggr(ln_mv[s][:, t, :], ln_st[s][:, t, :])
                last.then_inc(sem("ln_mv"), 1)

            def apply(s, src, k):
                n = LN_STEPS.index((s, k * T // 2, T // 2) if s != "a" else (s, TB * k, TB))
                first, blocks = LN_STEPS[n][1:]
                dve.wait_ge(sem("ln_mv"), n + 1)
                dve.wait_ge(sem("ln_rs"), n + 1)
                for t in range(first, first + blocks):
                    last = dve.tensor_scalar(XN[s][:, t, 0:C], src[:, t, :], ln_mv[s][:, t, 0:1], ln_rs[s][:, t:t + 1],
                                             ALU.subtract, ALU.mult)
                    if t % TB == TB - 1:
                        last.then_inc(sem(s + "_xn"), 1)

            for n in range(NH):
                maxima(n)
            for n in range(B * NH):
                if n + NH < B * NH:
                    maxima(n + NH)
                biased(n)
                m = n - 4
                if m >= 0 and m % NH == 3 and m // NH >= 1:
                    finish1(m // NH - 1)
                    stats("a", X2, "x2_done", m // NH, m // NH - 1)
                if m >= 0 and m % NH == 7 and m // NH >= 1:
                    apply("a", X2, m // NH - 1)
            apply("a", X2, 2)
            finish1(B - 1)
            stats("a", X2, "x2_done", B, B - 1)

            def maxima_of(s, b, nm):
                dve.wait_ge(sem("att_s"), through(s) + b + 1)
                t = slice(TB * b, TB * b + TB)
                rows = bank[4 + b % 2][:, :].rearrange("p (q k) -> p q k", q=TB)
                if s == "a":
                    then(dve.tensor_reduce(nm[:, t], rows, AX.X, ALU.max, negate=True))
                    dve.tensor_scalar(nm[:, t], nm[:, t], float(C) ** -0.5, None, ALU.mult).then_inc(sem("att_nm"), 1)
                else:
                    dve.tensor_reduce(nm[:, t], rows, AX.X, ALU.max, negate=True).then_inc(sem("att_nm"), 1)

            def x3_of(b):
                dve.wait_ge(sem("a_turned"), b + 1)
                for q in range(TB):
                    t = TB * b + q
                    last = dve.scalar_tensor_tensor(
                        out=X3[:, t, :], in0=bank[b % 2][:, q * C:q * C + C], scalar=rdena[:, t:t + 1],
                        in1=X2[:, t, :], op0=ALU.mult, op1=ALU.add)
                last.then_inc(sem("x3"), 1)

            def turned_p(s, b):
                dve.wait_ge(sem("att_pt_p"), through(s) + b + 1)
                dve.tensor_copy(S_PT[:, b, :, :].rearrange("p k q -> p (k q)"), bank[6 + b % 2][:, :]) \
                    .then_inc(sem("att_pt"), 1)

            for i in range(2, B + 4):
                if 0 <= i - 2 < B:
                    b = i - 2
                    maxima_of("a", b, nmaxa)
                    if b == 0:
                        apply("a", X2, B - 1)
                if 0 <= i - 3 < B:
                    b = i - 3
                    turned_p("a", b)
                    dve.wait_ge(sem("att_exp"), 2 * b + 2)
                    then(dve.reciprocal(rdena[:, TB * b:TB * b + TB], dena[:, TB * b:TB * b + TB]))
                if 0 <= i - 5 < B:
                    x3_of(i - 5)
            stats("b", X3, "x3", B // 2, 0)
            x3_of(B - 1)
            stats("b", X3, "x3", B, 1)
            for half in range(2):
                apply("b", X3, half)

            dve.wait_ge(sem("b_xf"), B)
            dve.tensor_scalar(mean2[0:C, :], msum[:, :], 1.0 / N, None, ALU.mult).then_inc(sem("mean2"), 1)
            dve.wait_ge(sem("r_logits"), 1)
            dve.tensor_reduce(col[:, 0:1], bank[4][0:B, 0:E2], AX.X, ALU.max, negate=True).then_inc(sem("r_nm"), 1)
            dve.wait_ge(sem("r_exp"), 1)
            then(dve.reciprocal(col[:, 2:3], col[:, 1:2]))
            dve.tensor_scalar(lg[:, 1, :], lg[:, 0, :], col[:, 2:3], None, ALU.mult).then_inc(sem("r_rw"), 1)
            dve.wait_ge(sem("r_loads"), 1)
            then(dve.reciprocal(lg[:, 2, :], bank[5][0:B, 0:E2]))
            then(dve.tensor_scalar(lg[:, 2, :], lg[:, 2, :], CAP2, 1.0, ALU.mult, ALU.min))
            dve.wait_ge(sem("r_rw"), 1)
            then(dve.tensor_tensor(lg[:, 3, :], lg[:, 2, :], lg[:, 1, :], ALU.mult))
            dve.tensor_reduce(col[:, 3:4], lg[:, 3, :], AX.X, ALU.max, negate=True).then_inc(sem("r_nm"), 1)
            dve.wait_ge(sem("r_exp"), 2)
            then(dve.reciprocal(col[:, 5:6], col[:, 4:5]))
            then(dve.tensor_scalar(lg[:, 5, :], lg[:, 4, :], col[:, 5:6], None, ALU.mult))
            then(dve.max(lg[:, 6, :], lg[:, 5, :]))
            dve.tensor_scalar(col[:, 6:7], lg[:, 6, 0:1], -1.0, None, ALU.mult).then_inc(sem("r_nm"), 1)
            then(dve.max_index(top_i[:, :], lg[:, 6, :], lg[:, 5, :]))
            id4 = ident[0:B, 0:B].unsqueeze(2).to_broadcast([B, B, TOPK])
            dve.tensor_tensor(spread[:, 1, :, :], top_i[:, 0:TOPK].unsqueeze(1).to_broadcast([B, B, TOPK]), id4,
                              ALU.mult).then_inc(sem("r_spread"), 1)
            dve.wait_ge(sem("r_exp"), 3)
            then(dve.reciprocal(col[:, 8:9], col[:, 7:8]))
            then(dve.tensor_scalar(lg[:, 7, 4:4 + TOPK], lg[:, 7, 0:TOPK], col[:, 8:9], None, ALU.mult))
            dve.tensor_tensor(spread[:, 0, :, :], lg[:, 7, 4:4 + TOPK].unsqueeze(1).to_broadcast([B, B, TOPK]), id4,
                              ALU.mult).then_inc(sem("r_spread"), 1)
            dve.wait_ge(sem("r_bcast"), 1)
            dve.tensor_copy(slot_e[:, :], bank[6][0:1, B * TOPK:2 * B * TOPK]).then_inc(sem("slot_e"), 1)
            dve.tensor_copy(tw[:, :], bank[6][:, 0:B * TOPK]).then_inc(sem("r_spread_read"), 2)
            dve.wait_ge(sem("slot_e"), 1)
            dve.wait_ge(sem("r_spread_read"), 2)
            dve.wait_ge(sem("w2a_landed"), 16)
            w2flat = W2A[:, :, :].rearrange("p e c -> p (e c)")
            for i in range(B * TOPK):
                e = dve.value_load(slot_e[0:1, i:i + 1], min_val=0, max_val=E2 - 1)
                dve.tensor_scalar(W2sel[:, i, :], w2flat[:, bass.ds(e * C, C)], tw[:, i:i + 1], None, ALU.mult) \
                    .then_inc(sem("w2sel"), 1)
                b2 = WAs[0:C, bass.ds(e + WA["b2"].start, 1)]
                if i % TOPK == 0:
                    dve.tensor_scalar(b2sel[:, i // TOPK, 0:1], b2, tw[0:C, i:i + 1], None, ALU.mult) \
                        .then_inc(sem("b2sel"), 1)
                else:
                    dve.wait_ge(sem("b2sel"), i)
                    dve.scalar_tensor_tensor(out=b2sel[:, i // TOPK, 1:2], in0=b2, scalar=tw[0:C, i:i + 1],
                                             in1=b2sel[:, i // TOPK, 0:1], op0=ALU.mult, op1=ALU.add) \
                        .then_inc(sem("b2sel"), 1)
            for i in range(B + 1):
                if i < B:
                    b = i
                    dve.wait_ge(sem("down2"), b + 1)
                    dve.wait_ge(sem("b2sel"), TOPK * (b + 1))
                    dve.tensor_scalar(UT[:, b * N:b * N + N], bank[4 + b % 2][0:C, 0:N], b2sel[:, b, 1:2], None, ALU.add) \
                        .then_inc(sem("ut"), 1)
                if i >= 1:
                    b = i - 1
                    dve.wait_ge(sem("u_turned"), b + 1)
                    dve.tensor_tensor(U[:, TB * b:TB * b + TB, :],
                                      bank[6 + b % 2][:, 0:TB * C].rearrange("p (q c) -> p q c", q=TB),
                                      XN["b"][:, TB * b:TB * b + TB, 0:C], ALU.add).then_inc(sem("u"), 1)
            def x4_of(half):
                t = slice(half * T // 2, (half + 1) * T // 2)
                wide = [P, T // 2, C]
                apply("u", U, half)
                dve.wait_ge(sem("u_xn"), B // 2 * (half + 1))
                then(dve.tensor_tensor(un[:, t, :], XN["u"][:, t, 0:C], gb[:, 0, :].unsqueeze(1).to_broadcast(wide), ALU.mult))
                dve.tensor_tensor(X4[:, t, :], un[:, t, :], X3b[:, t, :], ALU.add).then_inc(sem("x4"), 1)

            for half in range(2):
                stats("u", U, "u", B // 2 * (half + 1), half)
            dve.wait_ge(sem("gb_landed"), 16)
            dve.wait_ge(sem("x3b"), 1)
            for half in range(2):
                x4_of(half)
                stats("c", X4, "x4", half + 1, half)
            for half in range(2):
                apply("c", X4, half)

            def x5_of(b):
                t = slice(TB * b, TB * b + TB)
                dve.wait_ge(sem("tanh"), 2 * b + 2)
                dve.scalar_tensor_tensor(out=gm[:, t, 0:C], in0=th[:, t, C:2 * C], scalar=1.0,
                                         in1=XN["c"][:, t, 0:C], op0=ALU.add, op1=ALU.mult)
                then(dve.scalar_tensor_tensor(out=gm[:, t, C:2 * C], in0=th[:, t, 2 * C:3 * C], scalar=1.0,
                                              in1=th[:, t, 0:C], op0=ALU.add, op1=ALU.mult))
                then(dve.tensor_tensor(gs[:, t, :], gm[:, t, 0:C], gm[:, t, C:2 * C], ALU.add))
                dve.scalar_tensor_tensor(out=X5[:, t, :], in0=gs[:, t, :], scalar=0.5, in1=X4[:, t, :],
                                         op0=ALU.mult, op1=ALU.add).then_inc(sem("x5"), 1)

            for i in range(2, B + 5):
                if i - 2 < B:
                    maxima_of("c", i - 2, nmaxc)
                if 0 <= i - 3 < B:
                    turned_p("c", i - 3)
                if i >= 6:
                    x5_of(i - 6)
                if i - 2 < B:
                    b = i - 2
                    dve.wait_ge(sem("att_exp"), 2 * b + 2 + 2 * B)
                    then(dve.reciprocal(rdenc[:, TB * b:TB * b + TB], denc[:, TB * b:TB * b + TB]))
                    for q in range(TB):
                        t = TB * b + q
                        dve.tensor_scalar(S_P[:, b, q, :], S_P[:, b, q, :], rdenc[:, t:t + 1], None, ALU.mult) \
                            .then_inc(sem("c_pn"), 1)
            stats("d", X5, "x5", B // 2, 0)
            x5_of(B - 1)
            stats("d", X5, "x5", B, 1)
            for half in range(2):
                apply("d", X5, half)

            dve.wait_ge(sem("d_xn"), B)
            then(dve.tensor_copy(XH[:, :, :], XN["d"][:, :, 0:C]))
            dve.tensor_tensor(XL[:, :, :], XN["d"][:, :, 0:C], XH[:, :, :].bitcast(F32), ALU.subtract).then_inc(sem("xl"), 1)
            def per_expert(v):
                return v.unsqueeze(2).to_broadcast([P, T, E3])

            rows = bank[4][:, 0:T * E3].rearrange("p (t e) -> p t e", t=T)
            cnt = bank[5][:, 0:T * E3].rearrange("p (t e) -> p t e", t=T)
            dve.wait_ge(sem("logits3"), 1)
            then(dve.tensor_reduce(mx3[:, :], rows, AX.X, ALU.max))
            dve.tensor_tensor(d3[:, :, :], rows, per_expert(mx3[:, :]), ALU.subtract).then_inc(sem("d3"), 1)
            dve.wait_ge(sem("d3"), 1)
            then(dve.tensor_scalar(oh3[:, :, :], d3[:, :, :], 0.0, None, ALU.is_equal))
            rev = Cs[:, CST["rev"]].rearrange("p (t e) -> p t e", t=T)
            first = Cs[:, CST["first"]].rearrange("p (t e) -> p t e", t=T)
            then(dve.tensor_tensor(rv3[:, :, :], oh3[:, :, :], rev, ALU.mult))
            then(dve.tensor_reduce(mr3[:, :], rv3[:, :, :], AX.X, ALU.max))
            dve.tensor_tensor(ohb[:, :, :], rv3[:, :, :], per_expert(mr3[:, :]), ALU.is_equal).then_inc(sem("ohb"), 1)
            dve.wait_ge(sem("ohb"), 1)
            then(dve.tensor_tensor(sel3[:, 1, :, :], ohb[:, :, :], first, ALU.mult))
            dve.wait_ge(sem("ex3"), 1)
            then(dve.tensor_reduce(se3[:, :], ex3[:, :, :], AX.X, ALU.add))
            then(dve.reciprocal(prb[:, :], se3[:, :]))
            dve.wait_ge(sem("counts"), 1)
            then(dve.tensor_tensor(sel3[:, 0, :, :], ohb[:, :, :], cnt, ALU.mult))
            then(dve.tensor_reduce(cf3[:, :, :], sel3[:, :, :, :], AX.X, ALU.add))
            then(dve.tensor_scalar(kept[:, :], cf3[:, 0, :], float(CAP3), None, ALU.is_le))
            then(dve.tensor_tensor(gate3[:, :], prb[:, :], kept[:, :], ALU.mult))
            then(dve.tensor_tensor(sid[:, :], cf3[:, 0, :], cf3[:, 1, :], ALU.add))
            then(dve.tensor_tensor(sid[:, :], sid[:, :], kept[:, :], ALU.mult))
            then(dve.tensor_scalar(sid[:, :], sid[:, :], -1.0, None, ALU.add))
            dve.wait_ge(sem("iota_f"), 1)
            for t in range(T):
                if t >= 2:
                    dve.wait_ge(sem("gathered"), t - 1)
                dve.tensor_scalar(G3[:, t % 2, :], iota_f[:, :], sid[:, t:t + 1], None, ALU.is_equal).then_inc(sem("g3"), 1)
            dve.tensor_tensor(SD[:, :, :], ident.unsqueeze(1).to_broadcast([P, T, P]),
                              sid[:, :].unsqueeze(2).to_broadcast([P, T, P]), ALU.mult).then_inc(sem("sd"), 1)
            dve.wait_ge(sem("sb"), 2)
            slot_no = Cs[:, CST["slot"]]
            for j in range(2):
                dve.tensor_scalar(GT[:, j % 2, :], SB[:, :], slot_no[:, j:j + 1], None, ALU.is_equal).then_inc(sem("gt"), 1)
            dve.wait_ge(sem("yh"), 2)
            dve.tensor_tensor(YL[:, 0:8, :].rearrange("p j c -> p (j c)"), bank[1][:, :],
                              YH[:, 0:8, :].rearrange("p j c -> p (j c)").bitcast(F32), ALU.subtract).then_inc(sem("yl"), 1)
            dve.tensor_tensor(YL[:, 8:10, :].rearrange("p j c -> p (j c)"), bank[2][:, 0:2 * C],
                              YH[:, 8:10, :].rearrange("p j c -> p (j c)").bitcast(F32), ALU.subtract).then_inc(sem("yl"), 1)
            for j in range(2, SLOTS // P):
                dve.wait_ge(sem("scattered"), j - 1)
                dve.tensor_scalar(GT[:, j % 2, :], SB[:, :], slot_no[:, j:j + 1], None, ALU.is_equal).then_inc(sem("gt"), 1)
            for b in range(B):
                t = slice(TB * b, TB * b + TB)
                dve.wait_ge(sem("z_turned"), b + 1)
                then(dve.tensor_tensor(y3[:, t, :], bank[b][:, 0:TB * C].rearrange("p (q c) -> p q c", q=TB),
                                        gate3[:, t].unsqueeze(2).to_broadcast([P, TB, C]), ALU.mult))
                dve.tensor_scalar(fin3[:, t, :], y3[:, t, :], 0.0, 0.0, ALU.mult, ALU.is_equal)
                dve.tensor_scalar(sat3[:, t, :], y3[:, t, :], -1e4, 1e4, ALU.max, ALU.min)
                then(dve.tensor_tensor(nan3[:, t, :], y3[:, t, :], y3[:, t, :], ALU.is_equal))
                then(dve.tensor_tensor(sat3[:, t, :], sat3[:, t, :], nan3[:, t, :], ALU.mult))
                then(dve.copy_predicated(sat3[:, t, :], fin3[:, t, :], y3[:, t, :]))
                dve.tensor_tensor(Y6[:, t, :], sat3[:, t, :], X5[:, t, :], ALU.add).then_inc(sem("y6"), 1)


def pack(pairs, where, rows, width):
    a = np.zeros((rows, width), np.float32)
    for name, value in pairs.items():
        a[:value.shape[0], where[name]] = value
    return a


def with_bias(w, b):
    return np.concatenate([w, b[None, :]], 0)


def bias_tables(rpb):
    q = np.full((P, NH, TB, SPAN), MASKED, np.float32)
    k = np.full((P, NH, TB, SPAN), MASKED, np.float32)
    start = np.array([window_start(i) for i in range(HW)])
    n = np.arange(N)
    i, j = n // HW, n % HW
    ok = (i[None] >= start[i][:, None]) & (i[None] < start[i][:, None] + WIN) & \
         (j[None] >= start[j][:, None]) & (j[None] < start[j][:, None] + WIN)
    full = np.full((NH, N, N), MASKED, np.float32)
    qi, ki = np.nonzero(ok)
    full[:, qi, ki] = rpb[:, i[ki] - i[qi] + WIN - 1, j[ki] - j[qi] + WIN - 1]
    for s in range(TB):
        q[:, :, s, :] = full[:, s * P:s * P + P, OFF[s]:OFF[s] + SPAN].transpose(1, 0, 2)
        k[:, :, s, :] = full[:, OFF[s]:OFF[s] + SPAN, s * P:s * P + P].transpose(2, 0, 1)
    return q.reshape(P, NH, TB * SPAN), k.reshape(P, NH, TB * SPAN)


def kernel(**inputs):
    import concourse.bacc as bacc
    from concourse.bass_utils import run_bass_kernel_spmd

    a = {k: np.ascontiguousarray(np.asarray(v)) for k, v in inputs.items()}
    p = np.arange(P)
    pair = np.zeros((C, C), np.float32)
    for c in range(C):
        pair[c, c // 2 * 2:c // 2 * 2 + 2] = 0.5
    cst = pack({
        "ident": np.eye(P, dtype=np.float32),
        "prefix": (p[:, None] <= p[None]).astype(np.float32),
        "pair": pair,
        "rev": np.tile(np.arange(E3, 0, -1, dtype=np.float32), (P, T)),
        "scale": np.where(p < C, float(HD) ** -0.5, 1.0).astype(np.float32)[:, None],
        "first": np.tile(np.arange(E3, dtype=np.float32) * CAP3, (P, T)),
        "slot": (p[:, None] + P * np.arange(10)[None]).astype(np.float32),
    }, CST, P, CST_W)
    w8 = np.concatenate([with_bias(a["L0_conv_wq"], a["L0_conv_bq"]).T,
                         with_bias(a["L0_conv_wk"], a["L0_conv_bk"]).T], 1)
    wvT = np.zeros((C1, C1), np.float32)
    wvT[:C] = with_bias(a["L0_conv_wv"], a["L0_conv_bv"]).T
    wvT[C, C] = 1.0
    w0 = pack({
        "wvT": wvT, "wo": with_bias(a["L0_conv_wo"], a["L0_conv_bo"]),
        "wqk1": with_bias(np.concatenate([a["L1_conv_wq"].T, a["L1_conv_wk"].T], 1),
                          np.concatenate([a["L1_conv_bq"], a["L1_conv_bk"]])),
        "wv1": with_bias(a["L1_conv_wv"].T, a["L1_conv_bv"]),
    }, W0, C1, W0_W)
    bias_q, bias_k = bias_tables(a["L1_conv_rpb"])
    att = a["L3_attn_att_w"]
    y3 = np.zeros((C1, C1), np.float32)
    y3[np.arange(C), np.arange(C)] = att[2 * C:]
    y3[C, :C] = att[C:2 * C]
    y3[:C, C] = att[:C]
    gw = np.concatenate([a["L3_attn_z_w"], a["L3_attn_r_w"], a["L3_attn_f_w"]], 0)
    gbias = np.concatenate([a["L3_attn_z_b"], a["L3_attn_r_b"], a["L3_attn_f_b"]])
    wa = pack({
        "w1": np.concatenate([a["L2_ffn_W1"].transpose(1, 0, 2).reshape(C, E2 * F2), a["L2_ffn_b1"].reshape(1, E2 * F2)]),
        "wr": with_bias(a["L2_ffn_Wr"], a["L2_ffn_br"]),
        "b2": a["L2_ffn_b2"].T,
        "y3": y3,
        "gx": with_bias(gw[:, :C].T, gbias),
        "ga": gw[:, C:].T,
        "gate": with_bias(a["L3_ffn_gate_w"], a["L3_ffn_gate_b"]),
        "fb2": a["L3_ffn_b2"].T,
    }, WA, C1, WA_W)
    arrays = {
        "x": a["x"].reshape(B, N, C), "w8": w8, "w0": w0, "wa": wa,
        "w3": np.concatenate([a["L3_ffn_w1"].transpose(1, 0, 2), a["L3_ffn_b1"][None]], 0),
        "w2a": a["L2_ffn_W2"].transpose(1, 0, 2),
        "w2b": a["L3_ffn_w2"].reshape(E3, 2, P, C).transpose(2, 0, 1, 3),
        "cst": cst, "bias_q": bias_q, "bias_k": bias_k,
        "lnw": np.stack([a["L2_ffn_gamma"], a["L2_ffn_beta"]]),
    }
    arrays = {k: np.ascontiguousarray(v) for k, v in arrays.items()}
    nc = bacc.Bacc("TRN2", target_bir_lowering=False, num_devices=1)
    args = {n: nc.dram_tensor(n, v.shape, F32, kind="ExternalInput").ap() for n, v in arrays.items()}
    args["out"] = nc.dram_tensor("out", (B, N, C), F32, kind="ExternalOutput").ap()
    hybrid_kernel(nc, **args)
    r = run_bass_kernel_spmd(nc, [arrays], core_ids=[0])
    return r.results[0]["out"].reshape(B, HW, HW, C)
```

```python
from contextlib import ExitStack

import numpy as np
import concourse.bass as bass
from concourse import mybir

P = 128
B, HW, C = 4, 16, 64
N = HW * HW
TB = N // P
T = B * TB
C1 = C + 1
D0 = C // 8
NH, HD, WIN = 8, 8, 7
SPAN = (P // HW + WIN // 2) * HW
OFF = (0, N - SPAN)
NT = 9
KS = NT * HD
VW = 32
MASKED = -1e30
PE_HEADS = (1, 4, 7)
E2, F2, TOPK = 8, 128, 2
CAP2 = float(-(-B * N * 5 // (4 * E2)))
E3, F3 = 8, 256
CAP3 = -(-B * N * 5 // (4 * E3))
SLOTS = E3 * CAP3
HALF = SLOTS // P // 2
LN_EPS = 1e-5
FLT_MAX = 3.4028234663852886e38

F32, F32R, BF16, I32, U32 = (mybir.dt.float32, mybir.dt.float32r, mybir.dt.bfloat16,
                             mybir.dt.int32, mybir.dt.uint32)
ALU = mybir.AluOpType
ACT = mybir.ActivationFunctionType
AX = mybir.AxisListType


def window_start(i):
    return min(max(i - WIN // 2, 0), HW - WIN)


def columns(*pairs):
    at, where = 0, {}
    for name, width in pairs:
        where[name] = slice(at, at + width)
        at += width
    return where, at


CST, CST_W = columns(("ident", P), ("prefix", P), ("pair", C), ("rev", T * E3), ("scale", 1),
                     ("first", T * E3), ("slot", 10), ("expert", T * E3), ("fb1", E3 * 2), ("twice", C))
W0, W0_W = columns(("wvT", C1), ("wo", C), ("wqk1", 2 * C), ("wv1", C))
WA, WA_W = columns(("w1", E2 * F2), ("wr", E2), ("b2", E2), ("y3", C1), ("gx", 3 * C), ("ga", 3 * C),
                   ("gate", E3), ("fb2", E3))


def hybrid_kernel(nc, x, w8, w0, wa, w3, w2a, w2b, cst, bias_q, bias_k, lnw, out):
    ctx = ExitStack()
    with ctx:
        def sb(name, shape, dt=F32):
            return ctx.enter_context(nc.sbuf_tensor(name, shape, dt))

        sems = {}

        def sem(name):
            if name not in sems:
                sems[name] = ctx.enter_context(nc.semaphore(name))
            return sems[name]

        bank = [ctx.enter_context(nc.psum_tensor(f"bank{i}", [P, 512], F32)) for i in range(8)]

        q_parts = nc.dram_tensor("q_parts", (B, 3, C, N), BF16, kind="Internal").ap()
        k_parts = nc.dram_tensor("k_parts", (B, 5, C, N), BF16, kind="Internal").ap()

        W8 = sb("W8", [D0, 2 * C1])
        W0s = sb("W0s", [C1, W0_W])
        Cs = sb("Cs", [P, CST_W])
        identb = sb("identb", [P, P], BF16)
        onesb = sb("onesb", [P, P], BF16)
        bias_mem = sb("bias_mem", [P, 2 * NH * TB * SPAN])
        mid_mem = sb("mid_mem", [P, 7232])
        half_mem = sb("half_mem", [P, 4992])
        stack_mem = sb("stack_mem", [P, B * NH * N])
        taken = {}

        def view(mem, *shape):
            at = taken.get(id(mem), 0)
            size = int(np.prod(shape[1:]))
            taken[id(mem)] = at + size
            v = mem[0:shape[0], at:at + size]
            if len(shape) == 3:
                return v.rearrange("p (a b) -> p a b", a=shape[1])
            return v.rearrange("p (a b c) -> p a b c", a=shape[1], b=shape[2]) if len(shape) == 4 else v

        def view16(mem, *shape):
            at = taken.get(id(mem), 0)
            size = int(np.prod(shape[1:])) // 2
            taken[id(mem)] = at + size
            v = mem[0:shape[0], at:at + size].bitcast(BF16)
            if len(shape) == 3:
                return v.rearrange("p (a b) -> p a b", a=shape[1])
            return v.rearrange("p (a b c) -> p a b c", a=shape[1], b=shape[2]) if len(shape) == 4 else v

        biasQb = view16(half_mem, P, NH, TB * SPAN)
        biasQ = view(bias_mem, P, NH, TB * SPAN)
        biasK = view(bias_mem, P, NH, TB * SPAN)
        pb = TB * SPAN * len(PE_HEADS)
        bias_rest = bias_mem[:, 0:pb].rearrange("p (h s) -> p h s", h=len(PE_HEADS))
        bias_part = bias_mem[:, pb:pb * 5 // 2].bitcast(BF16).rearrange("p (i h s) -> p i h s", i=3, h=len(PE_HEADS))
        mhalf = sb("mhalf", [P, T])
        ident = Cs[:, CST["ident"]]

        X = sb("X", [P, T, C1])
        XT = sb("XT", [C1, B * N])
        A0 = sb("A0", [C1, C1])
        Wvo = sb("Wvo", [C1, C])
        G0 = sb("G0", [C1, B * N])
        S_P = sb("S_P", [P, B, TB, N])
        S_PT = sb("S_PT", [P, B, TB, N])
        nmax = sb("nmax", [P, T])
        den = sb("den", [P, T])
        rden = sb("rden", [P, T])
        CT = sb("CT", [C1, B * N])
        X1 = sb("X1", [P, T, C])

        gn_st = sb("gn_st", [C, B, 6])
        gn_mv = sb("gn_mv", [C, B, 3])
        gn_g = sb("gn_g", [C, B, 3])
        gn_v = sb("gn_v", [C, B])
        gn_sq = sb("gn_sq", [C, B])
        gn_r = sb("gn_r", [C, B])
        gn_nb = sb("gn_nb", [C, B])
        XN1 = sb("XN1", [C1, B * N])
        QK = view(mid_mem, P, B * N)
        qkr = view(mid_mem, P, B * N)
        part = view16(half_mem, P, 3, B * N)
        words = B * NH * N // 2
        QS, KSt = [stack_mem[0:KS, k * words:(k + 1) * words].bitcast(BF16)
                   .rearrange("r (b h n) -> r b h n", b=B, h=NH) for k in range(2)]
        V1 = view(mid_mem, P, T, NH, VW)
        nm1 = sb("nm1", [P, B, NH, TB], BF16)
        diag1 = view16(half_mem, P, 2, NH, TB * P)
        U1 = view(mid_mem, P, 3, TB * SPAN)
        P1 = view(mid_mem, P, 3, TB * SPAN)
        CT1 = view(mid_mem, P, 2, 512)
        rz1 = sb("rz1", [P, 2, TB * 2, 4])
        ctx1 = sb("ctx1", [P, 2, TB * 2, 4, HD])
        X2 = sb("X2", [P, T, C])

        taken.clear()
        LN = "abucd"
        LN_STEPS = [("a", TB * b, TB) for b in range(B)] + \
                   [(s, h * T // 2, T // 2) for s in "bucd" for h in range(2)]
        ln_st = {s: sb("ln_st" + s, [P, T, 6]) for s in LN}
        ln_mv = {s: sb("ln_mv" + s, [P, T, 2]) for s in LN}
        ln_ve = {s: sb("ln_ve" + s, [P, T]) for s in LN}
        ln_rs = {s: sb("ln_rs" + s, [P, T]) for s in LN}
        XN = {s: sb("XN" + s, [P, T, C1]) for s in "abc"}
        XF = {s: sb("XF" + s, [C1, B * N]) for s in "ab"}
        XN["u"], XN["d"] = XN["a"], XN["b"]
        XF["c"], XF["d"] = XF["a"], XF["b"]
        LHSa = XT
        LHSc = G0
        CTa = XN1[0:C, :]
        CTc = CT
        nmaxa = sb("nmaxa", [P, T])
        dena = sb("dena", [P, T])
        rdena = sb("rdena", [P, T])
        nmaxc = sb("nmaxc", [P, T])
        denc = sb("denc", [P, T])
        rdenc = sb("rdenc", [P, T])
        X3 = sb("X3", [P, T, C])
        WAs = sb("WAs", [C1, WA_W])
        W2A = view(half_mem, P, E2, C)
        msum = sb("msum", [C, B])
        mean2 = sb("mean2", [C1, B])
        lg = sb("lg", [B, 8, E2])
        col = sb("col", [B, 10])
        top_i = sb("top_i", [B, 8], U32)
        spread = sb("spread", [B, 2, B, TOPK])
        loads1 = sb("loads1", [B, B])
        ones4 = sb("ones4", [B, P])
        tw = sb("tw", [P, B * TOPK])
        slot_e = sb("slot_e", [1, B * TOPK], I32)
        W1sel = view(stack_mem, C1, B * TOPK, F2)
        W2sel = view(stack_mem, P, B * TOPK, C)
        chosen = sb("chosen", [P, B * TOPK])
        b2w = sb("b2w", [C, B * TOPK, E2])
        b2sel = sb("b2sel", [C, B])
        H2 = view(bias_mem, P, B, TOPK * N)
        UT = view(half_mem, C, B * N)
        U = view(mid_mem, P, T, C)
        gb = sb("gb", [P, 2, C])
        X3b = view(mid_mem, P, T, C)
        un = view(stack_mem, P, T, C)
        X4 = view(half_mem, P, T, C)
        th = view(stack_mem, P, T, 3 * C)
        gm = view(stack_mem, P, T, 2 * C)
        gs = sb("gs", [P, T, C])
        X5 = view(bias_mem, P, T, C)
        W3s = view(mid_mem, P, E3, F3)
        W2B = view(mid_mem, P, E3, 2, C)
        mx3 = sb("mx3", [P, T])
        d3 = sb("d3", [P, T, E3])
        ex3 = sb("ex3", [P, T, E3])
        prb = sb("prb", [P, T])
        se3 = sb("se3", [P, T])
        rv3 = sb("rv3", [P, T, E3])
        mr3 = sb("mr3", [P, T])
        oh3 = sb("oh3", [P, T, E3])
        ohb = sb("ohb", [P, T, E3], BF16)
        prefixb = sb("prefixb", [P, P], BF16)
        sel3 = sb("sel3", [P, 2, T, E3])
        cf3 = sb("cf3", [P, 2, T])
        kept = sb("kept", [P, T])
        gate3 = sb("gate3", [P, T])
        sid = sb("sid", [P, T])
        iota_f = view(half_mem, P, SLOTS)
        XHL = sb("XHL", [P, T, 2, C], F32R)
        one_hot = sb("one_hot", [P, 4 * T * P], F32R)
        G3 = one_hot[:, 0:3 * SLOTS].rearrange("p (k s) -> p k s", k=3)
        GT = one_hot[:, :].rearrange("p (k n) -> p k n", k=4)
        XB = view(stack_mem, P, SLOTS)
        H3 = view(bias_mem, P, 3, 2, CAP3)
        YT = view(stack_mem, C, SLOTS)
        YHL = sb("YHL", [P, SLOTS // P, 2, C], F32R)
        twice = sb("twice", [P, C], F32R)
        onesf = sb("onesf", [P, P])
        SD = view(bias_mem, P, T, P)
        SB = view(bias_mem, P, T * P)
        ZT = XHL[:, :, :, :].rearrange("p t k c -> p (t k c)")
        y3 = view(mid_mem, P, T, C)
        sat3 = view(mid_mem, P, T, C)
        nan3 = view(mid_mem, P, T, C)
        wild3 = sb("wild3", [P, T, C])
        Y6 = view(mid_mem, P, T, C)
        table = sb("table", [1, 1])

        def by_dve(n):
            return n - sum(k % NH in PE_HEADS for k in range(n))

        def through(s):
            return B if s == "c" else 0

        UP3 = ((bank[3], bank[4]), (bank[5], bank[2]))
        TURN_Y = (bank[6], bank[3])

        block = ctx.enter_context(nc.Block())

        x_t = x.rearrange("b (q p) c -> b p q c", p=P)
        o_t = out.rearrange("b (q p) c -> b p q c", p=P)

        def final(sp):
            for b in range(0, B, 2):
                sp.wait_ge(sem("y6"), b + 2)
                for k in range(2):
                    sp.dma_start(o_t[b + k], Y6[:, TB * (b + k):TB * (b + k) + TB, :]).then_inc(sem("out_stored"), 16)
            sp.wait_ge(sem("out_stored"), 16 * B)

        @block.sync
        def _(sp):
            sp.dma_start(X[:, 0:TB, 0:C], x_t[0]).then_inc(sem("x_landed0"), 16)
            sp.dma_start(Cs[:, :], cst).then_inc(sem("cst_landed"), 16)
            for b in range(1, B):
                sp.dma_start(X[:, TB * b:TB * b + TB, 0:C], x_t[b]).then_inc(sem(f"x_landed{b}"), 16)
            sp.dma_start(biasQ[:, :, :], bias_q).then_inc(sem("biasQ_landed"), 16)
            sp.dma_start(biasK[:, :, :], bias_k).then_inc(sem("biasK_landed"), 16)
            sp.dma_start(WAs[:, :], wa).then_inc(sem("wa_landed"), 16)
            for b in range(B):
                cols = slice(b * N, b * N + N)
                sp.wait_ge(sem("qk_part"), 3 * b + 3)
                sp.dma_start(q_parts[b].rearrange("i r n -> r i n"), part[0:C, :, cols]) \
                    .then_inc(sem(f"parts_stored{b}"), 16)
                for first, parts in ((0, 3), (3, 2)):
                    sp.dma_start(k_parts[b, first:first + parts].rearrange("i r n -> r i n"),
                                 part[C:2 * C, 0:parts, cols]).then_inc(sem(f"parts_stored{b}"), 16)
                sp.wait_ge(sem(f"parts_stored{b}"), 48)
                q_rows = q_parts[b].rearrange("i (d h) n -> (i d) (h n)", h=NH)
                k_rows = k_parts[b].rearrange("i (d h) n -> (i d) (h n)", h=NH)
                for a in range(3):
                    rows = slice(3 * HD * a, 3 * HD * a + 3 * HD)
                    sp.dma_start(QS[rows, b, :, :].rearrange("r h n -> r (h n)"), q_rows) \
                        .then_inc(sem(f"stack_landed{b}"), 16)
                    sp.dma_start(KSt[rows, b, :, :].rearrange("r h n -> r (h n)"), k_rows[HD * a:HD * a + 3 * HD]) \
                        .then_inc(sem(f"stack_landed{b}"), 16)
            sp.wait_ge(sem("x2_done"), B)
            sp.dma_start(W2A[:, :, :], w2a).then_inc(sem("w2a_landed"), 16)
            sp.dma_start(gb[:, :, :], lnw.unsqueeze(0).to_broadcast([P, 2, C])).then_inc(sem("gb_landed"), 16)
            sp.dma_start(W3s[:, :, :], w3).then_inc(sem("w3_landed"), 16)
            sp.dma_start(W2B[:, :, :, :], w2b).then_inc(sem("w2b_landed"), 16)
            final(sp)

        @block.gpsimd
        def _(pool):
            for k, (tile, value) in enumerate([
                    (XT[C:C1, :], 1.0), (X[:, :, C:C1], 1.0), (XN1[C:C1, :], 1.0), (mhalf[:, :], -0.5),
                    (V1[:, :, :, HD:VW], 0.0), (V1[:, :, :, HD:HD + 1], 1.0)]):
                if k:
                    pool.wait_ge(sem("pool_const"), k)
                pool.memset(tile, value).then_inc(sem("pool_const"), 1)
            pool.wait_ge(sem("cst_landed"), 16)
            pool.tensor_copy(identb[:, :], ident).then_inc(sem("pool_const"), 1)
            pool.wait_ge(sem("biasQ_landed"), 16)
            pool.tensor_copy(biasQb[:, :, :], biasQ[:, :, :]).then_inc(sem("pool_const"), 1)
            pool.wait_ge(sem("biasK_landed"), 16)
            pool.wait_ge(sem("pool_const"), 8)
            some_heads = slice(PE_HEADS[0], NH, PE_HEADS[1] - PE_HEADS[0])
            pool.tensor_copy(bias_part[:, 0, :, :], biasK[:, some_heads, :]).then_inc(sem("bias_part"), 1)
            pool.wait_ge(sem("bias_part"), 1)
            pool.tensor_tensor(bias_rest[:, :, :], biasK[:, some_heads, :], bias_part[:, 0, :, :], ALU.subtract) \
                .then_inc(sem("bias_part"), 1)
            pool.wait_ge(sem("gn_step"), 2)
            pool.tensor_tensor(gn_r[:, :], gn_v[:, :], mhalf[0:C, 0:B], ALU.pow).then_inc(sem("gn_rstd"), 1)
            pool.wait_ge(sem("bias_part"), 2)
            pool.tensor_copy(bias_part[:, 1, :, :], bias_rest[:, :, :]).then_inc(sem("bias_part"), 1)
            pool.wait_ge(sem("bias_part"), 3)
            pool.tensor_tensor(bias_part[:, 2, :, :], bias_rest[:, :, :], bias_part[:, 1, :, :], ALU.subtract) \
                .then_inc(sem("bias_part"), 1)
            for k, (tile, value) in enumerate([
                    (XN["c"][:, :, C:C1], 1.0), (onesf[:, :], 1.0), (XF["a"][C:C1, :], 1.0),
                    (XF["b"][C:C1, :], 1.0),
                    (mean2[C:C1, :], 1.0), (ones4[:, :], 1.0), (loads1[:, :], float(N))]):
                if k:
                    pool.wait_ge(sem("later_const"), k)
                pool.memset(tile, value).then_inc(sem("later_const"), 1)
            pool.tensor_copy(prefixb[:, :], Cs[:, CST["prefix"]]).then_inc(sem("later_const"), 1)
            def rstd(s, half=0):
                n = LN_STEPS.index((s, half * T // 2, T // 2) if s != "a" else (s, TB * half, TB))
                t = slice(LN_STEPS[n][1], LN_STEPS[n][1] + LN_STEPS[n][2])
                pool.wait_ge(sem("ln_mv"), n + 1)
                pool.tensor_scalar(ln_ve[s][:, t], ln_mv[s][:, t, 1], LN_EPS, None, ALU.add).then_inc(sem("ln_ve"), 1)
                pool.wait_ge(sem("ln_ve"), n + 1)
                pool.tensor_tensor(ln_rs[s][:, t], ln_ve[s][:, t], mhalf[:, t], ALU.pow).then_inc(sem("ln_rs"), 1)

            for b in range(B):
                for h in range(NH):
                    pool.wait_ge(sem("nm1"), b * NH + h + 1)
                    if b >= 2:
                        pool.wait_ge(sem("s1"), (b - 2) * NH + h + 1)
                    pool.tensor_tensor(
                        diag1[:, b % 2, h, :].rearrange("p (q k) -> p q k", q=TB),
                        identb[:, :].unsqueeze(1).to_broadcast([P, TB, P]),
                        nm1[:, b, h, :].unsqueeze(2).to_broadcast([P, TB, P]), ALU.mult) \
                        .then_inc(sem("diag1"), 1)
                    if h == 1 and b == B - 1:
                        rstd("a", 0)
            for b in range(1, B):
                rstd("a", b)
            pool.wait_ge(sem("x2_done"), B)
            pool.iota(iota_f[:, :], [[1, SLOTS]], base=0, channel_multiplier=0,
                      allow_small_or_imprecise_dtypes=True).then_inc(sem("later_const"), 1)
            for half in range(2):
                rstd("b", half)
            pool.wait_ge(sem("gb_landed"), 16)
            pool.tensor_tensor(X3b[:, :, :], X3[:, :, :], gb[:, 1, :].unsqueeze(1).to_broadcast([P, T, C]), ALU.add) \
                .then_inc(sem("x3b"), 1)
            for half in range(2):
                rstd("u", half)
            for half in range(2):
                rstd("c", half)
            for half in range(2):
                rstd("d", half)
            pool.wait_ge(sem("sid"), 1)
            pool.tensor_tensor(SD[:, :, :], ident.unsqueeze(1).to_broadcast([P, T, P]),
                               sid[:, :].unsqueeze(2).to_broadcast([P, T, P]), ALU.mult).then_inc(sem("sd"), 1)
            for h in range(2):
                t = slice(h * T // 2, (h + 1) * T // 2)
                pool.wait_ge(sem("y3"), h + 1)
                pool.tensor_tensor(Y6[:, t, :], y3[:, t, :], X5[:, t, :], ALU.add).then_inc(sem("sum3"), 1)

        @block.tensor
        def _(pe):
            def keep_warm(n, idle):
                for _ in range(n):
                    pe.matmul(idle[:, :].rearrange("p (k q) -> p k q", k=4), onesb[:, :],
                              onesb[:, :].unsqueeze(1).to_broadcast([P, 4, P]), start=True, stop=True)

            pe.wait_ge(sem("onesb"), 1)
            keep_warm(8, bank[2])
            pe.wait_ge(sem("w8_landed"), 16)
            pe.matmul(bank[6][0:C1, 0:C1], W8[:, 0:C1], W8[:, C1:2 * C1], start=True, stop=True) \
                .then_inc(sem("a0"), 1)
            pe.wait_ge(sem("w0_landed"), 16)
            pe.matmul(bank[7][0:C1, 0:C], W0s[:, W0["wvT"]], W0s[:, W0["wo"]], start=True, stop=True) \
                .then_inc(sem("wvo"), 1)
            pe.wait_ge(sem("cst_landed"), 16)

            def transposes(b, src, ready, count, done):
                pe.wait_ge(sem(ready), count)
                for q in range(TB):
                    last = pe.transpose(bank[b][0:C, q * P:q * P + P], src[:, TB * b + q, 0:C], ident)
                last.then_inc(sem(done), 1)

            def scores(b, lhs, rhs):
                for q in range(TB):
                    last = pe.matmul(bank[4 + b % 2][:, q * N:q * N + N], lhs[:, b * N + q * P:b * N + q * P + P],
                                     rhs[:, b * N:b * N + N], start=True, stop=True)
                return last

            def transpose_p(b):
                for k in range(TB):
                    for q in range(TB):
                        last = pe.transpose(bank[6 + b % 2][:, k * N + q * P:k * N + q * P + P],
                                            S_P[:, b, q, k * P:k * P + P], ident)
                return last

            def attend(b, values, width):
                for k in range(TB):
                    last = pe.matmul(bank[2 + b % 2][0:width, 0:N], values[:, TB * b + k, 0:width],
                                     S_PT[:, b, k, :], start=(k == 0), stop=(k == TB - 1))
                return last

            for b in range(B):
                pe.wait_ge(sem("x_landed" + str(b)), 16)
                if b == 0:
                    pass
                for q in range(TB):
                    last = pe.transpose(bank[b % 2][0:C, q * P:q * P + P] if b < 2 else
                                        bank[b][0:C, q * P:q * P + P], X[:, TB * b + q, 0:C], ident)
                last.then_inc(sem("xt_p"), 1)
            for b in range(B):
                pe.wait_ge(sem("xt"), b + 1)
                if b == 0:
                    pe.wait_ge(sem("pool_const"), 1)
                    pe.wait_ge(sem("a0_s"), 1)
                if b >= 2:
                    pe.wait_ge(sem("xt"), 4)
                pe.matmul(bank[b][0:C1, 0:N], A0[:, :], XT[:, b * N:b * N + N], start=True, stop=True) \
                    .then_inc(sem("g0_p"), 1)
            for i in range(B + 3):
                if i < B:
                    pe.wait_ge(sem("g0"), i + 1)
                    if i >= 2:
                        pe.wait_ge(sem("exp0"), 2 * (i - 1))
                    scores(i, G0, XT).then_inc(sem("s0"), 1)
                if 0 <= i - 1 < B:
                    b = i - 1
                    pe.wait_ge(sem("exp0"), 2 * b + 2)
                    if b == 0:
                        pe.wait_ge(sem("a0_s"), 1)
                        pe.wait_ge(sem("wvo_s"), 1)
                    if b >= 2:
                        pe.wait_ge(sem("pt0"), b - 1)
                    transpose_p(b).then_inc(sem("pt0_p"), 1)
                if 0 <= i - 2 < B:
                    b = i - 2
                    pe.wait_ge(sem("pt0"), b + 1)
                    if b == 0:
                        pe.wait_ge(sem("pool_const"), 2)
                        pe.wait_ge(sem("g0"), 4)
                    if b >= 2:
                        pe.wait_ge(sem("ct0"), b - 1)
                    attend(b, X, C1).then_inc(sem("ct0_p"), 1)
                if 0 <= i - 3 < B:
                    b = i - 3
                    pe.wait_ge(sem("ct0"), b + 1)
                    if b >= 2:
                        pe.wait_ge(sem("x1"), b - 1)
                    for q in range(TB):
                        last = pe.matmul(bank[b % 2][:, q * C:q * C + C], CT[:, b * N + q * P:b * N + q * P + P],
                                         Wvo[:, :], start=True, stop=True)
                    last.then_inc(sem("o0"), 1)

            for b in range(B):
                pe.wait_ge(sem("x1"), b + 1)
                for q in range(TB):
                    last = pe.transpose(bank[4 + b][0:C, q * P:q * P + P], X1[:, TB * b + q, :], ident)
                last.then_inc(sem("x1t_p"), 1)
            pe.wait_ge(sem("gn_step"), 1)
            pe.matmul(bank[0][0:C, 0:3 * B], Cs[0:C, CST["pair"]], gn_mv[:, :, :].rearrange("c b k -> c (b k)"),
                      start=True, stop=True).then_inc(sem("gn_pair"), 1)
            keep_warm(4, bank[1])
            for b in range(B):
                pe.wait_ge(sem("xn1_a" if b % 2 else "xn1"), b // 2 + 1)
                if b == 0:
                    pe.wait_ge(sem("pool_const"), 6)
                pe.matmul(bank[b][:, 0:N], W0s[:, W0["wqk1"]], XN1[:, b * N:b * N + N], start=True, stop=True) \
                    .then_inc(sem("qk_p"), 1)
            for t in range(T):
                last = pe.matmul(bank[4][:, t * C:t * C + C], XN1[:, t * P:t * P + P], W0s[:, W0["wv1"]],
                                 start=True, stop=True)
            last.then_inc(sem("v1_p"), 1)

            def max_scores(b, h):
                n = b * NH + h
                if n == 0:
                    keep_warm(20, bank[7])
                if h == 0:
                    pe.wait_ge(sem(f"stack_landed{b}"), 6 * 16)
                    if b == 0:
                        pe.wait_ge(sem("pool_const"), 8)
                        pe.wait_ge(sem("qkf"), B)
                if n >= 2:
                    pe.wait_ge(sem("nm1"), n - 1)
                for q in range(TB):
                    dst = bank[n % 2][:, q * SPAN:q * SPAN + SPAN]
                    pe.matmul(dst, QS[:, b, h, q * P:q * P + P], KSt[:, b, h, OFF[q]:OFF[q] + SPAN],
                              start=True, stop=False)
                    last = pe.matmul(dst, identb[:, :], biasQb[:, h, q * SPAN:q * SPAN + SPAN],
                                     start=False, stop=True)
                last.then_inc(sem("mx1"), 1)

            def exact_scores(b, h):
                n = b * NH + h
                pe.wait_ge(sem("diag1"), n + 1)
                if n >= 2:
                    if (n - 2) % NH in PE_HEADS:
                        pe.wait_ge(sem("p1"), n - 1)
                    else:
                        pe.wait_ge(sem("u1"), by_dve(n - 2) + 1)
                if n == PE_HEADS[0]:
                    pe.wait_ge(sem("bias_part"), 4)
                for k in range(TB):
                    span = slice(k * SPAN, k * SPAN + SPAN)
                    dst = bank[2 + n % 2][:, span]
                    pe.matmul(dst, KSt[:, b, h, k * P:k * P + P], QS[:, b, h, OFF[k]:OFF[k] + SPAN],
                              start=True, stop=False)
                    if h in PE_HEADS:
                        for i in range(3):
                            pe.matmul(dst, identb[:, :], bias_part[:, i, PE_HEADS.index(h), span], start=False, stop=False)
                    last = pe.matmul(dst, onesb[:, :], diag1[:, b % 2, h, OFF[k]:OFF[k] + SPAN],
                                     start=False, stop=True)
                last.then_inc(sem("s1"), 1)

            def attend1(b, h):
                n = b * NH + h
                pe.wait_ge(sem("p1"), n + 1)
                if n == 0:
                    pe.wait_ge(sem("v1"), 1)
                if h == 0 and b >= 2:
                    pe.wait_ge(sem("ct1"), b - 1)
                g, c0 = h % 4, (h // 4) * N
                for k in range(TB):
                    last = pe.matmul(bank[4 + b % 2][32 * g:32 * g + VW, c0 + OFF[k]:c0 + OFF[k] + SPAN],
                                     V1[:, TB * b + k, h, :], P1[:, n % 3, k * SPAN:k * SPAN + SPAN],
                                     start=(k == 0), stop=(k == TB - 1), skip_group_check=True)
                last.then_inc(sem("av1"), 1)

            def turn1(b):
                pe.wait_ge(sem("ct1"), b + 1)
                if b >= 1:
                    pe.wait_ge(sem("ctx1"), b)
                for q in range(TB):
                    for g in range(2):
                        j = q * 2 + g
                        last = pe.transpose(bank[6][:, j * P:j * P + P],
                                            CT1[:, b % 2, g * N + q * P:g * N + q * P + P], ident)
                last.then_inc(sem("turn1"), 1)

            LAG = 2
            for h in range(NH):
                max_scores(0, h)
            for n in range(B * NH + LAG):
                b, h = divmod(n, NH)
                if b < B:
                    if b + 1 < B:
                        max_scores(b + 1, h)
                    exact_scores(b, h)
                m = n - LAG
                if m >= 0:
                    attend1(m // NH, m % NH)
                    if m % NH == 2 and m // NH >= 1:
                        turn1(m // NH - 1)

            def features(s, b, i):
                pe.wait_ge(sem(s + "_xn"), b + 1)
                for q in range(TB):
                    last = pe.transpose(bank[i][0:C, q * P:q * P + P], XN[s][:, TB * b + q, 0:C], ident)
                last.then_inc(sem(s + "_xf_p"), 1)

            def self_attention(s, lhs, width, hand_on, warm, middle=None):
                for i in range(B + 5):
                    keep_warm(warm.get(i, 0), bank[7])
                    if s == "a" and i == 2:
                        turn1(B - 1)
                    if 0 <= i - 2 < B:
                        b = i - 2
                        pe.wait_ge(sem("c_lhs" if middle else "a_xf"), b + 1)
                        if b == 0:
                            pe.wait_ge(sem("later_const"), 7)
                        if b >= 2:
                            pe.wait_ge(sem("att_exp"), 2 * through(s) + 2 * (b - 1))
                        scores(b, lhs, XF[s]).then_inc(sem("att_s"), 1)
                    if i < B:
                        if i >= 2:
                            pe.wait_ge(sem(s + "_xf"), i - 1)
                        elif s == "a":
                            pe.wait_ge(sem("nm1"), B * NH - 1 + i)
                        features(s, i, i % 2)
                    if middle and 0 <= i - 1 < B:
                        middle(i - 1)
                    if 0 <= i - 3 < B:
                        b = i - 3
                        pe.wait_ge(sem("c_pn" if s == "c" else "att_exp"), 2 * b + 2)
                        if b >= 2:
                            pe.wait_ge(sem("att_pt"), through(s) + b - 1)
                        transpose_p(b).then_inc(sem("att_pt_p"), 1)
                    if 0 <= i - 4 < B:
                        b = i - 4
                        pe.wait_ge(sem("att_pt"), through(s) + b + 1)
                        if b >= 2:
                            pe.wait_ge(sem("att_ct"), through(s) + b - 1)
                        attend(b, XN[s], width).then_inc(sem("att_ct_p"), 1)
                    if 0 <= i - 5:
                        hand_on(i - 5)

            def hand_on_a(b):
                pe.wait_ge(sem("att_ct"), b + 1)
                if b == 0:
                    pe.wait_ge(sem("a_xf"), B)
                if b >= 2:
                    pe.wait_ge(sem("x3"), b - 1)
                for q in range(TB):
                    last = pe.transpose(bank[b % 2][:, q * C:q * C + C], CTa[:, b * N + q * P:b * N + q * P + P],
                                        ident[0:C, 0:C])
                last.then_inc(sem("a_turned"), 1)

            self_attention("a", XF["a"], C, hand_on_a, {3: 2})

            for b in range(B):
                if b == 0:
                    keep_warm(8, bank[7])
                if b < 2:
                    pe.wait_ge(sem("x3"), b + 3)
                features("b", b, b)
            pe.wait_ge(sem("mean2"), 1)
            pe.wait_ge(sem("wa_landed"), 16)
            pe.matmul(bank[4][0:B, 0:E2], mean2[:, :], WAs[:, WA["wr"]], start=True, stop=True).then_inc(sem("r_logits"), 1)
            pe.wait_ge(sem("r_rw"), 1)
            pe.matmul(bank[5][0:B, 0:E2], loads1[:, :], lg[:, 1, :], start=True, stop=True).then_inc(sem("r_loads"), 1)
            keep_warm(10, bank[7])
            pe.wait_ge(sem("r_spread"), 2)
            pe.matmul(bank[6][:, 0:2 * B * TOPK], ones4[:, :], spread[:, :, :, :].rearrange("p a b k -> p (a b k)"),
                      start=True, stop=True).then_inc(sem("r_bcast"), 1)
            keep_warm(8, bank[7])
            for i in range(B + 2):
                if i < B:
                    b = i
                    pe.wait_ge(sem("sel_a"), 2 * b + 1)
                    pe.wait_ge(sem("sel_v"), 2 * b + 1)
                    pe.wait_ge(sem("b_xf"), B)
                    for k in range(TOPK):
                        last = pe.matmul(bank[b][:, k * N:k * N + N], W1sel[:, TOPK * b + k, :],
                                         XF["b"][:, b * N:b * N + N], start=True, stop=True)
                    last.then_inc(sem("up2"), 1)
                if 0 <= i - 1 < B:
                    b = i - 1
                    pe.wait_ge(sem("gelu"), b + 1)
                    pe.wait_ge(sem("sel_a"), 2 * b + 2)
                    pe.wait_ge(sem("sel_v"), 2 * b + 2)
                    if b == 0:
                        pe.wait_ge(sem("r_spread_read"), 2)
                    if b >= 2:
                        pe.wait_ge(sem("ut"), b - 1)
                    for k in range(TOPK):
                        last = pe.matmul(bank[4 + b % 2][0:C, 0:N], W2sel[:, TOPK * b + k, :],
                                         H2[:, b, k * N:k * N + N], start=(k == 0), stop=(k == TOPK - 1))
                    last.then_inc(sem("down2"), 1)
                if 0 <= i - 2 < B:
                    b = i - 2
                    pe.wait_ge(sem("ut"), b + 1)
                    if b >= 2:
                        pe.wait_ge(sem("u"), b - 1)
                    for q in range(TB):
                        last = pe.transpose(bank[6 + b % 2][:, q * C:q * C + C], UT[:, b * N + q * P:b * N + q * P + P],
                                            ident[0:C, 0:C])
                    last.then_inc(sem("u_turned"), 1)

            def middle_c(b):
                pe.wait_ge(sem("c_xf"), b + 1)
                if b >= 2:
                    pe.wait_ge(sem("c_lhs"), b - 1)
                pe.matmul(bank[2 + b % 2][0:C1, 0:N], WAs[:, WA["y3"]], XF["c"][:, b * N:b * N + N],
                          start=True, stop=True).then_inc(sem("c_lhs_p"), 1)

            def hand_on_c(b):
                pe.wait_ge(sem("att_ct"), B + b + 1)
                if b == 0:
                    pe.wait_ge(sem("c_xf"), B)
                if b >= 2:
                    pe.wait_ge(sem("tanh"), 2 * (b - 1))
                for q in range(TB):
                    c = slice(b * N + q * P, b * N + q * P + P)
                    dst = bank[b % 2][:, q * 3 * C:(q + 1) * 3 * C]
                    pe.matmul(dst, XF["c"][:, c], WAs[:, WA["gx"]], start=True, stop=False)
                    last = pe.matmul(dst, CTc[:, c], WAs[:, WA["ga"]], start=False, stop=True)
                last.then_inc(sem("gates"), 1)

            keep_warm(36, bank[0])
            pe.wait_ge(sem("gelu"), B)
            self_attention("c", LHSc, C1, hand_on_c, {1: 1, 2: 3, 3: 3}, middle_c)

            for i in range(B + 2):
                if i < B:
                    if i < 2:
                        pe.wait_ge(sem("tanh"), 2 * (i + 3))
                    if i == 0:
                        keep_warm(12, bank[7])
                    features("d", i, i)
                if i >= 2:
                    pe.wait_ge(sem("d_xf"), i - 1)
                    for t in range(TB * (i - 2), TB * (i - 1)):
                        last = pe.matmul(bank[4][:, t * E3:t * E3 + E3], XF["d"][:, t * P:t * P + P],
                                         WAs[:, WA["gate"]], start=True, stop=True)
            last.then_inc(sem("logits3"), 1)
            pe.wait_ge(sem("ohb"), 1)
            pe.wait_ge(sem("later_const"), 8)
            flat = ohb[:, :, :].rearrange("p t e -> p (t e)")
            last = pe.matmul(bank[5][:, 0:T * E3], prefixb[:, :], flat, start=True, stop=False, skip_group_check=True)
            for back in range(1, T):
                last = pe.matmul(bank[5][:, back * E3:T * E3], onesb[:, :], flat[:, 0:(T - back) * E3],
                                 start=False, stop=(back == T - 1), skip_group_check=True)
            last.then_inc(sem("counts"), 1)
            keep_warm(6, bank[7])
            chunks = [(0, 512), (512, 512), (1024, 256)]
            for t in range(T):
                pe.wait_ge(sem("g3"), t + 1)
                if t == 0:
                    pe.wait_ge(sem("xl"), 1)
                for c, (at, width) in enumerate(chunks):
                    last = pe.matmul(bank[c][:, 0:width], XHL[:, t, :, :].rearrange("p k c -> p (k c)"),
                                     G3[:, t % 3, at:at + width], start=(t == 0), stop=(t == T - 1))
                last.then_inc(sem("gathered"), 1)
                if t == 4:
                    pe.wait_ge(sem("sd"), 1)
                    for h in range(2):
                        last = pe.matmul(bank[6 + h][:, :], onesf[:, :],
                                         SD[:, 4 * h:4 * h + 4, :].rearrange("p t q -> p (t q)"), start=True, stop=True)
                    last.then_inc(sem("sb_p"), 1)

            def turn_y(half):
                if half == 0:
                    pe.wait_ge(sem("sb"), 2)
                pe.wait_ge(sem("yt"), E3 // 2 * (half + 1))
                for j in range(HALF):
                    last = pe.transpose(TURN_Y[half][:, j * C:j * C + C],
                                        YT[:, (half * HALF + j) * P:(half * HALF + j + 1) * P], ident[0:C, 0:C])
                last.then_inc(sem("y_turned"), 1)

            def scatter(j):
                pe.wait_ge(sem("yl"), j // HALF + 1)
                pe.wait_ge(sem("gt"), j + 1)
                if j == 0:
                    pe.wait_ge(sem("sb"), 2)
                for c in range(2):
                    last = pe.matmul(bank[6 + c][:, :], YHL[:, j, :, :].rearrange("p k c -> p (k c)"),
                                     GT[:, j % 4, c * 512:c * 512 + 512], start=(j == 0), stop=(j == 2 * HALF - 1))
                last.then_inc(sem("scattered"), 1)

            for e in range(E3 + 1):
                if e < E3:
                    pe.wait_ge(sem("xb"), 1 if e < 6 else 2)
                    if e == 0:
                        pe.wait_ge(sem("w3_landed"), 16)
                    if e == 1:
                        pe.wait_ge(sem("xb"), 2)
                    if e == 3:
                        pe.wait_ge(sem("xb_v"), 1)
                    if e >= 2:
                        pe.wait_ge(sem("h3"), e - 1)
                        pe.wait_ge(sem("h3_v"), e - 1)
                    for k in range(2):
                        last = pe.matmul(UP3[k][e % 2][:, 0:CAP3], W3s[:, e, k * P:k * P + P],
                                         XB[:, e * CAP3:e * CAP3 + CAP3], start=True, stop=True)
                    last.then_inc(sem("up3"), 1)
                if e == 6:
                    turn_y(0)
                if e >= 7:
                    for j in range(2 * (e - 7), 2 * (e - 7) + 2):
                        scatter(j)
                if e >= 1:
                    f = e - 1
                    pe.wait_ge(sem("h3"), f + 1)
                    pe.wait_ge(sem("h3_v"), f + 1)
                    if f == 0:
                        pe.wait_ge(sem("w2b_landed"), 16)
                    if f == 1:
                        pe.wait_ge(sem("xb_v"), 1)
                    if f >= 2:
                        pe.wait_ge(sem("yt"), f - 1)
                    dst = bank[f % 2]
                    for k in range(2):
                        last = pe.matmul(dst[0:C, 0:CAP3], W2B[:, f, k, :], H3[:, f % 3, k, :],
                                         start=(k == 0), stop=(k == 1))
                    last.then_inc(sem("down3"), 1)
            scatter(4)
            turn_y(1)
            for j in range(HALF, 2 * HALF):
                scatter(j)
            pe.wait_ge(sem("xl"), 2)
            for h in range(2):
                pe.wait_ge(sem("zt"), 1)
                pe.wait_ge(sem("zt_v"), 1)
                for q in range(T // 2):
                    t = h * T // 2 + q
                    last = pe.matmul(bank[h][:, q * C:q * C + C], ZT[:, t * P:t * P + P], twice[:, :],
                                     start=True, stop=True)
                last.then_inc(sem("z_turned"), 1)

        @block.scalar
        def _(act):
            act.dma_start(W8[:, :], w8).then_inc(sem("w8_landed"), 16)
            act.dma_start(W0s[:, :], w0).then_inc(sem("w0_landed"), 16)
            act.wait_ge(sem("a0"), 1)
            act.activation(A0[:, :], bank[6][0:C1, 0:C1], ACT.Copy, scale=float(D0) ** -0.5) \
                .then_inc(sem("a0_s"), 1)
            for b in range(B):
                act.wait_ge(sem("g0_p"), b + 1)
                act.activation(G0[:, b * N:b * N + N], bank[b][0:C1, 0:N], ACT.Copy).then_inc(sem("g0"), 1)
            for i in range(B + 1):
                if i < B:
                    act.wait_ge(sem("nm0"), i + 1)
                    for q in range(TB):
                        t = TB * i + q
                        act.activation(S_P[:, i, q, :], bank[4 + i % 2][:, q * N:q * N + N], ACT.Exp,
                                       bias=nmax[:, t:t + 1], accum_out=den[:, t:t + 1]).then_inc(sem("exp0"), 1)
                if i >= 1:
                    b = i - 1
                    act.wait_ge(sem("ct0_p"), b + 1)
                    act.activation(CT[:, b * N:b * N + N], bank[2 + b % 2][0:C1, 0:N], ACT.Copy) \
                        .then_inc(sem("ct0"), 1)
            act.wait_ge(sem("gn_step"), 3)
            act.wait_ge(sem("gn_rstd"), 1)
            for b in (1, 3):
                act.activation(XN1[0:C, b * N:b * N + N], bank[4 + b][0:C, 0:N], ACT.Identity,
                               bias=gn_nb[:, b:b + 1], scale=gn_r[:, b:b + 1]).then_inc(sem("xn1_a"), 1)
            for b in range(B):
                act.wait_ge(sem("qk_p"), b + 1)
                act.activation(QK[:, b * N:b * N + N], bank[b][:, 0:N], ACT.Copy,
                               scale=Cs[:, CST["scale"]]).then_inc(sem("qkf"), 1)
            act.wait_ge(sem("v1_p"), 1)
            act.activation(V1[:, :, :, 0:HD],
                           bank[4][:, :].rearrange("p (t h d) -> p t h d", t=T, h=NH), ACT.Copy).then_inc(sem("v1"), 1)
            for n in range(B * NH + 3):
                b, h = divmod(n, NH)
                if b < B:
                    if n >= 3:
                        act.wait_ge(sem("av1"), n - 2)
                    if h in PE_HEADS:
                        act.wait_ge(sem("s1"), n + 1)
                        act.activation(P1[:, n % 3, :], bank[2 + n % 2][:, 0:TB * SPAN], ACT.Exp).then_inc(sem("p1"), 1)
                    else:
                        act.wait_ge(sem("u1"), by_dve(n) + 1)
                        act.activation(P1[:, n % 3, :], U1[:, n % 3, :], ACT.Exp).then_inc(sem("p1"), 1)
                m = n - 3
                if m >= 0 and m % NH == NH - 1:
                    b = m // NH
                    act.wait_ge(sem("av1"), (b + 1) * NH)
                    if b >= 2:
                        act.wait_ge(sem("turn1"), b - 1)
                    act.activation(CT1[:, b % 2, :], bank[4 + b % 2][:, :], ACT.Copy).then_inc(sem("ct1"), 1)


            def attention_act(s, nm, dn, ct, width):
                for i in range(B + 6):
                    if i < B:
                        act.wait_ge(sem(s + "_xf_p"), i + 1)
                        act.activation(XF[s][0:C, i * N:i * N + N], bank[i % 2][0:C, 0:N], ACT.Copy) \
                            .then_inc(sem(s + "_xf"), 1)
                    if s == "c" and 0 <= i - 1 < B:
                        b = i - 1
                        act.wait_ge(sem("c_lhs_p"), b + 1)
                        act.activation(LHSc[:, b * N:b * N + N], bank[2 + b % 2][0:C1, 0:N], ACT.Copy) \
                            .then_inc(sem("c_lhs"), 1)
                    if 0 <= i - 2 < B:
                        b = i - 2
                        act.wait_ge(sem("att_nm"), through(s) + b + 1)
                        for q in range(TB):
                            t = TB * b + q
                            act.activation(S_P[:, b, q, :], bank[4 + b % 2][:, q * N:q * N + N], ACT.Exp,
                                           bias=nm[:, t:t + 1], scale=float(C) ** -0.5 if s == "a" else 1.0,
                                           accum_out=dn[:, t:t + 1]).then_inc(sem("att_exp"), 1)
                    if 0 <= i - 4 < B:
                        b = i - 4
                        act.wait_ge(sem("att_ct_p"), through(s) + b + 1)
                        act.activation(ct[:, b * N:b * N + N], bank[2 + b % 2][0:width, 0:N], ACT.Copy) \
                            .then_inc(sem("att_ct"), 1)
                    if s == "c" and 0 <= i - 5 < B:
                        b = i - 5
                        act.wait_ge(sem("gates"), b + 1)
                        g = bank[b % 2][:, 0:TB * 3 * C].rearrange("p (q f) -> p q f", q=TB)
                        t = slice(TB * b, TB * b + TB)
                        act.activation(th[:, t, 0:C], g[:, :, 0:C], ACT.Tanh).then_inc(sem("tanh"), 1)
                        act.activation(th[:, t, C:3 * C], g[:, :, C:3 * C], ACT.Tanh, scale=0.5).then_inc(sem("tanh"), 1)

            attention_act("a", nmaxa, dena, CTa, C)
            for b in range(B):
                act.wait_ge(sem("b_xf_p"), b + 1)
                act.activation(XF["b"][0:C, b * N:b * N + N], bank[b][0:C, 0:N], ACT.Copy, accum_out=msum[:, b:b + 1]) \
                    .then_inc(sem("b_xf"), 1)
            act.wait_ge(sem("r_nm"), 1)
            act.activation(lg[:, 0, :], bank[4][0:B, 0:E2], ACT.Exp, bias=col[:, 0:1], accum_out=col[:, 1:2]) \
                .then_inc(sem("r_exp"), 1)
            act.wait_ge(sem("r_nm"), 2)
            act.activation(lg[:, 4, :], lg[:, 3, :], ACT.Exp, bias=col[:, 3:4], accum_out=col[:, 4:5]) \
                .then_inc(sem("r_exp"), 1)
            act.wait_ge(sem("r_nm"), 3)
            act.activation(lg[:, 7, 0:TOPK], lg[:, 6, 0:TOPK], ACT.Exp, bias=col[:, 6:7], accum_out=col[:, 7:8]) \
                .then_inc(sem("r_exp"), 1)
            act.wait_ge(sem("pool_const"), 4)
            act.activation(table[:, :], mhalf[0:1, 0:1], ACT.Gelu).then_inc(sem("table"), 1)
            act.wait_ge(sem("slot_e"), 1)
            act.wait_ge(sem("r_spread_read"), 2)
            act.wait_ge(sem("w2a_landed"), 16)
            w2flat = W2A[:, :, :].rearrange("p e c -> p (e c)")
            for i in range(0, B * TOPK, TOPK):
                e = act.value_load(slot_e[0:1, i:i + 1], min_val=0, max_val=E2 - 1)
                act.activation(W1sel[:, i, :], WAs[:, bass.ds(e * F2, F2)], ACT.Copy).then_inc(sem("sel_a"), 1)
                act.activation(W2sel[:, i, :], w2flat[:, bass.ds(e * C, C)], ACT.Copy, scale=tw[:, i:i + 1]) \
                    .then_inc(sem("sel_a"), 1)
            for b in range(B):
                act.wait_ge(sem("up2"), b + 1)
                act.activation(H2[:, b, :], bank[b][:, :], ACT.Gelu).then_inc(sem("gelu"), 1)
            act.wait_ge(sem("table"), 1)
            act.activation(table[:, :], mhalf[0:1, 0:1], ACT.Exp)
            attention_act("c", nmaxc, denc, CTc, C1)
            for b in range(B):
                act.wait_ge(sem("d_xf_p"), b + 1)
                act.activation(XF["d"][0:C, b * N:b * N + N], bank[b][0:C, 0:N], ACT.Copy).then_inc(sem("d_xf"), 1)
            for b in range(B):
                act.wait_ge(sem("d_xn"), b + 1)
                act.activation(XHL[:, TB * b:TB * b + TB, 0, :], XN["d"][:, TB * b:TB * b + TB, 0:C], ACT.Copy) \
                    .then_inc(sem("xh"), 1)
            act.wait_ge(sem("d3"), 1)
            act.activation(ex3[:, :, :], d3[:, :, :], ACT.Exp).then_inc(sem("ex3"), 1)
            act.wait_ge(sem("sb_p"), 1)
            for h in range(2):
                act.activation(SB[:, h * 512:h * 512 + 512], bank[6 + h][:, :], ACT.Copy).then_inc(sem("sb"), 1)
            act.wait_ge(sem("gathered"), T)
            for c, at, width in ((0, 0, 512), (2, 1024, 256)):
                act.activation(XB[:, at:at + width], bank[c][:, 0:width], ACT.Copy).then_inc(sem("xb"), 1)

            def y_high(half):
                act.wait_ge(sem("y_turned"), half + 1)
                act.activation(YHL[:, half * HALF:(half + 1) * HALF, 0, :],
                               TURN_Y[half][:, 0:HALF * C].rearrange("p (j c) -> p j c", j=HALF), ACT.Copy) \
                    .then_inc(sem("yh"), 1)

            for e in range(E3 + 1):
                if e < E3:
                    act.wait_ge(sem("up3"), e + 1)
                    if e >= 3:
                        act.wait_ge(sem("down3"), e - 2)
                    act.activation(H3[:, e % 3, 0, :], UP3[0][e % 2][:, 0:CAP3], ACT.Relu,
                                   bias=Cs[:, CST["fb1"]][:, 2 * e:2 * e + 1]).then_inc(sem("h3"), 1)
                if e == 6:
                    y_high(0)
                if e >= 1:
                    f = e - 1
                    act.wait_ge(sem("down3"), f + 1)
                    act.activation(YT[:, f * CAP3:f * CAP3 + CAP3], bank[f % 2][0:C, 0:CAP3], ACT.Identity,
                                   bias=WAs[0:C, WA["fb2"]][:, f:f + 1]).then_inc(sem("yt"), 1)
            y_high(1)
            act.wait_ge(sem("scattered"), SLOTS // P)
            act.activation(ZT[:, 0:512], bank[6][:, :], ACT.Copy).then_inc(sem("zt"), 1)
            for h in range(2):
                t = slice(h * T // 2, (h + 1) * T // 2)
                act.wait_ge(sem("y3"), h + 1)
                act.activation(wild3[:, t, :], y3[:, t, :], ACT.Abs, scale=0.0).then_inc(sem("wild3"), 1)

        @block.vector
        def _(dve):
            steps = [0]

            def counted(ins):
                steps[0] += 1
                ins.then_inc(sem("vector_step"), 1)
                return steps[0]

            def then(ins):
                dve.wait_ge(sem("vector_step"), counted(ins))

            dve.memset(onesb[:, :], 1.0).then_inc(sem("onesb"), 1)
            for b in range(B):
                dve.wait_ge(sem("xt_p"), b + 1)
                dve.tensor_copy(XT[0:C, b * N:b * N + N], bank[b][0:C, 0:N]).then_inc(sem("xt"), 1)
            dve.wait_ge(sem("wvo"), 1)
            dve.tensor_copy(Wvo[:, :], bank[7][0:C1, 0:C]).then_inc(sem("wvo_s"), 1)
            for i in range(B + 3):
                if i < B:
                    dve.wait_ge(sem("s0"), i + 1)
                    dve.tensor_reduce(nmax[:, TB * i:TB * i + TB],
                                      bank[4 + i % 2][:, :].rearrange("p (q k) -> p q k", q=TB),
                                      AX.X, ALU.max, negate=True).then_inc(sem("nm0"), 1)
                if 0 <= i - 1 < B:
                    b = i - 1
                    dve.wait_ge(sem("pt0_p"), b + 1)
                    dve.tensor_copy(S_PT[:, b, :, :].rearrange("p k q -> p (k q)"), bank[6 + b % 2][:, :]) \
                        .then_inc(sem("pt0"), 1)
                    dve.wait_ge(sem("exp0"), 2 * b + 2)
                    dve.reciprocal(rden[:, TB * b:TB * b + TB], den[:, TB * b:TB * b + TB]).then_inc(sem("rd0"), 1)
                if 0 <= i - 3 < B:
                    b = i - 3
                    dve.wait_ge(sem("o0"), b + 1)
                    dve.wait_ge(sem("rd0"), b + 1)
                    for q in range(TB):
                        t = TB * b + q
                        last = dve.scalar_tensor_tensor(
                            out=X1[:, t, :], in0=bank[b % 2][:, q * C:q * C + C], scalar=rden[:, t:t + 1],
                            in1=X[:, t, 0:C], op0=ALU.mult, op1=ALU.add)
                    last.then_inc(sem("x1"), 1)
            stats = []
            for b in range(B):
                dve.wait_ge(sem("x1t_p"), b + 1)
                stats.append(counted(dve.bn_stats(gn_st[:, b, :], bank[4 + b][0:C, 0:N])))
            for b in range(B):
                dve.wait_ge(sem("vector_step"), stats[b])
                last = counted(dve.bn_aggr(gn_mv[:, b, 0:2], gn_st[:, b, :]))
            dve.wait_ge(sem("vector_step"), last)
            dve.tensor_tensor(gn_mv[:, :, 2], gn_mv[:, :, 0], gn_mv[:, :, 0], ALU.mult).then_inc(sem("gn_step"), 1)
            dve.wait_ge(sem("gn_pair"), 1)
            then(dve.tensor_copy(gn_g[:, :, :].rearrange("c b k -> c (b k)"), bank[0][0:C, 0:3 * B]))
            then(dve.tensor_tensor(gn_sq[:, :], gn_g[:, :, 0], gn_g[:, :, 0], ALU.mult))
            then(dve.scalar_tensor_tensor(out=gn_v[:, :], in0=gn_g[:, :, 1], scalar=LN_EPS, in1=gn_g[:, :, 2],
                                          op0=ALU.add, op1=ALU.add))
            dve.tensor_tensor(gn_v[:, :], gn_v[:, :], gn_sq[:, :], ALU.subtract).then_inc(sem("gn_step"), 1)
            dve.wait_ge(sem("gn_rstd"), 1)
            dve.scalar_tensor_tensor(out=gn_nb[:, :], in0=gn_g[:, :, 0], scalar=-1.0, in1=gn_r[:, :],
                                     op0=ALU.mult, op1=ALU.mult).then_inc(sem("gn_step"), 1)
            dve.wait_ge(sem("gn_step"), 3)
            for b in (0, 2):
                dve.tensor_scalar(XN1[0:C, b * N:b * N + N], bank[4 + b][0:C, 0:N], gn_r[:, b:b + 1],
                                  gn_nb[:, b:b + 1], ALU.mult, ALU.add).then_inc(sem("xn1"), 1)
            for b in range(B):
                c = slice(b * N, b * N + N)
                dve.wait_ge(sem("qkf"), b + 1)
                dve.tensor_copy(part[:, 0, c], QK[:, c]).then_inc(sem("qk_part"), 1)
                dve.wait_ge(sem("qk_part"), 3 * b + 1)
                then(dve.tensor_tensor(qkr[:, c], QK[:, c], part[:, 0, c], ALU.subtract))
                dve.tensor_copy(part[:, 1, c], qkr[:, c]).then_inc(sem("qk_part"), 1)
                dve.wait_ge(sem("qk_part"), 3 * b + 2)
                dve.tensor_tensor(part[:, 2, c], qkr[:, c], part[:, 1, c], ALU.subtract).then_inc(sem("qk_part"), 1)

            def maxima(n):
                dve.wait_ge(sem("mx1"), n + 1)
                dve.tensor_reduce(nm1[:, n // NH, n % NH, :],
                                  bank[n % 2][:, 0:TB * SPAN].rearrange("p (q k) -> p q k", q=TB),
                                  AX.X, ALU.max, negate=True).then_inc(sem("nm1"), 1)

            def biased(n):
                dve.wait_ge(sem("s1"), n + 1)
                if n == 0:
                    dve.wait_ge(sem("biasK_landed"), 16)
                if n >= 3:
                    dve.wait_ge(sem("p1"), n - 2)
                dve.tensor_tensor(U1[:, n % 3, :], bank[2 + n % 2][:, 0:TB * SPAN], biasK[:, n % NH, :], ALU.add) \
                    .then_inc(sem("u1"), 1)

            def finish1_reciprocal(b):
                dve.wait_ge(sem("turn1"), b + 1)
                v = bank[6][:, :].rearrange("p (j g w) -> p j g w", j=2 * TB, g=4)
                counted(dve.reciprocal(rz1[:, b % 2, :, :], v[:, :, :, HD]))

            def finish1_divide(b):
                v = bank[6][:, :].rearrange("p (j g w) -> p j g w", j=2 * TB, g=4)
                dve.wait_ge(sem("vector_step"), steps[0])
                dve.tensor_tensor(ctx1[:, b % 2, :, :, :], v[:, :, :, 0:HD],
                                  rz1[:, b % 2, :, :].unsqueeze(3).to_broadcast([P, 2 * TB, 4, HD]), ALU.mult) \
                    .then_inc(sem("ctx1"), 1)

            def finish1_add(b):
                dve.wait_ge(sem("ctx1"), b + 1)
                dve.tensor_tensor(X2[:, TB * b:TB * b + TB, :].rearrange("p q c -> p (q c)"),
                                  ctx1[:, b % 2, :, :, :].rearrange("p j g d -> p (j g d)"),
                                  X1[:, TB * b:TB * b + TB, :].rearrange("p q c -> p (q c)"), ALU.add) \
                    .then_inc(sem("x2_done"), 1)

            def blocks_of(s, k):
                n = LN_STEPS.index((s, k * T // 2, T // 2) if s != "a" else (s, TB * k, TB))
                first, blocks = LN_STEPS[n][1:]
                return range(first, first + blocks), n + 1

            def moments(s, src, ready, count, k):
                dve.wait_ge(sem(ready), count)
                for t in blocks_of(s, k)[0]:
                    last = dve.bn_stats(ln_st[s][:, t, :], src[:, t, :])
                counted(last)

            def aggregate(s, k):
                dve.wait_ge(sem("vector_step"), steps[0])
                for t in blocks_of(s, k)[0]:
                    last = dve.bn_aggr(ln_mv[s][:, t, :], ln_st[s][:, t, :])
                last.then_inc(sem("ln_mv"), 1)

            def stats(s, src, ready, count, k):
                moments(s, src, ready, count, k)
                aggregate(s, k)

            def apply(s, src, k):
                blocks, n = blocks_of(s, k)
                dve.wait_ge(sem("ln_mv"), n)
                dve.wait_ge(sem("ln_rs"), n)
                for t in blocks:
                    last = dve.tensor_scalar(XN[s][:, t, 0:C], src[:, t, :], ln_mv[s][:, t, 0:1], ln_rs[s][:, t:t + 1],
                                             ALU.subtract, ALU.mult)
                    if t % TB == TB - 1:
                        last.then_inc(sem(s + "_xn"), 1)

            for n in range(NH):
                maxima(n)
            for n in range(B * NH + 4):
                if n + NH < B * NH:
                    maxima(n + NH)
                if n < B * NH and n % NH not in PE_HEADS:
                    biased(n)
                b, step = (n - 4) // NH - 1, (n - 4) % NH
                if b >= 0:
                    if step == 2:
                        finish1_reciprocal(b)
                    if step == 3:
                        finish1_divide(b)
                    if step == 4:
                        finish1_add(b)
                    if step == 5:
                        moments("a", X2, "x2_done", b + 1, b)
                    if step == 6:
                        aggregate("a", b)
                    if step == 7:
                        apply("a", X2, b)
            finish1_reciprocal(B - 1)
            finish1_divide(B - 1)
            finish1_add(B - 1)
            stats("a", X2, "x2_done", B, B - 1)

            def maxima_of(s, b, nm):
                dve.wait_ge(sem("att_s"), through(s) + b + 1)
                t = slice(TB * b, TB * b + TB)
                rows = bank[4 + b % 2][:, :].rearrange("p (q k) -> p q k", q=TB)
                if s == "a":
                    then(dve.tensor_reduce(nm[:, t], rows, AX.X, ALU.max, negate=True))
                    dve.tensor_scalar(nm[:, t], nm[:, t], float(C) ** -0.5, None, ALU.mult).then_inc(sem("att_nm"), 1)
                else:
                    dve.tensor_reduce(nm[:, t], rows, AX.X, ALU.max, negate=True).then_inc(sem("att_nm"), 1)

            def x3_of(b):
                dve.wait_ge(sem("a_turned"), b + 1)
                for q in range(TB):
                    t = TB * b + q
                    last = dve.scalar_tensor_tensor(
                        out=X3[:, t, :], in0=bank[b % 2][:, q * C:q * C + C], scalar=rdena[:, t:t + 1],
                        in1=X2[:, t, :], op0=ALU.mult, op1=ALU.add)
                last.then_inc(sem("x3"), 1)

            def turned_p(s, b):
                dve.wait_ge(sem("att_pt_p"), through(s) + b + 1)
                dve.tensor_copy(S_PT[:, b, :, :].rearrange("p k q -> p (k q)"), bank[6 + b % 2][:, :]) \
                    .then_inc(sem("att_pt"), 1)

            for i in range(2, B + 4):
                if 0 <= i - 2 < B:
                    b = i - 2
                    maxima_of("a", b, nmaxa)
                    if b == 0:
                        apply("a", X2, B - 1)
                if 0 <= i - 3 < B:
                    b = i - 3
                    turned_p("a", b)
                    dve.wait_ge(sem("att_exp"), 2 * b + 2)
                    then(dve.reciprocal(rdena[:, TB * b:TB * b + TB], dena[:, TB * b:TB * b + TB]))
                if 0 <= i - 5 < B:
                    x3_of(i - 5)
            stats("b", X3, "x3", B // 2, 0)
            x3_of(B - 1)
            stats("b", X3, "x3", B, 1)
            for half in range(2):
                apply("b", X3, half)

            dve.wait_ge(sem("b_xf"), B)
            dve.tensor_scalar(mean2[0:C, :], msum[:, :], 1.0 / N, None, ALU.mult).then_inc(sem("mean2"), 1)
            dve.wait_ge(sem("r_logits"), 1)
            dve.tensor_reduce(col[:, 0:1], bank[4][0:B, 0:E2], AX.X, ALU.max, negate=True).then_inc(sem("r_nm"), 1)
            dve.wait_ge(sem("r_exp"), 1)
            then(dve.reciprocal(col[:, 2:3], col[:, 1:2]))
            dve.tensor_scalar(lg[:, 1, :], lg[:, 0, :], col[:, 2:3], None, ALU.mult).then_inc(sem("r_rw"), 1)
            dve.wait_ge(sem("r_loads"), 1)
            then(dve.reciprocal(lg[:, 2, :], bank[5][0:B, 0:E2]))
            then(dve.tensor_scalar(lg[:, 2, :], lg[:, 2, :], CAP2, 1.0, ALU.mult, ALU.min))
            dve.wait_ge(sem("r_rw"), 1)
            then(dve.tensor_tensor(lg[:, 3, :], lg[:, 2, :], lg[:, 1, :], ALU.mult))
            dve.tensor_reduce(col[:, 3:4], lg[:, 3, :], AX.X, ALU.max, negate=True).then_inc(sem("r_nm"), 1)
            dve.wait_ge(sem("r_exp"), 2)
            then(dve.reciprocal(col[:, 5:6], col[:, 4:5]))
            then(dve.tensor_scalar(lg[:, 5, :], lg[:, 4, :], col[:, 5:6], None, ALU.mult))
            then(dve.max(lg[:, 6, :], lg[:, 5, :]))
            dve.tensor_scalar(col[:, 6:7], lg[:, 6, 0:1], -1.0, None, ALU.mult).then_inc(sem("r_nm"), 1)
            then(dve.max_index(top_i[:, :], lg[:, 6, :], lg[:, 5, :]))
            id4 = ident[0:B, 0:B].unsqueeze(2).to_broadcast([B, B, TOPK])
            dve.tensor_tensor(spread[:, 1, :, :], top_i[:, 0:TOPK].unsqueeze(1).to_broadcast([B, B, TOPK]), id4,
                              ALU.mult).then_inc(sem("r_spread"), 1)
            dve.wait_ge(sem("r_exp"), 3)
            then(dve.reciprocal(col[:, 8:9], col[:, 7:8]))
            then(dve.tensor_scalar(lg[:, 7, 4:4 + TOPK], lg[:, 7, 0:TOPK], col[:, 8:9], None, ALU.mult))
            dve.tensor_tensor(spread[:, 0, :, :], lg[:, 7, 4:4 + TOPK].unsqueeze(1).to_broadcast([B, B, TOPK]), id4,
                              ALU.mult).then_inc(sem("r_spread"), 1)
            dve.wait_ge(sem("r_bcast"), 1)
            dve.tensor_copy(slot_e[:, :], bank[6][0:1, B * TOPK:2 * B * TOPK]).then_inc(sem("slot_e"), 1)
            dve.tensor_copy(tw[:, :], bank[6][:, 0:B * TOPK]).then_inc(sem("r_spread_read"), 1)
            dve.tensor_copy(chosen[:, :], bank[6][:, B * TOPK:2 * B * TOPK]).then_inc(sem("r_spread_read"), 1)
            dve.wait_ge(sem("slot_e"), 1)
            dve.wait_ge(sem("r_spread_read"), 2)
            dve.wait_ge(sem("w2a_landed"), 16)
            w2flat = W2A[:, :, :].rearrange("p e c -> p (e c)")
            for i in range(1, B * TOPK, TOPK):
                e = dve.value_load(slot_e[0:1, i:i + 1], min_val=0, max_val=E2 - 1)
                dve.tensor_copy(W1sel[:, i, :], WAs[:, bass.ds(e * F2, F2)]).then_inc(sem("sel_v"), 1)
                dve.tensor_scalar(W2sel[:, i, :], w2flat[:, bass.ds(e * C, C)], tw[:, i:i + 1], None, ALU.mult) \
                    .then_inc(sem("sel_v"), 1)
            cube = [C, B * TOPK, E2]
            e_no = Cs[0:C, CST["expert"]].rearrange("p (i e) -> p i e", i=B * TOPK)
            then(dve.tensor_tensor(b2w[:, :, :], e_no, chosen[0:C, :].unsqueeze(2).to_broadcast(cube), ALU.is_equal))
            then(dve.tensor_tensor(b2w[:, :, :], b2w[:, :, :], tw[0:C, :].unsqueeze(2).to_broadcast(cube), ALU.mult))
            then(dve.tensor_tensor(b2w[:, :, :], b2w[:, :, :], WAs[0:C, WA["b2"]].unsqueeze(1).to_broadcast(cube),
                                   ALU.mult))
            dve.tensor_reduce(b2sel[:, :], b2w[:, :, :].rearrange("p (b k) e -> p b (k e)", b=B), AX.X, ALU.add) \
                .then_inc(sem("b2sel"), 1)
            for i in range(B + 1):
                if i < B:
                    b = i
                    dve.wait_ge(sem("down2"), b + 1)
                    dve.wait_ge(sem("b2sel"), 1)
                    dve.tensor_scalar(UT[:, b * N:b * N + N], bank[4 + b % 2][0:C, 0:N], b2sel[:, b:b + 1], None, ALU.add) \
                        .then_inc(sem("ut"), 1)
                if i >= 1:
                    b = i - 1
                    dve.wait_ge(sem("u_turned"), b + 1)
                    dve.tensor_tensor(U[:, TB * b:TB * b + TB, :],
                                      bank[6 + b % 2][:, 0:TB * C].rearrange("p (q c) -> p q c", q=TB),
                                      XN["b"][:, TB * b:TB * b + TB, 0:C], ALU.add).then_inc(sem("u"), 1)
            def x4_of(half):
                t = slice(half * T // 2, (half + 1) * T // 2)
                wide = [P, T // 2, C]
                apply("u", U, half)
                dve.wait_ge(sem("u_xn"), B // 2 * (half + 1))
                then(dve.tensor_tensor(un[:, t, :], XN["u"][:, t, 0:C], gb[:, 0, :].unsqueeze(1).to_broadcast(wide), ALU.mult))
                dve.tensor_tensor(X4[:, t, :], un[:, t, :], X3b[:, t, :], ALU.add).then_inc(sem("x4"), 1)

            for half in range(2):
                stats("u", U, "u", B // 2 * (half + 1), half)
            dve.wait_ge(sem("gb_landed"), 16)
            dve.wait_ge(sem("x3b"), 1)
            for half in range(2):
                x4_of(half)
                stats("c", X4, "x4", half + 1, half)
            for half in range(2):
                apply("c", X4, half)

            def x5_of(b):
                t = slice(TB * b, TB * b + TB)
                dve.wait_ge(sem("tanh"), 2 * b + 2)
                dve.scalar_tensor_tensor(out=gm[:, t, 0:C], in0=th[:, t, C:2 * C], scalar=1.0,
                                         in1=XN["c"][:, t, 0:C], op0=ALU.add, op1=ALU.mult)
                then(dve.scalar_tensor_tensor(out=gm[:, t, C:2 * C], in0=th[:, t, 2 * C:3 * C], scalar=1.0,
                                              in1=th[:, t, 0:C], op0=ALU.add, op1=ALU.mult))
                then(dve.tensor_tensor(gs[:, t, :], gm[:, t, 0:C], gm[:, t, C:2 * C], ALU.add))
                dve.scalar_tensor_tensor(out=X5[:, t, :], in0=gs[:, t, :], scalar=0.5, in1=X4[:, t, :],
                                         op0=ALU.mult, op1=ALU.add).then_inc(sem("x5"), 1)

            for i in range(2, B + 5):
                if i - 2 < B:
                    maxima_of("c", i - 2, nmaxc)
                if 0 <= i - 3 < B:
                    turned_p("c", i - 3)
                if i >= 6:
                    x5_of(i - 6)
                if i - 2 < B:
                    b = i - 2
                    dve.wait_ge(sem("att_exp"), 2 * b + 2 + 2 * B)
                    then(dve.reciprocal(rdenc[:, TB * b:TB * b + TB], denc[:, TB * b:TB * b + TB]))
                    for q in range(TB):
                        t = TB * b + q
                        dve.tensor_scalar(S_P[:, b, q, :], S_P[:, b, q, :], rdenc[:, t:t + 1], None, ALU.mult) \
                            .then_inc(sem("c_pn"), 1)
            stats("d", X5, "x5", B // 2, 0)
            x5_of(B - 1)
            stats("d", X5, "x5", B, 1)
            for half in range(2):
                apply("d", X5, half)

            dve.wait_ge(sem("d_xn"), B)
            dve.wait_ge(sem("xh"), B)
            dve.tensor_tensor(XHL[:, :, 1, :], XN["d"][:, :, 0:C], XHL[:, :, 0, :].bitcast(F32), ALU.subtract) \
                .then_inc(sem("xl"), 1)
            dve.tensor_copy(twice[:, :], Cs[:, CST["twice"]]).then_inc(sem("xl"), 1)

            def per_expert(v):
                return v.unsqueeze(2).to_broadcast([P, T, E3])

            rows = bank[4][:, 0:T * E3].rearrange("p (t e) -> p t e", t=T)
            cnt = bank[5][:, 0:T * E3].rearrange("p (t e) -> p t e", t=T)
            dve.wait_ge(sem("logits3"), 1)
            then(dve.tensor_reduce(mx3[:, :], rows, AX.X, ALU.max))
            dve.tensor_tensor(d3[:, :, :], rows, per_expert(mx3[:, :]), ALU.subtract).then_inc(sem("d3"), 1)
            dve.wait_ge(sem("d3"), 1)
            then(dve.tensor_scalar(oh3[:, :, :], d3[:, :, :], 0.0, None, ALU.is_equal))
            rev = Cs[:, CST["rev"]].rearrange("p (t e) -> p t e", t=T)
            first = Cs[:, CST["first"]].rearrange("p (t e) -> p t e", t=T)
            then(dve.tensor_tensor(rv3[:, :, :], oh3[:, :, :], rev, ALU.mult))
            then(dve.tensor_reduce(mr3[:, :], rv3[:, :, :], AX.X, ALU.max))
            dve.tensor_tensor(ohb[:, :, :], rv3[:, :, :], per_expert(mr3[:, :]), ALU.is_equal).then_inc(sem("ohb"), 1)
            dve.wait_ge(sem("ohb"), 1)
            then(dve.tensor_tensor(sel3[:, 1, :, :], ohb[:, :, :], first, ALU.mult))
            dve.wait_ge(sem("ex3"), 1)
            then(dve.tensor_reduce(se3[:, :], ex3[:, :, :], AX.X, ALU.add))
            then(dve.reciprocal(prb[:, :], se3[:, :]))
            dve.wait_ge(sem("counts"), 1)
            then(dve.tensor_tensor(sel3[:, 0, :, :], ohb[:, :, :], cnt, ALU.mult))
            then(dve.tensor_reduce(cf3[:, :, :], sel3[:, :, :, :], AX.X, ALU.add))
            then(dve.tensor_scalar(kept[:, :], cf3[:, 0, :], float(CAP3), None, ALU.is_le))
            then(dve.tensor_tensor(gate3[:, :], prb[:, :], kept[:, :], ALU.mult))
            then(dve.tensor_tensor(sid[:, :], cf3[:, 0, :], cf3[:, 1, :], ALU.add))
            then(dve.tensor_tensor(sid[:, :], sid[:, :], kept[:, :], ALU.mult))
            dve.tensor_scalar(sid[:, :], sid[:, :], -1.0, None, ALU.add).then_inc(sem("sid"), 1)
            dve.wait_ge(sem("sid"), 1)
            dve.wait_ge(sem("later_const"), 9)
            for t in range(T):
                if t >= 3:
                    dve.wait_ge(sem("gathered"), t - 2)
                dve.tensor_scalar(G3[:, t % 3, :], iota_f[:, :], sid[:, t:t + 1], None, ALU.is_equal).then_inc(sem("g3"), 1)
            dve.wait_ge(sem("gathered"), T)
            dve.tensor_copy(XB[:, 512:1024], bank[1][:, :]).then_inc(sem("xb_v"), 1)
            dve.wait_ge(sem("sb"), 2)
            slot_no = Cs[:, CST["slot"]]

            def one_hot_slots(j):
                if j >= 4:
                    dve.wait_ge(sem("scattered"), j - 3)
                dve.tensor_scalar(GT[:, j % 4, :], SB[:, :], slot_no[:, j:j + 1], None, ALU.is_equal).then_inc(sem("gt"), 1)

            def y_low(half):
                j = slice(half * HALF, (half + 1) * HALF)
                dve.wait_ge(sem("yh"), half + 1)
                dve.tensor_tensor(YHL[:, j, 1, :], TURN_Y[half][:, 0:HALF * C].rearrange("p (j c) -> p j c", j=HALF),
                                  YHL[:, j, 0, :].bitcast(F32), ALU.subtract).then_inc(sem("yl"), 1)

            for e in range(E3):
                dve.wait_ge(sem("up3"), e + 1)
                if e >= 3:
                    dve.wait_ge(sem("down3"), e - 2)
                dve.tensor_scalar(H3[:, e % 3, 1, :], UP3[1][e % 2][:, 0:CAP3],
                                  Cs[:, CST["fb1"]][:, 2 * e + 1:2 * e + 2], 0.0, ALU.add, ALU.max).then_inc(sem("h3_v"), 1)
                if e < 4:
                    one_hot_slots(e)
                if e == 6:
                    y_low(0)
            for j in range(4, 7):
                one_hot_slots(j)
            y_low(1)
            for j in range(7, 2 * HALF):
                one_hot_slots(j)
            dve.wait_ge(sem("scattered"), SLOTS // P)
            dve.tensor_copy(ZT[:, 512:1024], bank[7][:, :]).then_inc(sem("zt_v"), 1)
            halves = [slice(h * T // 2, (h + 1) * T // 2) for h in range(2)]
            for h, t in enumerate(halves):
                dve.wait_ge(sem("z_turned"), h + 1)
                dve.tensor_tensor(y3[:, t, :], bank[h][:, 0:T // 2 * C].rearrange("p (q c) -> p q c", q=T // 2),
                                  gate3[:, t].unsqueeze(2).to_broadcast([P, T // 2, C]), ALU.mult).then_inc(sem("y3"), 1)
            for h, t in enumerate(halves):
                dve.wait_ge(sem("y3"), h + 1)
                then(dve.tensor_tensor(nan3[:, t, :], y3[:, t, :], y3[:, t, :], ALU.is_equal))
                then(dve.scalar_tensor_tensor(out=sat3[:, t, :], in0=y3[:, t, :], scalar=1e4, in1=nan3[:, t, :],
                                              op0=ALU.min, op1=ALU.mult))
                then(dve.scalar_tensor_tensor(out=sat3[:, t, :], in0=sat3[:, t, :], scalar=-1e4, in1=X5[:, t, :],
                                              op0=ALU.max, op1=ALU.add))
                dve.wait_ge(sem("wild3"), h + 1)
                dve.wait_ge(sem("sum3"), h + 1)
                dve.copy_predicated(Y6[:, t, :], wild3[:, t, :].bitcast(I32), sat3[:, t, :]).then_inc(sem("y6"), TB)


def pack(pairs, where, rows, width):
    a = np.zeros((rows, width), np.float32)
    for name, value in pairs.items():
        a[:value.shape[0], where[name]] = value
    return a


def with_bias(w, b):
    return np.concatenate([w, b[None, :]], 0)


def feature_head(w):
    return w.reshape(*w.shape[:-1], NH, HD).swapaxes(-1, -2).reshape(w.shape)


def bias_tables(rpb):
    q = np.full((P, NH, TB, SPAN), MASKED, np.float32)
    k = np.full((P, NH, TB, SPAN), MASKED, np.float32)
    start = np.array([window_start(i) for i in range(HW)])
    n = np.arange(N)
    i, j = n // HW, n % HW
    ok = (i[None] >= start[i][:, None]) & (i[None] < start[i][:, None] + WIN) & \
         (j[None] >= start[j][:, None]) & (j[None] < start[j][:, None] + WIN)
    full = np.full((NH, N, N), MASKED, np.float32)
    qi, ki = np.nonzero(ok)
    full[:, qi, ki] = rpb[:, i[ki] - i[qi] + WIN - 1, j[ki] - j[qi] + WIN - 1]
    for s in range(TB):
        q[:, :, s, :] = full[:, s * P:s * P + P, OFF[s]:OFF[s] + SPAN].transpose(1, 0, 2)
        k[:, :, s, :] = full[:, OFF[s]:OFF[s] + SPAN, s * P:s * P + P].transpose(2, 0, 1)
    return q.reshape(P, NH, TB * SPAN), k.reshape(P, NH, TB * SPAN)


def kernel(**inputs):
    import concourse.bacc as bacc
    from concourse.bass_utils import run_bass_kernel_spmd

    a = {k: np.ascontiguousarray(np.asarray(v)) for k, v in inputs.items()}
    p = np.arange(P)
    pair = np.zeros((C, C), np.float32)
    for c in range(C):
        pair[c, c // 2 * 2:c // 2 * 2 + 2] = 0.5
    cst = pack({
        "ident": np.eye(P, dtype=np.float32),
        "prefix": (p[:, None] <= p[None]).astype(np.float32),
        "pair": pair,
        "rev": np.tile(np.arange(E3, 0, -1, dtype=np.float32), (P, T)),
        "scale": np.where(p < C, float(HD) ** -0.5, 1.0).astype(np.float32)[:, None],
        "first": np.tile(np.arange(E3, dtype=np.float32) * CAP3, (P, T)),
        "expert": np.tile(np.arange(E3, dtype=np.float32), (P, T)),
        "fb1": a["L3_ffn_b1"].reshape(E3, 2, P).transpose(2, 0, 1).reshape(P, E3 * 2),
        "twice": np.tile(np.eye(C, dtype=np.float32), (2, 1)),
        "slot": (p[:, None] + P * np.arange(10)[None]).astype(np.float32),
    }, CST, P, CST_W)
    w8 = np.concatenate([with_bias(a["L0_conv_wq"], a["L0_conv_bq"]).T,
                         with_bias(a["L0_conv_wk"], a["L0_conv_bk"]).T], 1)
    wvT = np.zeros((C1, C1), np.float32)
    wvT[:C] = with_bias(a["L0_conv_wv"], a["L0_conv_bv"]).T
    wvT[C, C] = 1.0
    w0 = pack({
        "wvT": wvT, "wo": with_bias(a["L0_conv_wo"], a["L0_conv_bo"]),
        "wqk1": with_bias(np.concatenate([feature_head(a["L1_conv_wq"].T), feature_head(a["L1_conv_wk"].T)], 1),
                          np.concatenate([feature_head(a["L1_conv_bq"]), feature_head(a["L1_conv_bk"])])),
        "wv1": with_bias(a["L1_conv_wv"].T, a["L1_conv_bv"]),
    }, W0, C1, W0_W)
    bias_q, bias_k = bias_tables(a["L1_conv_rpb"])
    att = a["L3_attn_att_w"]
    y3 = np.zeros((C1, C1), np.float32)
    y3[np.arange(C), np.arange(C)] = att[2 * C:]
    y3[C, :C] = att[C:2 * C]
    y3[:C, C] = att[:C]
    gw = np.concatenate([a["L3_attn_z_w"], a["L3_attn_r_w"], a["L3_attn_f_w"]], 0)
    gbias = np.concatenate([a["L3_attn_z_b"], a["L3_attn_r_b"], a["L3_attn_f_b"]])
    wa = pack({
        "w1": np.concatenate([a["L2_ffn_W1"].transpose(1, 0, 2).reshape(C, E2 * F2), a["L2_ffn_b1"].reshape(1, E2 * F2)]),
        "wr": with_bias(a["L2_ffn_Wr"], a["L2_ffn_br"]),
        "b2": a["L2_ffn_b2"].T,
        "y3": y3,
        "gx": with_bias(gw[:, :C].T, gbias),
        "ga": gw[:, C:].T,
        "gate": with_bias(a["L3_ffn_gate_w"], a["L3_ffn_gate_b"]),
        "fb2": a["L3_ffn_b2"].T,
    }, WA, C1, WA_W)
    arrays = {
        "x": a["x"].reshape(B, N, C), "w8": w8, "w0": w0, "wa": wa,
        "w3": np.tile(a["L3_ffn_w1"].transpose(1, 0, 2), (2, 1, 1)),
        "w2a": a["L2_ffn_W2"].transpose(1, 0, 2),
        "w2b": a["L3_ffn_w2"].reshape(E3, 2, P, C).transpose(2, 0, 1, 3),
        "cst": cst, "bias_q": bias_q, "bias_k": bias_k,
        "lnw": np.stack([a["L2_ffn_gamma"], a["L2_ffn_beta"]]),
    }
    arrays = {k: np.ascontiguousarray(v) for k, v in arrays.items()}
    nc = bacc.Bacc("TRN2", target_bir_lowering=False, num_devices=1)
    args = {n: nc.dram_tensor(n, v.shape, F32, kind="ExternalInput").ap() for n, v in arrays.items()}
    args["out"] = nc.dram_tensor("out", (B, N, C), F32, kind="ExternalOutput").ap()
    hybrid_kernel(nc, **args)
    r = run_bass_kernel_spmd(nc, [arrays], core_ids=[0])
    return r.results[0]["out"].reshape(B, HW, HW, C)
```

```python
from contextlib import ExitStack

import numpy as np
import concourse.bass as bass
from concourse import mybir

P = 128
B, HW, C = 4, 16, 64
N = HW * HW
TB = N // P
T = B * TB
C1 = C + 1
D0 = C // 8
NH, HD, WIN = 8, 8, 7
SPAN = (P // HW + WIN // 2) * HW
OFF = (0, N - SPAN)
NT = 9
KS = NT * HD
VW = 32
MASKED = -1e30
WARM = {"start": 8, "stacks": 8, "b_norm": 12, "logits": 2, "loads": 4, "routing": 10,
        "selection": 11, "c_norm": 34, "c_steps": {1: 1, 2: 3, 3: 3}, "a_steps": {3: 4},
        "d_norm": 18, "d_norm_2": 2, "first_expert": 5, "slots": 9, "results": 1,
        "results_low": 3}
AHEAD = 3
PE_HEADS = (1, 4, 7)
E2, F2, TOPK = 8, 128, 2
CAP2 = float(-(-B * N * 5 // (4 * E2)))
E3, F3 = 8, 256
CAP3 = -(-B * N * 5 // (4 * E3))
SLOTS = E3 * CAP3
HALF = SLOTS // P // 2
LN_EPS = 1e-5

F32, F32R, BF16, I32, U32 = (mybir.dt.float32, mybir.dt.float32r, mybir.dt.bfloat16,
                             mybir.dt.int32, mybir.dt.uint32)
ALU = mybir.AluOpType
ACT = mybir.ActivationFunctionType
AX = mybir.AxisListType


def window_start(i):
    return min(max(i - WIN // 2, 0), HW - WIN)


def columns(*pairs):
    at, where = 0, {}
    for name, width in pairs:
        where[name] = slice(at, at + width)
        at += width
    return where, at


CST, CST_W = columns(("ident", P), ("prefix", P), ("pair", C), ("rev", T * E3),
                     ("first", T * E3), ("slot", 10), ("expert", T * E3), ("fb1", E3 * 2), ("twice", C))
W0, W0_W = columns(("wvT", C1), ("wo", C), ("wqk1", 2 * C), ("wv1", C))
WA, WA_W = columns(("w1", E2 * F2), ("wr", E2), ("b2", E2), ("y3", C1), ("gx", 3 * C), ("ga", 3 * C),
                   ("gate", E3), ("fb2", E3))


def hybrid_kernel(nc, x, w8, w0, wa, w3, w2a, w2b, cst, bias_q, bias_k, lnw, out):
    ctx = ExitStack()
    with ctx:
        def sb(name, shape, dt=F32):
            return ctx.enter_context(nc.sbuf_tensor(name, shape, dt))

        sems = {}

        def sem(name):
            if name not in sems:
                sems[name] = ctx.enter_context(nc.semaphore(name))
            return sems[name]

        bank = [ctx.enter_context(nc.psum_tensor(f"bank{i}", [P, 512], F32)) for i in range(8)]

        q_parts = nc.dram_tensor("q_parts", (B, 3, C, N), BF16, kind="Internal").ap()
        k_parts = nc.dram_tensor("k_parts", (B, 5, C, N), BF16, kind="Internal").ap()

        W8 = sb("W8", [D0, 2 * C1])
        W0s = sb("W0s", [C1, W0_W])
        Cs = sb("Cs", [P, CST_W])
        identb = sb("identb", [P, P], BF16)
        onesb = sb("onesb", [P, P], BF16)
        bias_mem = sb("bias_mem", [P, 2 * NH * TB * SPAN])
        mid_mem = sb("mid_mem", [P, 7232])
        half_mem = sb("half_mem", [P, 4992])
        stack_mem = sb("stack_mem", [P, B * NH * N])
        taken = {}

        def view(mem, *shape):
            at = taken.get(id(mem), 0)
            size = int(np.prod(shape[1:]))
            taken[id(mem)] = at + size
            v = mem[0:shape[0], at:at + size]
            if len(shape) == 3:
                return v.rearrange("p (a b) -> p a b", a=shape[1])
            return v.rearrange("p (a b c) -> p a b c", a=shape[1], b=shape[2]) if len(shape) == 4 else v

        def view16(mem, *shape):
            at = taken.get(id(mem), 0)
            size = int(np.prod(shape[1:])) // 2
            taken[id(mem)] = at + size
            v = mem[0:shape[0], at:at + size].bitcast(BF16)
            if len(shape) == 3:
                return v.rearrange("p (a b) -> p a b", a=shape[1])
            return v.rearrange("p (a b c) -> p a b c", a=shape[1], b=shape[2]) if len(shape) == 4 else v

        biasQb = view16(half_mem, P, NH, TB * SPAN)
        biasQ = view(bias_mem, P, NH, TB * SPAN)
        biasK = view(bias_mem, P, NH, TB * SPAN)
        pb = TB * SPAN * len(PE_HEADS)
        bias_rest = bias_mem[:, 0:pb].rearrange("p (h s) -> p h s", h=len(PE_HEADS))
        bias_part = bias_mem[:, pb:pb * 5 // 2].bitcast(BF16).rearrange("p (i h s) -> p i h s", i=3, h=len(PE_HEADS))
        mhalf = sb("mhalf", [P, T])
        ident = Cs[:, CST["ident"]]

        X = sb("X", [P, T, C1])
        XT = sb("XT", [C1, B * N])
        A0 = sb("A0", [C1, C1])
        Wvo = sb("Wvo", [C1, C])
        G0 = sb("G0", [C1, B * N])
        S_P = sb("S_P", [P, B, TB, N])
        S_PT = sb("S_PT", [P, B, TB, N])
        nmax = sb("nmax", [P, T])
        den = sb("den", [P, T])
        rden = sb("rden", [P, T])
        CT = sb("CT", [C1, B * N])
        X1 = sb("X1", [P, T, C])

        gn_st = sb("gn_st", [C, B, 6])
        gn_mv = sb("gn_mv", [C, B, 3])
        gn_g = sb("gn_g", [C, B, 3])
        gn_v = sb("gn_v", [C, B])
        gn_sq = sb("gn_sq", [C, B])
        gn_r = sb("gn_r", [C, B])
        gn_nb = sb("gn_nb", [C, B])
        XN1 = sb("XN1", [C1, B * N])
        QK = view(mid_mem, P, B * N)
        qkr = view(mid_mem, P, B * N)
        part = view16(half_mem, P, 3, B * N)
        words = B * NH * N // 2
        QS, KSt = [stack_mem[0:KS, k * words:(k + 1) * words].bitcast(BF16)
                   .rearrange("r (b h n) -> r b h n", b=B, h=NH) for k in range(2)]
        V1 = view(mid_mem, P, T, NH, VW)
        nm1 = sb("nm1", [P, B, NH, TB], BF16)
        diag1 = view16(half_mem, P, 2, NH, TB * P)
        U1 = view(mid_mem, P, 3, TB * SPAN)
        P1 = view(mid_mem, P, 3, TB * SPAN)
        CT1 = view(mid_mem, P, 2, 512)
        rz1 = sb("rz1", [P, 2, TB * 2, 4])
        ctx1 = sb("ctx1", [P, 2, TB * 2, 4, HD])
        X2 = sb("X2", [P, T, C])

        taken.clear()
        LN = "abucd"
        LN_STEPS = [("a", TB * b, TB) for b in range(B)] + \
                   [(s, h * T // 2, T // 2) for s in "bucd" for h in range(2)]
        ln_st = {s: sb("ln_st" + s, [P, T, 6]) for s in LN}
        ln_mv = {s: sb("ln_mv" + s, [P, T, 2]) for s in LN}
        ln_ve = {s: sb("ln_ve" + s, [P, T]) for s in LN}
        ln_rs = {s: sb("ln_rs" + s, [P, T]) for s in LN}
        ln_nm = {s: sb("ln_nm" + s, [P, T]) for s in LN}
        ln_nb = {s: sb("ln_nb" + s, [P, T]) for s in LN}
        ON_ACT = [("b", 0), ("u", 1), ("c", 0), ("d", 0)]
        XN = {s: sb("XN" + s, [P, T, C1]) for s in "abc"}
        XF = {s: sb("XF" + s, [C1, B * N]) for s in "ab"}
        XN["u"], XN["d"] = XN["a"], XN["b"]
        XF["c"], XF["d"] = XF["a"], XF["b"]
        LHSc = G0
        CTa = XN1[0:C, :]
        CTc = CT
        nmaxa = sb("nmaxa", [P, T])
        dena = sb("dena", [P, T])
        rdena = sb("rdena", [P, T])
        nmaxc = sb("nmaxc", [P, T])
        denc = sb("denc", [P, T])
        rdenc = sb("rdenc", [P, T])
        X3 = sb("X3", [P, T, C])
        WAs = sb("WAs", [C1, WA_W])
        W2A = view(half_mem, P, E2, C)
        msum = sb("msum", [C, B])
        mean2 = sb("mean2", [C1, B])
        lg = sb("lg", [B, 8, E2])
        col = sb("col", [B, 10])
        top_i = sb("top_i", [B, 8], U32)
        spread = sb("spread", [B, 2, B, TOPK])
        loads1 = sb("loads1", [B, B])
        ones4 = sb("ones4", [B, P])
        tw = sb("tw", [P, B * TOPK])
        slot_e = sb("slot_e", [1, B * TOPK], I32)
        W1sel = view(stack_mem, C1, B * TOPK, F2)
        W2sel = view(stack_mem, P, B * TOPK, C)
        chosen = sb("chosen", [P, B * TOPK])
        b2w = sb("b2w", [C, B * TOPK, E2])
        b2sel = sb("b2sel", [C, B])
        H2 = view(bias_mem, P, B, TOPK * N)
        UT = view(half_mem, C, B * N)
        U = view(mid_mem, P, T, C)
        gb = sb("gb", [P, 2, C])
        X3b = view(mid_mem, P, T, C)
        un = view(stack_mem, P, T, C)
        X4 = view(half_mem, P, T, C)
        th = view(stack_mem, P, T, 3 * C)
        gm = view(stack_mem, P, T, 2 * C)
        gs = sb("gs", [P, T, C])
        X5 = view(bias_mem, P, T, C)
        W3s = view(mid_mem, P, E3, F3)
        W2B = view(mid_mem, P, E3, 2, C)
        mx3 = sb("mx3", [P, T])
        d3 = sb("d3", [P, T, E3])
        ex3 = sb("ex3", [P, T, E3])
        prb = sb("prb", [P, T])
        se3 = sb("se3", [P, T])
        rv3 = sb("rv3", [P, T, E3])
        mr3 = sb("mr3", [P, T])
        ohb = sb("ohb", [P, T, E3], BF16)
        prefixb = sb("prefixb", [P, P], BF16)
        sel3 = sb("sel3", [P, T, 2, E3])
        number = sb("number", [P, T])
        gate3 = sb("gate3", [P, T])
        sid = sb("sid", [P, T])
        iota_f = view(half_mem, P, SLOTS)
        XHL = sb("XHL", [P, T, 2, C], F32R)
        one_hot = sb("one_hot", [P, 4 * T * P], F32R)
        G3 = one_hot[:, 0:3 * SLOTS].rearrange("p (k s) -> p k s", k=3)
        GT = one_hot[:, :].rearrange("p (k n) -> p k n", k=4)
        XB = view(stack_mem, P, SLOTS)
        H3 = view(bias_mem, P, 3, 2, CAP3)
        YT = view(stack_mem, C, SLOTS)
        YHL = sb("YHL", [P, SLOTS // P, 2, C], F32R)
        twice = sb("twice", [P, C], F32R)
        onesf = sb("onesf", [P, P], F32R)
        SD = YHL[:, :, :, :].rearrange("p j k c -> p (j k c)")[:, 0:T * P].rearrange("p (t q) -> p t q", t=T)
        SB = view(bias_mem, P, T * P)
        ZT = XHL[:, :, :, :].rearrange("p t k c -> p (t k c)")
        y3 = view(mid_mem, P, T, C)
        sat3 = view(mid_mem, P, T, C)
        nan3 = view(mid_mem, P, T, C)
        wild3 = sb("wild3", [P, T, C])
        Y6 = view(mid_mem, P, T, C)
        table = sb("table", [1, 1])

        def by_dve(n):
            return n - sum(k % NH in PE_HEADS for k in range(n))

        def normed(engine, s, b):
            half = b // (B // 2)
            if (s, half) in ON_ACT:
                engine.wait_ge(sem("xn_act"), B // 2 * ON_ACT.index((s, half)) + b % (B // 2) + 1)
            else:
                others = sum((s, h) in ON_ACT for h in range(half))
                engine.wait_ge(sem(s + "_xn"), b + 1 - B // 2 * others)

        def through(s):
            return B if s == "c" else 0

        UP3 = ((bank[3], bank[4]), (bank[5], bank[2]))
        TURN_Y = (bank[6], bank[3])

        block = ctx.enter_context(nc.Block())

        x_t = x.rearrange("b (q p) c -> b p q c", p=P)
        o_t = out.rearrange("b (q p) c -> b p q c", p=P)

        def store(queue, b, target, source, parts):
            queue.wait_ge(sem("qk_part"), 3 * b + parts)
            queue.dma_start(target.rearrange("i r n -> r i n"), source[:, 0:parts, b * N:b * N + N]) \
                .then_inc(sem(f"parts_stored{b}"), 16)

        def store_queries(queue, b):
            store(queue, b, q_parts[b], part[0:C], 3)

        def store_keys(queue, b):
            store(queue, b, k_parts[b, 0:3], part[C:2 * C], 3)

        def store_repeated(queue, b):
            store(queue, b, k_parts[b, 3:5], part[C:2 * C], 2)

        def load_stack(queue, b, pieces):
            queue.wait_ge(sem(f"parts_stored{b}"), 3 * 16)
            for piece in pieces:
                if piece == "queries":
                    rows = q_parts[b].rearrange("i (d h) n -> (i d) (h n)", h=NH)
                    stack, rows = QS, rows.unsqueeze(0).to_broadcast([3, 3 * HD, NH * N])
                else:
                    rows = k_parts[b, piece:piece + 3].rearrange("i (d h) n -> (i d) (h n)", h=NH)
                    stack = KSt[3 * HD * piece:3 * HD * piece + 3 * HD]
                queue.dma_start(stack[:, b, :, :].rearrange("r h n -> r (h n)"), rows) \
                    .then_inc(sem(f"stack_landed{b}"), 16)

        def final(sp):
            for b in range(0, B, 2):
                sp.wait_ge(sem("y6"), b + 2)
                for k in range(2):
                    sp.dma_start(o_t[b + k], Y6[:, TB * (b + k):TB * (b + k) + TB, :]) \
                        .then_inc(sem("out_stored"), 16)
            sp.wait_ge(sem("out_stored"), 16 * B)

        @block.sync
        def _(sp):
            sp.dma_start(X[:, 0:TB, 0:C], x_t[0]).then_inc(sem("x_landed0"), 16)
            sp.dma_start(Cs[:, :], cst).then_inc(sem("cst_landed"), 16)
            for b in range(1, B):
                sp.dma_start(X[:, TB * b:TB * b + TB, 0:C], x_t[b]).then_inc(sem(f"x_landed{b}"), 16)
            sp.dma_start(biasQ[:, :, :], bias_q).then_inc(sem("biasQ_landed"), 16)
            sp.dma_start(biasK[:, :, :], bias_k).then_inc(sem("biasK_landed"), 16)
            sp.dma_start(WAs[:, :], wa).then_inc(sem("wa_landed"), 16)
            store_repeated(sp, 0)
            store_queries(sp, 0)
            load_stack(sp, 0, ("queries", 1))
            for b in range(1, B):
                store_repeated(sp, b)
                store_queries(sp, b)
                store_keys(sp, b)
                load_stack(sp, b, ("queries", 0, 1, 2))
            sp.wait_ge(sem("x2_done"), B)
            sp.dma_start(W2A[:, :, :], w2a).then_inc(sem("w2a_landed"), 16)
            sp.dma_start(gb[:, :, :], lnw.unsqueeze(0).to_broadcast([P, 2, C])).then_inc(sem("gb_landed"), 16)
            sp.dma_start(W3s[:, :, :], w3).then_inc(sem("w3_landed"), 16)
            sp.dma_start(W2B[:, :, :, :], w2b).then_inc(sem("w2b_landed"), 16)
            final(sp)

        @block.gpsimd
        def _(pool):
            for k, (tile, value) in enumerate([
                    (XT[C:C1, :], 1.0), (X[:, :, C:C1], 1.0), (XN1[C:C1, :], 1.0), (mhalf[:, :], -0.5),
                    (V1[:, :, :, HD:VW], 0.0), (V1[:, :, :, HD:HD + 1], 1.0)]):
                if k:
                    pool.wait_ge(sem("pool_const"), k)
                pool.memset(tile, value).then_inc(sem("pool_const"), 1)
            pool.wait_ge(sem("cst_landed"), 16)
            pool.tensor_copy(identb[:, :], ident).then_inc(sem("pool_const"), 1)
            pool.wait_ge(sem("biasQ_landed"), 16)
            pool.tensor_copy(biasQb[:, :, :], biasQ[:, :, :]).then_inc(sem("pool_const"), 1)
            pool.wait_ge(sem("biasK_landed"), 16)
            pool.wait_ge(sem("pool_const"), 8)
            some_heads = slice(PE_HEADS[0], NH, PE_HEADS[1] - PE_HEADS[0])
            pool.tensor_copy(bias_part[:, 0, :, :], biasK[:, some_heads, :]).then_inc(sem("bias_part"), 1)
            pool.wait_ge(sem("bias_part"), 1)
            pool.tensor_tensor(bias_rest[:, :, :], biasK[:, some_heads, :], bias_part[:, 0, :, :], ALU.subtract) \
                .then_inc(sem("bias_part"), 1)
            pool.wait_ge(sem("gn_step"), 2)
            pool.tensor_tensor(gn_r[:, :], gn_v[:, :], mhalf[0:C, 0:B], ALU.pow).then_inc(sem("gn_rstd"), 1)
            pool.wait_ge(sem("bias_part"), 2)
            pool.tensor_copy(bias_part[:, 1, :, :], bias_rest[:, :, :]).then_inc(sem("bias_part"), 1)
            pool.wait_ge(sem("bias_part"), 3)
            pool.tensor_tensor(bias_part[:, 2, :, :], bias_rest[:, :, :], bias_part[:, 1, :, :], ALU.subtract) \
                .then_inc(sem("bias_part"), 1)
            for k, (tile, value) in enumerate([
                    (XN["c"][:, :, C:C1], 1.0), (XF["a"][C:C1, :], 1.0),
                    (XF["b"][C:C1, :], 1.0),
                    (mean2[C:C1, :], 1.0), (ones4[:, :], 1.0), (loads1[:, :], float(N))]):
                if k:
                    pool.wait_ge(sem("later_const"), k)
                pool.memset(tile, value).then_inc(sem("later_const"), 1)
            pool.tensor_copy(prefixb[:, :], Cs[:, CST["prefix"]]).then_inc(sem("later_const"), 1)

            def rstd(s, half=0):
                n = LN_STEPS.index((s, half * T // 2, T // 2) if s != "a" else (s, TB * half, TB))
                t = slice(LN_STEPS[n][1], LN_STEPS[n][1] + LN_STEPS[n][2])
                pool.wait_ge(sem("ln_mv"), n + 1)
                pool.tensor_scalar(ln_ve[s][:, t], ln_mv[s][:, t, 1], LN_EPS, None, ALU.add) \
                    .then_inc(sem("ln_ve"), 1)
                on_act = (s, half) in ON_ACT
                if on_act:
                    pool.tensor_scalar(ln_nm[s][:, t], ln_mv[s][:, t, 0], -1.0, None, ALU.mult) \
                        .then_inc(sem("ln_nm"), 1)
                pool.wait_ge(sem("ln_ve"), n + 1)
                pool.tensor_tensor(ln_rs[s][:, t], ln_ve[s][:, t], mhalf[:, t], ALU.pow).then_inc(sem("ln_rs"), 1)
                if on_act:
                    pool.wait_ge(sem("ln_rs"), n + 1)
                    pool.wait_ge(sem("ln_nm"), 2 * ON_ACT.index((s, half)) + 1)
                    pool.tensor_tensor(ln_nb[s][:, t], ln_nm[s][:, t], ln_rs[s][:, t], ALU.mult) \
                        .then_inc(sem("ln_nm"), 1)

            for b in range(B):
                for h in range(NH):
                    pool.wait_ge(sem("nm1"), b * NH + h + 1)
                    if b >= 2:
                        pool.wait_ge(sem("s1"), (b - 2) * NH + h + 1)
                    pool.tensor_tensor(
                        diag1[:, b % 2, h, :].rearrange("p (q k) -> p q k", q=TB),
                        identb[:, :].unsqueeze(1).to_broadcast([P, TB, P]),
                        nm1[:, b, h, :].unsqueeze(2).to_broadcast([P, TB, P]), ALU.mult) \
                        .then_inc(sem("diag1"), 1)
                    if h == 6 and b >= 2:
                        rstd("a", b - 2)
            for b in range(2, B):
                rstd("a", b)
            pool.wait_ge(sem("x2_done"), B)
            pool.iota(iota_f[:, :], [[1, SLOTS]], base=1, channel_multiplier=0,
                      allow_small_or_imprecise_dtypes=True).then_inc(sem("later_const"), 1)
            for half in range(2):
                rstd("b", half)
            pool.wait_ge(sem("gb_landed"), 16)
            pool.tensor_tensor(X3b[:, :, :], X3[:, :, :], gb[:, 1, :].unsqueeze(1).to_broadcast([P, T, C]), ALU.add) \
                .then_inc(sem("x3b"), 1)
            for half in range(2):
                rstd("u", half)
            for half in range(2):
                rstd("c", half)
            for half in range(2):
                rstd("d", half)
            pool.wait_ge(sem("sid"), 1)
            pool.tensor_tensor(SD[:, :, :], ident.unsqueeze(1).to_broadcast([P, T, P]),
                               sid[:, :].unsqueeze(2).to_broadcast([P, T, P]), ALU.mult).then_inc(sem("sd"), 1)
            for h in range(2):
                t = slice(h * T // 2, (h + 1) * T // 2)
                pool.wait_ge(sem("y3"), h + 1)
                pool.tensor_tensor(Y6[:, t, :], y3[:, t, :], X5[:, t, :], ALU.add).then_inc(sem("sum3"), 1)

        @block.tensor
        def _(pe):
            def keep_warm(n, idle):
                for _ in range(n):
                    pe.matmul(idle[:, :].rearrange("p (k q) -> p k q", k=4), onesb[:, :],
                              onesb[:, :].unsqueeze(1).to_broadcast([P, 4, P]), start=True, stop=True)

            pe.wait_ge(sem("onesb"), 1)
            keep_warm(WARM["start"], bank[2])
            pe.wait_ge(sem("w8_landed"), 16)
            pe.matmul(bank[6][0:C1, 0:C1], W8[:, 0:C1], W8[:, C1:2 * C1], start=True, stop=True) \
                .then_inc(sem("a0"), 1)
            pe.wait_ge(sem("w0_landed"), 16)
            pe.matmul(bank[7][0:C1, 0:C], W0s[:, W0["wvT"]], W0s[:, W0["wo"]], start=True, stop=True) \
                .then_inc(sem("wvo"), 1)
            pe.wait_ge(sem("cst_landed"), 16)

            def scores(b, lhs, rhs):
                for q in range(TB):
                    last = pe.matmul(bank[4 + b % 2][:, q * N:q * N + N], lhs[:, b * N + q * P:b * N + q * P + P],
                                     rhs[:, b * N:b * N + N], start=True, stop=True)
                return last

            def transpose_p(b):
                for k in range(TB):
                    for q in range(TB):
                        last = pe.transpose(bank[6 + b % 2][:, k * N + q * P:k * N + q * P + P],
                                            S_P[:, b, q, k * P:k * P + P], ident)
                return last

            def attend(b, values, width):
                for k in range(TB):
                    last = pe.matmul(bank[2 + b % 2][0:width, 0:N], values[:, TB * b + k, 0:width],
                                     S_PT[:, b, k, :], start=(k == 0), stop=(k == TB - 1))
                return last

            for b in range(B):
                pe.wait_ge(sem(f"x_landed{b}"), 16)
                for q in range(TB):
                    last = pe.transpose(bank[b][0:C, q * P:q * P + P], X[:, TB * b + q, 0:C], ident)
                last.then_inc(sem("xt_p"), 1)
            for b in range(B):
                pe.wait_ge(sem("xt"), b + 1)
                if b == 0:
                    pe.wait_ge(sem("pool_const"), 1)
                    pe.wait_ge(sem("scaled"), 1)
                pe.matmul(bank[b][0:C1, 0:N], A0[:, :], XT[:, b * N:b * N + N], start=True, stop=True) \
                    .then_inc(sem("g0_p"), 1)
            for i in range(B + 3):
                if i < B:
                    pe.wait_ge(sem("g0"), i + 1)
                    if i >= 2:
                        pe.wait_ge(sem("exp0"), 2 * (i - 1))
                    scores(i, G0, XT).then_inc(sem("s0"), 1)
                if 0 <= i - 1 < B:
                    b = i - 1
                    pe.wait_ge(sem("exp0"), 2 * b + 2)
                    if b == 0:
                        pe.wait_ge(sem("wvo_s"), 1)
                    if b >= 2:
                        pe.wait_ge(sem("pt0"), b - 1)
                    transpose_p(b).then_inc(sem("pt0_p"), 1)
                if 0 <= i - 2 < B:
                    b = i - 2
                    pe.wait_ge(sem("pt0"), b + 1)
                    if b == 0:
                        pe.wait_ge(sem("pool_const"), 2)
                        pe.wait_ge(sem("g0"), 4)
                    if b >= 2:
                        pe.wait_ge(sem("ct0"), b - 1)
                    attend(b, X, C1).then_inc(sem("ct0_p"), 1)
                if 0 <= i - 3 < B:
                    b = i - 3
                    pe.wait_ge(sem("ct0"), b + 1)
                    if b >= 2:
                        pe.wait_ge(sem("x1"), b - 1)
                    for q in range(TB):
                        last = pe.matmul(bank[b % 2][:, q * C:q * C + C], CT[:, b * N + q * P:b * N + q * P + P],
                                         Wvo[:, :], start=True, stop=True)
                    last.then_inc(sem("o0"), 1)

            for b in range(B):
                pe.wait_ge(sem("x1"), b + 1)
                for q in range(TB):
                    last = pe.transpose(bank[4 + b][0:C, q * P:q * P + P], X1[:, TB * b + q, :], ident)
                last.then_inc(sem("x1t_p"), 1)
            pe.wait_ge(sem("gn_step"), 1)
            pe.matmul(bank[0][0:C, 0:3 * B], Cs[0:C, CST["pair"]], gn_mv[:, :, :].rearrange("c b k -> c (b k)"),
                      start=True, stop=True).then_inc(sem("gn_pair"), 1)
            for b in range(B):
                pe.wait_ge(sem("xn1_a" if b % 2 else "xn1"), b // 2 + 1)
                if b == 0:
                    pe.wait_ge(sem("pool_const"), 6)
                    pe.wait_ge(sem("scaled"), 2)
                pe.matmul(bank[b][:, 0:N], W0s[:, W0["wqk1"]], XN1[:, b * N:b * N + N], start=True, stop=True) \
                    .then_inc(sem("qk_p"), 1)
            for t in range(T):
                last = pe.matmul(bank[4][:, t * C:t * C + C], XN1[:, t * P:t * P + P], W0s[:, W0["wv1"]],
                                 start=True, stop=True)
            last.then_inc(sem("v1_p"), 1)

            def max_scores(b, h):
                n = b * NH + h
                if n == 0:
                    keep_warm(WARM["stacks"], bank[7])
                if h == 0:
                    pe.wait_ge(sem(f"stack_landed{b}"), 4 * 16)
                    if b == 0:
                        pe.wait_ge(sem("pool_const"), 8)
                        pe.wait_ge(sem("qkf"), B - 1)
                if n >= 2:
                    pe.wait_ge(sem("nm1"), n - 1)
                for q in range(TB):
                    dst = bank[n % 2][:, q * SPAN:q * SPAN + SPAN]
                    pe.matmul(dst, QS[:, b, h, q * P:q * P + P], KSt[:, b, h, OFF[q]:OFF[q] + SPAN],
                              start=True, stop=False)
                    last = pe.matmul(dst, identb[:, :], biasQb[:, h, q * SPAN:q * SPAN + SPAN],
                                     start=False, stop=True)
                last.then_inc(sem("mx1"), 1)

            def exact_scores(b, h):
                n = b * NH + h
                pe.wait_ge(sem("diag1"), n + 1)
                if n >= 2:
                    if (n - 2) % NH in PE_HEADS:
                        pe.wait_ge(sem("p1"), n - 1)
                    else:
                        pe.wait_ge(sem("u1"), by_dve(n - 2) + 1)
                if n == PE_HEADS[0]:
                    pe.wait_ge(sem("bias_part"), 4)
                for k in range(TB):
                    span = slice(k * SPAN, k * SPAN + SPAN)
                    dst = bank[2 + n % 2][:, span]
                    pe.matmul(dst, KSt[:, b, h, k * P:k * P + P], QS[:, b, h, OFF[k]:OFF[k] + SPAN],
                              start=True, stop=False)
                    if h in PE_HEADS:
                        for i in range(3):
                            pe.matmul(dst, identb[:, :], bias_part[:, i, PE_HEADS.index(h), span],
                                      start=False, stop=False)
                    last = pe.matmul(dst, onesb[:, :], diag1[:, b % 2, h, OFF[k]:OFF[k] + SPAN],
                                     start=False, stop=True)
                last.then_inc(sem("s1"), 1)

            def attend1(b, h):
                n = b * NH + h
                pe.wait_ge(sem("p1"), n + 1)
                if n == 0:
                    pe.wait_ge(sem("v1"), 1)
                if h == 0 and b >= 2:
                    pe.wait_ge(sem("ct1"), b - 1)
                g, c0 = h % 4, (h // 4) * N
                for k in range(TB):
                    last = pe.matmul(bank[4 + b % 2][32 * g:32 * g + VW, c0 + OFF[k]:c0 + OFF[k] + SPAN],
                                     V1[:, TB * b + k, h, :], P1[:, n % 3, k * SPAN:k * SPAN + SPAN],
                                     start=(k == 0), stop=(k == TB - 1), skip_group_check=True)
                last.then_inc(sem("av1"), 1)

            def turn1(b):
                pe.wait_ge(sem("ct1"), b + 1)
                if b >= 1:
                    pe.wait_ge(sem("ctx1"), b)
                for q in range(TB):
                    for g in range(2):
                        j = q * 2 + g
                        last = pe.transpose(bank[6][:, j * P:j * P + P],
                                            CT1[:, b % 2, g * N + q * P:g * N + q * P + P], ident)
                last.then_inc(sem("turn1"), 1)

            LAG = 2
            for n in range(AHEAD):
                max_scores(n // NH, n % NH)
            for n in range(B * NH + LAG):
                b, h = divmod(n, NH)
                if b < B:
                    if n + AHEAD < B * NH:
                        max_scores((n + AHEAD) // NH, (n + AHEAD) % NH)
                    exact_scores(b, h)
                m = n - LAG
                if m >= 0:
                    attend1(m // NH, m % NH)
                    if m % NH == 2 and m // NH >= 1:
                        turn1(m // NH - 1)

            def features(s, b, i):
                normed(pe, s, b)
                for q in range(TB):
                    last = pe.transpose(bank[i][0:C, q * P:q * P + P], XN[s][:, TB * b + q, 0:C], ident)
                last.then_inc(sem(s + "_xf_p"), 1)

            def self_attention(s, lhs, width, hand_on, warm, middle=None):
                for i in range(B + 5):
                    keep_warm(warm.get(i, 0), bank[7])
                    if s == "a" and i == 2:
                        turn1(B - 1)
                    if 0 <= i - 2 < B:
                        b = i - 2
                        pe.wait_ge(sem("c_lhs" if middle else "a_xf"), b + 1)
                        if b == 0:
                            pe.wait_ge(sem("later_const"), 6)
                        if b >= 2:
                            pe.wait_ge(sem("att_exp"), 2 * through(s) + 2 * (b - 1))
                        scores(b, lhs, XF[s]).then_inc(sem("att_s"), 1)
                    if i < B:
                        if i >= 2:
                            pe.wait_ge(sem(s + "_xf"), i - 1)
                        elif s == "a":
                            pe.wait_ge(sem("nm1"), B * NH - 1 + i)
                        features(s, i, i % 2)
                    if middle and 0 <= i - 1 < B:
                        middle(i - 1)
                    if 0 <= i - 3 < B:
                        b = i - 3
                        pe.wait_ge(sem("c_pn" if s == "c" else "att_exp"), 2 * b + 2)
                        if b >= 2:
                            pe.wait_ge(sem("att_pt"), through(s) + b - 1)
                        transpose_p(b).then_inc(sem("att_pt_p"), 1)
                    if 0 <= i - 4 < B:
                        b = i - 4
                        pe.wait_ge(sem("att_pt"), through(s) + b + 1)
                        if b >= 2:
                            pe.wait_ge(sem("att_ct"), through(s) + b - 1)
                        attend(b, XN[s], width).then_inc(sem("att_ct_p"), 1)
                    if i >= 5:
                        hand_on(i - 5)

            def hand_on_a(b):
                pe.wait_ge(sem("att_ct"), b + 1)
                if b == 0:
                    pe.wait_ge(sem("a_xf"), B)
                if b >= 2:
                    pe.wait_ge(sem("x3"), b - 1)
                for q in range(TB):
                    last = pe.transpose(bank[b % 2][:, q * C:q * C + C], CTa[:, b * N + q * P:b * N + q * P + P],
                                        ident[0:C, 0:C])
                last.then_inc(sem("a_turned"), 1)

            self_attention("a", XF["a"], C, hand_on_a, WARM["a_steps"])

            keep_warm(WARM["b_norm"], bank[7])
            for b in range(B):
                if b < 2:
                    pe.wait_ge(sem("x3"), b + 3)
                features("b", b, b)
            keep_warm(WARM["logits"], bank[7])
            pe.wait_ge(sem("mean2"), 1)
            pe.wait_ge(sem("wa_landed"), 16)
            pe.matmul(bank[4][0:B, 0:E2], mean2[:, :], WAs[:, WA["wr"]], start=True, stop=True) \
                .then_inc(sem("r_logits"), 1)
            keep_warm(WARM["loads"], bank[7])
            pe.wait_ge(sem("r_rw"), 1)
            pe.matmul(bank[5][0:B, 0:E2], loads1[:, :], lg[:, 1, :], start=True, stop=True) \
                .then_inc(sem("r_loads"), 1)
            keep_warm(WARM["routing"], bank[7])
            pe.wait_ge(sem("r_spread"), 2)
            pe.matmul(bank[6][:, 0:2 * B * TOPK], ones4[:, :], spread[:, :, :, :].rearrange("p a b k -> p (a b k)"),
                      start=True, stop=True).then_inc(sem("r_bcast"), 1)
            keep_warm(WARM["selection"], bank[7])
            for i in range(B + 2):
                if i < B:
                    b = i
                    pe.wait_ge(sem("sel_a"), 2 * b + 1)
                    pe.wait_ge(sem("sel_v"), 2 * b + 1)
                    pe.wait_ge(sem("b_xf"), B)
                    for k in range(TOPK):
                        last = pe.matmul(bank[b][:, k * N:k * N + N], W1sel[:, TOPK * b + k, :],
                                         XF["b"][:, b * N:b * N + N], start=True, stop=True)
                    last.then_inc(sem("up2"), 1)
                if 0 <= i - 1 < B:
                    b = i - 1
                    pe.wait_ge(sem("gelu"), b + 1)
                    pe.wait_ge(sem("sel_a"), 2 * b + 2)
                    pe.wait_ge(sem("sel_v"), 2 * b + 2)
                    if b == 0:
                        pe.wait_ge(sem("r_spread_read"), 2)
                    if b >= 2:
                        pe.wait_ge(sem("ut"), b - 1)
                    for k in range(TOPK):
                        last = pe.matmul(bank[4 + b % 2][0:C, 0:N], W2sel[:, TOPK * b + k, :],
                                         H2[:, b, k * N:k * N + N], start=(k == 0), stop=(k == TOPK - 1))
                    last.then_inc(sem("down2"), 1)
                if 0 <= i - 2 < B:
                    b = i - 2
                    pe.wait_ge(sem("ut"), b + 1)
                    if b >= 2:
                        pe.wait_ge(sem("u"), b - 1)
                    for q in range(TB):
                        last = pe.transpose(bank[6 + b % 2][:, q * C:q * C + C], UT[:, b * N + q * P:b * N + q * P + P],
                                            ident[0:C, 0:C])
                    last.then_inc(sem("u_turned"), 1)

            def middle_c(b):
                pe.wait_ge(sem("c_xf"), b + 1)
                if b >= 2:
                    pe.wait_ge(sem("c_lhs"), b - 1)
                pe.matmul(bank[2 + b % 2][0:C1, 0:N], WAs[:, WA["y3"]], XF["c"][:, b * N:b * N + N],
                          start=True, stop=True).then_inc(sem("c_lhs_p"), 1)

            def hand_on_c(b):
                pe.wait_ge(sem("att_ct"), B + b + 1)
                if b == 0:
                    pe.wait_ge(sem("c_xf"), B)
                if b >= 2:
                    pe.wait_ge(sem("tanh"), 2 * (b - 1))
                for q in range(TB):
                    c = slice(b * N + q * P, b * N + q * P + P)
                    dst = bank[b % 2][:, q * 3 * C:(q + 1) * 3 * C]
                    pe.matmul(dst, XF["c"][:, c], WAs[:, WA["gx"]], start=True, stop=False)
                    last = pe.matmul(dst, CTc[:, c], WAs[:, WA["ga"]], start=False, stop=True)
                last.then_inc(sem("gates"), 1)

            keep_warm(WARM["c_norm"], bank[0])
            pe.wait_ge(sem("gelu"), B)
            self_attention("c", LHSc, C1, hand_on_c, WARM["c_steps"], middle_c)

            for i in range(B + 2):
                if i < B:
                    if i < 2:
                        pe.wait_ge(sem("tanh"), 2 * (i + 3))
                    if i == 0:
                        keep_warm(WARM["d_norm"], bank[7])
                    if i == 2:
                        keep_warm(WARM["d_norm_2"], bank[7])
                    features("d", i, i)
                if i >= 2:
                    pe.wait_ge(sem("d_xf"), i - 1)
                    for t in range(TB * (i - 2), TB * (i - 1)):
                        last = pe.matmul(bank[4][:, t * E3:t * E3 + E3], XF["d"][:, t * P:t * P + P],
                                         WAs[:, WA["gate"]], start=True, stop=True)
            last.then_inc(sem("logits3"), 1)
            keep_warm(WARM["first_expert"], bank[7])
            pe.wait_ge(sem("ohb"), 1)
            pe.wait_ge(sem("later_const"), 7)
            flat = ohb[:, :, :].rearrange("p t e -> p (t e)")
            last = pe.matmul(bank[5][:, 0:T * E3], prefixb[:, :], flat, start=True, stop=False, skip_group_check=True)
            for back in range(1, T):
                last = pe.matmul(bank[5][:, back * E3:T * E3], onesb[:, :], flat[:, 0:(T - back) * E3],
                                 start=False, stop=(back == T - 1), skip_group_check=True)
            last.then_inc(sem("counts"), 1)
            keep_warm(WARM["slots"], bank[7])
            chunks = [(0, 512), (512, 512), (1024, 256)]
            for t in range(T):
                pe.wait_ge(sem("g3"), t + 1)
                if t == 0:
                    pe.wait_ge(sem("xl"), 1)
                for c, (at, width) in enumerate(chunks):
                    last = pe.matmul(bank[c][:, 0:width], XHL[:, t, :, :].rearrange("p k c -> p (k c)"),
                                     G3[:, t % 3, at:at + width], start=(t == 0), stop=(t == T - 1))
                last.then_inc(sem("gathered"), 1)
                if t == 4:
                    pe.wait_ge(sem("onesb"), 2)
                    pe.wait_ge(sem("sd"), 1)
                    for h in range(2):
                        last = pe.matmul(bank[6 + h][:, :], onesf[:, :],
                                         SD[:, 4 * h:4 * h + 4, :].rearrange("p t q -> p (t q)"), start=True, stop=True)
                    last.then_inc(sem("sb_p"), 1)

            def turn_y(half):
                if half == 0:
                    pe.wait_ge(sem("sb"), 2)
                pe.wait_ge(sem("yt"), E3 // 2 * (half + 1))
                for j in range(HALF):
                    last = pe.transpose(TURN_Y[half][:, j * C:j * C + C],
                                        YT[:, (half * HALF + j) * P:(half * HALF + j + 1) * P], ident[0:C, 0:C])
                last.then_inc(sem("y_turned"), 1)

            def scatter(j):
                pe.wait_ge(sem("yl"), j // HALF + 1)
                pe.wait_ge(sem("gt"), j + 1)
                if j == 0:
                    pe.wait_ge(sem("sb"), 2)
                for c in range(2):
                    last = pe.matmul(bank[6 + c][:, :], YHL[:, j, :, :].rearrange("p k c -> p (k c)"),
                                     GT[:, j % 4, c * 512:c * 512 + 512], start=(j == 0), stop=(j == 2 * HALF - 1))
                last.then_inc(sem("scattered"), 1)

            for e in range(E3 + 1):
                if e < E3:
                    pe.wait_ge(sem("xb"), 1 if e == 0 else 2)
                    if e == 0:
                        pe.wait_ge(sem("w3_landed"), 16)
                    if e == 3:
                        pe.wait_ge(sem("xb_v"), 1)
                    if e >= 2:
                        pe.wait_ge(sem("h3"), e - 1)
                        pe.wait_ge(sem("h3_v"), e - 1)
                    for k in range(2):
                        last = pe.matmul(UP3[k][e % 2][:, 0:CAP3], W3s[:, e, k * P:k * P + P],
                                         XB[:, e * CAP3:e * CAP3 + CAP3], start=True, stop=True)
                    last.then_inc(sem("up3"), 1)
                if e == 5:
                    turn_y(0)
                if e >= 6:
                    for j in range(2 * (e - 6), min(2 * (e - 6) + 2, HALF)):
                        scatter(j)
                if e >= 1:
                    f = e - 1
                    pe.wait_ge(sem("h3"), f + 1)
                    pe.wait_ge(sem("h3_v"), f + 1)
                    if f == 0:
                        pe.wait_ge(sem("w2b_landed"), 16)
                    if f == 1:
                        pe.wait_ge(sem("xb_v"), 1)
                    if f >= 2:
                        pe.wait_ge(sem("yt"), f - 1)
                    dst = bank[f % 2]
                    for k in range(2):
                        last = pe.matmul(dst[0:C, 0:CAP3], W2B[:, f, k, :], H3[:, f % 3, k, :],
                                         start=(k == 0), stop=(k == 1))
                    last.then_inc(sem("down3"), 1)
            keep_warm(WARM["results"], bank[4])
            turn_y(1)
            keep_warm(WARM["results_low"], bank[4])
            for j in range(HALF, 2 * HALF):
                scatter(j)
            pe.wait_ge(sem("xl"), 2)
            for h in range(2):
                pe.wait_ge(sem("zt"), 1)
                pe.wait_ge(sem("zt_v"), 1)
                for q in range(T // 2):
                    t = h * T // 2 + q
                    last = pe.matmul(bank[h][:, q * C:q * C + C], ZT[:, t * P:t * P + P], twice[:, :],
                                     start=True, stop=True)
                last.then_inc(sem("z_turned"), 1)

        @block.scalar
        def _(act):
            act.dma_start(W8[:, :], w8).then_inc(sem("w8_landed"), 16)
            act.dma_start(W0s[:, :], w0).then_inc(sem("w0_landed"), 16)
            act.wait_ge(sem("a0"), 1)
            act.activation(A0[:, :], bank[6][0:C1, 0:C1], ACT.Copy, scale=float(D0) ** -0.5) \
                .then_inc(sem("scaled"), 1)
            act.wait_ge(sem("w0_landed"), 16)
            wq = W0s[:, W0["wqk1"].start:W0["wqk1"].start + C]
            act.activation(wq, wq, ACT.Copy, scale=float(HD) ** -0.5).then_inc(sem("scaled"), 1)
            for b in range(B):
                act.wait_ge(sem("g0_p"), b + 1)
                act.activation(G0[:, b * N:b * N + N], bank[b][0:C1, 0:N], ACT.Copy).then_inc(sem("g0"), 1)
            for i in range(B + 1):
                if i < B:
                    act.wait_ge(sem("nm0"), i + 1)
                    for q in range(TB):
                        t = TB * i + q
                        act.activation(S_P[:, i, q, :], bank[4 + i % 2][:, q * N:q * N + N], ACT.Exp,
                                       bias=nmax[:, t:t + 1], accum_out=den[:, t:t + 1]).then_inc(sem("exp0"), 1)
                if i >= 1:
                    b = i - 1
                    act.wait_ge(sem("ct0_p"), b + 1)
                    act.activation(CT[:, b * N:b * N + N], bank[2 + b % 2][0:C1, 0:N], ACT.Copy) \
                        .then_inc(sem("ct0"), 1)
            act.wait_ge(sem("gn_step"), 3)
            act.wait_ge(sem("gn_rstd"), 1)
            for b in (1, 3):
                act.activation(XN1[0:C, b * N:b * N + N], bank[4 + b][0:C, 0:N], ACT.Identity,
                               bias=gn_nb[:, b:b + 1], scale=gn_r[:, b:b + 1]).then_inc(sem("xn1_a"), 1)
            for b in range(1, B):
                act.wait_ge(sem("qk_p"), b + 1)
                act.activation(QK[:, b * N:b * N + N], bank[b][:, 0:N], ACT.Copy).then_inc(sem("qkf"), 1)
            store_keys(act, 0)
            load_stack(act, 0, (0, 2))
            act.wait_ge(sem("v1_p"), 1)
            act.activation(V1[:, :, :, 0:HD],
                           bank[4][:, :].rearrange("p (t h d) -> p t h d", t=T, h=NH), ACT.Copy).then_inc(sem("v1"), 1)
            for n in range(B * NH + 3):
                b, h = divmod(n, NH)
                if b < B:
                    if n >= 3:
                        act.wait_ge(sem("av1"), n - 2)
                    if h in PE_HEADS:
                        act.wait_ge(sem("s1"), n + 1)
                        act.activation(P1[:, n % 3, :], bank[2 + n % 2][:, 0:TB * SPAN], ACT.Exp) \
                            .then_inc(sem("p1"), 1)
                    else:
                        act.wait_ge(sem("u1"), by_dve(n) + 1)
                        act.activation(P1[:, n % 3, :], U1[:, n % 3, :], ACT.Exp).then_inc(sem("p1"), 1)
                m = n - 3
                if m >= 0 and m % NH == NH - 1:
                    b = m // NH
                    act.wait_ge(sem("av1"), (b + 1) * NH)
                    if b >= 2:
                        act.wait_ge(sem("turn1"), b - 1)
                    act.activation(CT1[:, b % 2, :], bank[4 + b % 2][:, :], ACT.Copy).then_inc(sem("ct1"), 1)

            def apply_act(s, src, half):
                act.wait_ge(sem("ln_nm"), 2 * ON_ACT.index((s, half)) + 2)
                for t in range(half * T // 2, (half + 1) * T // 2):
                    last = act.activation(XN[s][:, t, 0:C], src[:, t, :], ACT.Identity,
                                          bias=ln_nb[s][:, t:t + 1], scale=ln_rs[s][:, t:t + 1])
                    if t % TB == TB - 1:
                        last.then_inc(sem("xn_act"), 1)

            def attention_act(s, nm, dn, ct, width):
                for i in range(B + 6):
                    if i < B:
                        act.wait_ge(sem(s + "_xf_p"), i + 1)
                        act.activation(XF[s][0:C, i * N:i * N + N], bank[i % 2][0:C, 0:N], ACT.Copy) \
                            .then_inc(sem(s + "_xf"), 1)
                    if s == "c" and 0 <= i - 1 < B:
                        b = i - 1
                        act.wait_ge(sem("c_lhs_p"), b + 1)
                        act.activation(LHSc[:, b * N:b * N + N], bank[2 + b % 2][0:C1, 0:N], ACT.Copy) \
                            .then_inc(sem("c_lhs"), 1)
                    if 0 <= i - 2 < B:
                        b = i - 2
                        act.wait_ge(sem("att_nm"), through(s) + b + 1)
                        for q in range(TB):
                            t = TB * b + q
                            act.activation(S_P[:, b, q, :], bank[4 + b % 2][:, q * N:q * N + N], ACT.Exp,
                                           bias=nm[:, t:t + 1], scale=float(C) ** -0.5 if s == "a" else 1.0,
                                           accum_out=dn[:, t:t + 1]).then_inc(sem("att_exp"), 1)
                    if 0 <= i - 4 < B:
                        b = i - 4
                        act.wait_ge(sem("att_ct_p"), through(s) + b + 1)
                        act.activation(ct[:, b * N:b * N + N], bank[2 + b % 2][0:width, 0:N], ACT.Copy) \
                            .then_inc(sem("att_ct"), 1)
                    if s == "c" and 0 <= i - 5 < B:
                        b = i - 5
                        act.wait_ge(sem("gates"), b + 1)
                        g = bank[b % 2][:, 0:TB * 3 * C].rearrange("p (q f) -> p q f", q=TB)
                        t = slice(TB * b, TB * b + TB)
                        act.activation(th[:, t, 0:C], g[:, :, 0:C], ACT.Tanh).then_inc(sem("tanh"), 1)
                        act.activation(th[:, t, C:3 * C], g[:, :, C:3 * C], ACT.Tanh, scale=0.5) \
                            .then_inc(sem("tanh"), 1)

            attention_act("a", nmaxa, dena, CTa, C)
            apply_act("b", X3, 0)
            for b in range(B):
                act.wait_ge(sem("b_xf_p"), b + 1)
                act.activation(XF["b"][0:C, b * N:b * N + N], bank[b][0:C, 0:N], ACT.Copy, accum_out=msum[:, b:b + 1]) \
                    .then_inc(sem("b_xf"), 1)
            act.wait_ge(sem("r_nm"), 1)
            act.activation(lg[:, 0, :], bank[4][0:B, 0:E2], ACT.Exp, bias=col[:, 0:1], accum_out=col[:, 1:2]) \
                .then_inc(sem("r_exp"), 1)
            act.wait_ge(sem("r_nm"), 2)
            act.activation(lg[:, 4, :], lg[:, 3, :], ACT.Exp, bias=col[:, 3:4], accum_out=col[:, 4:5]) \
                .then_inc(sem("r_exp"), 1)
            act.wait_ge(sem("r_nm"), 3)
            act.activation(lg[:, 7, 0:TOPK], lg[:, 6, 0:TOPK], ACT.Exp, bias=col[:, 6:7], accum_out=col[:, 7:8]) \
                .then_inc(sem("r_exp"), 1)
            act.wait_ge(sem("pool_const"), 4)
            act.activation(table[:, :], mhalf[0:1, 0:1], ACT.Gelu).then_inc(sem("table"), 1)
            act.wait_ge(sem("slot_e"), 1)
            act.wait_ge(sem("r_spread_read"), 2)
            act.wait_ge(sem("w2a_landed"), 16)
            w2flat = W2A[:, :, :].rearrange("p e c -> p (e c)")
            for i in range(0, B * TOPK, TOPK):
                e = act.value_load(slot_e[0:1, i:i + 1], min_val=0, max_val=E2 - 1)
                act.activation(W1sel[:, i, :], WAs[:, bass.ds(e * F2, F2)], ACT.Copy).then_inc(sem("sel_a"), 1)
                act.activation(W2sel[:, i, :], w2flat[:, bass.ds(e * C, C)], ACT.Copy, scale=tw[:, i:i + 1]) \
                    .then_inc(sem("sel_a"), 1)
            for b in range(B):
                act.wait_ge(sem("up2"), b + 1)
                act.activation(H2[:, b, :], bank[b][:, :], ACT.Gelu).then_inc(sem("gelu"), 1)
            act.wait_ge(sem("table"), 1)
            act.activation(table[:, :], mhalf[0:1, 0:1], ACT.Exp)
            apply_act("u", U, 1)
            apply_act("c", X4, 0)
            attention_act("c", nmaxc, denc, CTc, C1)
            apply_act("d", X5, 0)
            for b in range(B):
                act.wait_ge(sem("d_xf_p"), b + 1)
                act.activation(XF["d"][0:C, b * N:b * N + N], bank[b][0:C, 0:N], ACT.Copy).then_inc(sem("d_xf"), 1)
            for b in range(B):
                normed(act, "d", b)
                act.activation(XHL[:, TB * b:TB * b + TB, 0, :], XN["d"][:, TB * b:TB * b + TB, 0:C], ACT.Copy) \
                    .then_inc(sem("xh"), 1)
            act.wait_ge(sem("d3"), 1)
            act.activation(ex3[:, :, :], d3[:, :, :], ACT.Exp).then_inc(sem("ex3"), 1)
            act.wait_ge(sem("sb_p"), 1)
            for h in range(2):
                act.activation(SB[:, h * 512:h * 512 + 512], bank[6 + h][:, :], ACT.Copy).then_inc(sem("sb"), 1)
            act.wait_ge(sem("gathered"), T)
            for c, at, width in ((0, 0, 512), (2, 1024, 256)):
                act.activation(XB[:, at:at + width], bank[c][:, 0:width], ACT.Copy).then_inc(sem("xb"), 1)

            def y_high(half):
                act.wait_ge(sem("y_turned"), half + 1)
                act.activation(YHL[:, half * HALF:(half + 1) * HALF, 0, :],
                               TURN_Y[half][:, 0:HALF * C].rearrange("p (j c) -> p j c", j=HALF), ACT.Copy) \
                    .then_inc(sem("yh"), 1)

            for e in range(E3 + 1):
                if e < E3:
                    act.wait_ge(sem("up3"), e + 1)
                    if e >= 3:
                        act.wait_ge(sem("down3"), e - 2)
                    act.activation(H3[:, e % 3, 0, :], UP3[0][e % 2][:, 0:CAP3], ACT.Relu,
                                   bias=Cs[:, CST["fb1"]][:, 2 * e:2 * e + 1]).then_inc(sem("h3"), 1)
                if e == 5:
                    y_high(0)
                if e >= 1:
                    f = e - 1
                    act.wait_ge(sem("down3"), f + 1)
                    act.activation(YT[:, f * CAP3:f * CAP3 + CAP3], bank[f % 2][0:C, 0:CAP3], ACT.Identity,
                                   bias=WAs[0:C, WA["fb2"]][:, f:f + 1]).then_inc(sem("yt"), 1)
            y_high(1)
            act.wait_ge(sem("scattered"), SLOTS // P)
            act.activation(ZT[:, 0:512], bank[6][:, :], ACT.Copy).then_inc(sem("zt"), 1)
            for h in range(2):
                t = slice(h * T // 2, (h + 1) * T // 2)
                act.wait_ge(sem("y3"), h + 1)
                act.activation(wild3[:, t, :], y3[:, t, :], ACT.Abs, scale=0.0).then_inc(sem("wild3"), 1)

        @block.vector
        def _(dve):
            steps = [0]

            def counted(ins):
                steps[0] += 1
                ins.then_inc(sem("vector_step"), 1)
                return steps[0]

            def then(ins):
                dve.wait_ge(sem("vector_step"), counted(ins))

            dve.memset(onesb[:, :], 1.0).then_inc(sem("onesb"), 1)
            dve.wait_ge(sem("onesb"), 1)
            dve.tensor_copy(onesf[:, :], onesb[:, :]).then_inc(sem("onesb"), 1)
            for b in range(B):
                dve.wait_ge(sem("xt_p"), b + 1)
                dve.tensor_copy(XT[0:C, b * N:b * N + N], bank[b][0:C, 0:N]).then_inc(sem("xt"), 1)
            dve.wait_ge(sem("wvo"), 1)
            dve.tensor_copy(Wvo[:, :], bank[7][0:C1, 0:C]).then_inc(sem("wvo_s"), 1)
            for i in range(B + 3):
                if i < B:
                    dve.wait_ge(sem("s0"), i + 1)
                    dve.tensor_reduce(nmax[:, TB * i:TB * i + TB],
                                      bank[4 + i % 2][:, :].rearrange("p (q k) -> p q k", q=TB),
                                      AX.X, ALU.max, negate=True).then_inc(sem("nm0"), 1)
                if 0 <= i - 1 < B:
                    b = i - 1
                    dve.wait_ge(sem("pt0_p"), b + 1)
                    dve.tensor_copy(S_PT[:, b, :, :].rearrange("p k q -> p (k q)"), bank[6 + b % 2][:, :]) \
                        .then_inc(sem("pt0"), 1)
                    dve.wait_ge(sem("exp0"), 2 * b + 2)
                    dve.reciprocal(rden[:, TB * b:TB * b + TB], den[:, TB * b:TB * b + TB]).then_inc(sem("rd0"), 1)
                if 0 <= i - 3 < B:
                    b = i - 3
                    dve.wait_ge(sem("o0"), b + 1)
                    dve.wait_ge(sem("rd0"), b + 1)
                    for q in range(TB):
                        t = TB * b + q
                        last = dve.scalar_tensor_tensor(
                            out=X1[:, t, :], in0=bank[b % 2][:, q * C:q * C + C], scalar=rden[:, t:t + 1],
                            in1=X[:, t, 0:C], op0=ALU.mult, op1=ALU.add)
                    last.then_inc(sem("x1"), 1)
            stats = []
            for b in range(B):
                dve.wait_ge(sem("x1t_p"), b + 1)
                stats.append(counted(dve.bn_stats(gn_st[:, b, :], bank[4 + b][0:C, 0:N])))
            for b in range(B):
                dve.wait_ge(sem("vector_step"), stats[b])
                last = counted(dve.bn_aggr(gn_mv[:, b, 0:2], gn_st[:, b, :]))
            dve.wait_ge(sem("vector_step"), last)
            dve.tensor_tensor(gn_mv[:, :, 2], gn_mv[:, :, 0], gn_mv[:, :, 0], ALU.mult).then_inc(sem("gn_step"), 1)
            dve.wait_ge(sem("gn_pair"), 1)
            then(dve.tensor_copy(gn_g[:, :, :].rearrange("c b k -> c (b k)"), bank[0][0:C, 0:3 * B]))
            then(dve.tensor_tensor(gn_sq[:, :], gn_g[:, :, 0], gn_g[:, :, 0], ALU.mult))
            then(dve.scalar_tensor_tensor(out=gn_v[:, :], in0=gn_g[:, :, 1], scalar=LN_EPS, in1=gn_g[:, :, 2],
                                          op0=ALU.add, op1=ALU.add))
            dve.tensor_tensor(gn_v[:, :], gn_v[:, :], gn_sq[:, :], ALU.subtract).then_inc(sem("gn_step"), 1)
            dve.wait_ge(sem("gn_rstd"), 1)
            dve.scalar_tensor_tensor(out=gn_nb[:, :], in0=gn_g[:, :, 0], scalar=-1.0, in1=gn_r[:, :],
                                     op0=ALU.mult, op1=ALU.mult).then_inc(sem("gn_step"), 1)
            dve.wait_ge(sem("gn_step"), 3)
            for b in (0, 2):
                dve.tensor_scalar(XN1[0:C, b * N:b * N + N], bank[4 + b][0:C, 0:N], gn_r[:, b:b + 1],
                                  gn_nb[:, b:b + 1], ALU.mult, ALU.add).then_inc(sem("xn1"), 1)
            for b in range(B):
                c = slice(b * N, b * N + N)
                if b == 0:
                    dve.wait_ge(sem("qk_p"), 1)
                    whole = bank[0][:, 0:N]
                else:
                    dve.wait_ge(sem("qkf"), b)
                    whole = QK[:, c]
                dve.tensor_copy(part[:, 0, c], whole).then_inc(sem("qk_part"), 1)
                dve.wait_ge(sem("qk_part"), 3 * b + 1)
                then(dve.tensor_tensor(qkr[:, c], whole, part[:, 0, c], ALU.subtract))
                dve.tensor_copy(part[:, 1, c], qkr[:, c]).then_inc(sem("qk_part"), 1)
                dve.wait_ge(sem("qk_part"), 3 * b + 2)
                dve.tensor_tensor(part[:, 2, c], qkr[:, c], part[:, 1, c], ALU.subtract).then_inc(sem("qk_part"), 1)

            def maxima(n):
                dve.wait_ge(sem("mx1"), n + 1)
                dve.tensor_reduce(nm1[:, n // NH, n % NH, :],
                                  bank[n % 2][:, 0:TB * SPAN].rearrange("p (q k) -> p q k", q=TB),
                                  AX.X, ALU.max, negate=True).then_inc(sem("nm1"), 1)

            def biased(n):
                dve.wait_ge(sem("s1"), n + 1)
                if n == 0:
                    dve.wait_ge(sem("biasK_landed"), 16)
                if n >= 3:
                    dve.wait_ge(sem("p1"), n - 2)
                dve.tensor_tensor(U1[:, n % 3, :], bank[2 + n % 2][:, 0:TB * SPAN], biasK[:, n % NH, :], ALU.add) \
                    .then_inc(sem("u1"), 1)

            def finish1_reciprocal(b):
                dve.wait_ge(sem("turn1"), b + 1)
                v = bank[6][:, :].rearrange("p (j g w) -> p j g w", j=2 * TB, g=4)
                counted(dve.reciprocal(rz1[:, b % 2, :, :], v[:, :, :, HD]))

            def finish1_divide(b):
                v = bank[6][:, :].rearrange("p (j g w) -> p j g w", j=2 * TB, g=4)
                dve.wait_ge(sem("vector_step"), steps[0])
                dve.tensor_tensor(ctx1[:, b % 2, :, :, :], v[:, :, :, 0:HD],
                                  rz1[:, b % 2, :, :].unsqueeze(3).to_broadcast([P, 2 * TB, 4, HD]), ALU.mult) \
                    .then_inc(sem("ctx1"), 1)

            def finish1_add(b):
                dve.wait_ge(sem("ctx1"), b + 1)
                dve.tensor_tensor(X2[:, TB * b:TB * b + TB, :].rearrange("p q c -> p (q c)"),
                                  ctx1[:, b % 2, :, :, :].rearrange("p j g d -> p (j g d)"),
                                  X1[:, TB * b:TB * b + TB, :].rearrange("p q c -> p (q c)"), ALU.add) \
                    .then_inc(sem("x2_done"), 1)

            def blocks_of(s, k):
                n = LN_STEPS.index((s, k * T // 2, T // 2) if s != "a" else (s, TB * k, TB))
                first, blocks = LN_STEPS[n][1:]
                return range(first, first + blocks), n + 1

            def moments(s, src, ready, count, k):
                dve.wait_ge(sem(ready), count)
                for t in blocks_of(s, k)[0]:
                    last = dve.bn_stats(ln_st[s][:, t, :], src[:, t, :])
                counted(last)

            def aggregate(s, k):
                dve.wait_ge(sem("vector_step"), steps[0])
                for t in blocks_of(s, k)[0]:
                    last = dve.bn_aggr(ln_mv[s][:, t, :], ln_st[s][:, t, :])
                last.then_inc(sem("ln_mv"), 1)

            def stats(s, src, ready, count, k):
                moments(s, src, ready, count, k)
                aggregate(s, k)

            def apply(s, src, k):
                blocks, n = blocks_of(s, k)
                dve.wait_ge(sem("ln_mv"), n)
                dve.wait_ge(sem("ln_rs"), n)
                for t in blocks:
                    last = dve.tensor_scalar(XN[s][:, t, 0:C], src[:, t, :], ln_mv[s][:, t, 0:1], ln_rs[s][:, t:t + 1],
                                             ALU.subtract, ALU.mult)
                    if t % TB == TB - 1:
                        last.then_inc(sem(s + "_xn"), 1)

            for n in range(AHEAD):
                maxima(n)
            for n in range(B * NH + 5):
                if n + AHEAD < B * NH:
                    maxima(n + AHEAD)
                if n < B * NH and n % NH not in PE_HEADS:
                    biased(n)
                b, step = (n - 4) // NH - 1, (n - 4) % NH
                if b >= 0:
                    if step == 2:
                        finish1_reciprocal(b)
                    if step == 3:
                        finish1_divide(b)
                    if step == 4:
                        finish1_add(b)
                    if step == 5:
                        moments("a", X2, "x2_done", b + 1, b)
                    if step == 6:
                        aggregate("a", b)
                    if step == 0 and b >= 1:
                        apply("a", X2, b - 1)
            finish1_reciprocal(B - 1)
            finish1_divide(B - 1)
            finish1_add(B - 1)
            stats("a", X2, "x2_done", B, B - 1)

            def maxima_of(s, b, nm):
                dve.wait_ge(sem("att_s"), through(s) + b + 1)
                t = slice(TB * b, TB * b + TB)
                rows = bank[4 + b % 2][:, :].rearrange("p (q k) -> p q k", q=TB)
                if s == "a":
                    then(dve.tensor_reduce(nm[:, t], rows, AX.X, ALU.max, negate=True))
                    dve.tensor_scalar(nm[:, t], nm[:, t], float(C) ** -0.5, None, ALU.mult) \
                        .then_inc(sem("att_nm"), 1)
                else:
                    dve.tensor_reduce(nm[:, t], rows, AX.X, ALU.max, negate=True).then_inc(sem("att_nm"), 1)

            def x3_of(b):
                dve.wait_ge(sem("a_turned"), b + 1)
                for q in range(TB):
                    t = TB * b + q
                    last = dve.scalar_tensor_tensor(
                        out=X3[:, t, :], in0=bank[b % 2][:, q * C:q * C + C], scalar=rdena[:, t:t + 1],
                        in1=X2[:, t, :], op0=ALU.mult, op1=ALU.add)
                last.then_inc(sem("x3"), 1)

            def turned_p(s, b):
                dve.wait_ge(sem("att_pt_p"), through(s) + b + 1)
                dve.tensor_copy(S_PT[:, b, :, :].rearrange("p k q -> p (k q)"), bank[6 + b % 2][:, :]) \
                    .then_inc(sem("att_pt"), 1)

            for i in range(2, B + 4):
                if 0 <= i - 2 < B:
                    b = i - 2
                    maxima_of("a", b, nmaxa)
                    if b == 0:
                        apply("a", X2, B - 1)
                if 0 <= i - 3 < B:
                    b = i - 3
                    turned_p("a", b)
                    dve.wait_ge(sem("att_exp"), 2 * b + 2)
                    then(dve.reciprocal(rdena[:, TB * b:TB * b + TB], dena[:, TB * b:TB * b + TB]))
                if 0 <= i - 5 < B:
                    x3_of(i - 5)
            stats("b", X3, "x3", B // 2, 0)
            x3_of(B - 1)
            stats("b", X3, "x3", B, 1)
            apply("b", X3, 1)

            dve.wait_ge(sem("b_xf"), B)
            dve.tensor_scalar(mean2[0:C, :], msum[:, :], 1.0 / N, None, ALU.mult).then_inc(sem("mean2"), 1)
            dve.wait_ge(sem("r_logits"), 1)
            dve.tensor_reduce(col[:, 0:1], bank[4][0:B, 0:E2], AX.X, ALU.max, negate=True).then_inc(sem("r_nm"), 1)
            dve.wait_ge(sem("r_exp"), 1)
            then(dve.reciprocal(col[:, 2:3], col[:, 1:2]))
            dve.tensor_scalar(lg[:, 1, :], lg[:, 0, :], col[:, 2:3], None, ALU.mult).then_inc(sem("r_rw"), 1)
            dve.wait_ge(sem("r_loads"), 1)
            then(dve.reciprocal(lg[:, 2, :], bank[5][0:B, 0:E2]))
            then(dve.tensor_scalar(lg[:, 2, :], lg[:, 2, :], CAP2, 1.0, ALU.mult, ALU.min))
            dve.wait_ge(sem("r_rw"), 1)
            then(dve.tensor_tensor(lg[:, 3, :], lg[:, 2, :], lg[:, 1, :], ALU.mult))
            dve.tensor_reduce(col[:, 3:4], lg[:, 3, :], AX.X, ALU.max, negate=True).then_inc(sem("r_nm"), 1)
            dve.wait_ge(sem("r_exp"), 2)
            then(dve.reciprocal(col[:, 5:6], col[:, 4:5]))
            then(dve.tensor_scalar(lg[:, 5, :], lg[:, 4, :], col[:, 5:6], None, ALU.mult))
            then(dve.max(lg[:, 6, :], lg[:, 5, :]))
            dve.tensor_scalar(col[:, 6:7], lg[:, 6, 0:1], -1.0, None, ALU.mult).then_inc(sem("r_nm"), 1)
            then(dve.max_index(top_i[:, :], lg[:, 6, :], lg[:, 5, :]))
            id4 = ident[0:B, 0:B].unsqueeze(2).to_broadcast([B, B, TOPK])
            dve.tensor_tensor(spread[:, 1, :, :], top_i[:, 0:TOPK].unsqueeze(1).to_broadcast([B, B, TOPK]), id4,
                              ALU.mult).then_inc(sem("r_spread"), 1)
            dve.wait_ge(sem("r_exp"), 3)
            then(dve.reciprocal(col[:, 8:9], col[:, 7:8]))
            then(dve.tensor_scalar(lg[:, 7, 4:4 + TOPK], lg[:, 7, 0:TOPK], col[:, 8:9], None, ALU.mult))
            dve.tensor_tensor(spread[:, 0, :, :], lg[:, 7, 4:4 + TOPK].unsqueeze(1).to_broadcast([B, B, TOPK]), id4,
                              ALU.mult).then_inc(sem("r_spread"), 1)
            dve.wait_ge(sem("r_bcast"), 1)
            dve.tensor_copy(slot_e[:, :], bank[6][0:1, B * TOPK:2 * B * TOPK]).then_inc(sem("slot_e"), 1)
            dve.tensor_copy(tw[:, :], bank[6][:, 0:B * TOPK]).then_inc(sem("r_spread_read"), 1)
            dve.tensor_copy(chosen[:, :], bank[6][:, B * TOPK:2 * B * TOPK]).then_inc(sem("r_spread_read"), 1)
            dve.wait_ge(sem("slot_e"), 1)
            dve.wait_ge(sem("r_spread_read"), 2)
            dve.wait_ge(sem("w2a_landed"), 16)
            w2flat = W2A[:, :, :].rearrange("p e c -> p (e c)")
            for i in range(1, B * TOPK, TOPK):
                e = dve.value_load(slot_e[0:1, i:i + 1], min_val=0, max_val=E2 - 1)
                dve.tensor_copy(W1sel[:, i, :], WAs[:, bass.ds(e * F2, F2)]).then_inc(sem("sel_v"), 1)
                dve.tensor_scalar(W2sel[:, i, :], w2flat[:, bass.ds(e * C, C)], tw[:, i:i + 1], None, ALU.mult) \
                    .then_inc(sem("sel_v"), 1)
            cube = [C, B * TOPK, E2]
            e_no = Cs[0:C, CST["expert"]].rearrange("p (i e) -> p i e", i=B * TOPK)
            then(dve.tensor_tensor(b2w[:, :, :], e_no, chosen[0:C, :].unsqueeze(2).to_broadcast(cube), ALU.is_equal))
            then(dve.tensor_tensor(b2w[:, :, :], b2w[:, :, :], tw[0:C, :].unsqueeze(2).to_broadcast(cube), ALU.mult))
            then(dve.tensor_tensor(b2w[:, :, :], b2w[:, :, :], WAs[0:C, WA["b2"]].unsqueeze(1).to_broadcast(cube),
                                   ALU.mult))
            dve.tensor_reduce(b2sel[:, :], b2w[:, :, :].rearrange("p (b k) e -> p b (k e)", b=B), AX.X, ALU.add) \
                .then_inc(sem("b2sel"), 1)
            for i in range(B + 1):
                if i < B:
                    b = i
                    dve.wait_ge(sem("down2"), b + 1)
                    dve.wait_ge(sem("b2sel"), 1)
                    dve.tensor_scalar(UT[:, b * N:b * N + N], bank[4 + b % 2][0:C, 0:N], b2sel[:, b:b + 1],
                                      None, ALU.add) \
                        .then_inc(sem("ut"), 1)
                if i >= 1:
                    b = i - 1
                    dve.wait_ge(sem("u_turned"), b + 1)
                    dve.tensor_tensor(U[:, TB * b:TB * b + TB, :],
                                      bank[6 + b % 2][:, 0:TB * C].rearrange("p (q c) -> p q c", q=TB),
                                      XN["b"][:, TB * b:TB * b + TB, 0:C], ALU.add).then_inc(sem("u"), 1)
                if i == B - 1:
                    stats("u", U, "u", B // 2, 0)

            def x4_of(half):
                t = slice(half * T // 2, (half + 1) * T // 2)
                wide = [P, T // 2, C]
                if half == 0:
                    apply("u", U, half)
                normed(dve, "u", B // 2 * (half + 1) - 1)
                then(dve.tensor_tensor(un[:, t, :], XN["u"][:, t, 0:C], gb[:, 0, :].unsqueeze(1).to_broadcast(wide),
                                       ALU.mult))
                dve.tensor_tensor(X4[:, t, :], un[:, t, :], X3b[:, t, :], ALU.add).then_inc(sem("x4"), 1)

            stats("u", U, "u", B, 1)
            dve.wait_ge(sem("gb_landed"), 16)
            dve.wait_ge(sem("x3b"), 1)
            for half in range(2):
                x4_of(half)
                stats("c", X4, "x4", half + 1, half)
            apply("c", X4, 1)

            def x5_of(b):
                t = slice(TB * b, TB * b + TB)
                dve.wait_ge(sem("tanh"), 2 * b + 2)
                dve.scalar_tensor_tensor(out=gm[:, t, 0:C], in0=th[:, t, C:2 * C], scalar=1.0,
                                         in1=XN["c"][:, t, 0:C], op0=ALU.add, op1=ALU.mult)
                then(dve.scalar_tensor_tensor(out=gm[:, t, C:2 * C], in0=th[:, t, 2 * C:3 * C], scalar=1.0,
                                              in1=th[:, t, 0:C], op0=ALU.add, op1=ALU.mult))
                then(dve.tensor_tensor(gs[:, t, :], gm[:, t, 0:C], gm[:, t, C:2 * C], ALU.add))
                dve.scalar_tensor_tensor(out=X5[:, t, :], in0=gs[:, t, :], scalar=0.5, in1=X4[:, t, :],
                                         op0=ALU.mult, op1=ALU.add).then_inc(sem("x5"), 1)

            for i in range(2, B + 5):
                if i - 2 < B:
                    maxima_of("c", i - 2, nmaxc)
                if 0 <= i - 3 < B:
                    turned_p("c", i - 3)
                if i >= 6:
                    x5_of(i - 6)
                if i - 2 < B:
                    b = i - 2
                    dve.wait_ge(sem("att_exp"), 2 * b + 2 + 2 * B)
                    then(dve.reciprocal(rdenc[:, TB * b:TB * b + TB], denc[:, TB * b:TB * b + TB]))
                    for q in range(TB):
                        t = TB * b + q
                        dve.tensor_scalar(S_P[:, b, q, :], S_P[:, b, q, :], rdenc[:, t:t + 1], None, ALU.mult) \
                            .then_inc(sem("c_pn"), 1)
            stats("d", X5, "x5", B // 2, 0)
            x5_of(B - 1)
            stats("d", X5, "x5", B, 1)
            apply("d", X5, 1)

            def per_expert(v):
                return v.unsqueeze(2).to_broadcast([P, T, E3])

            rows = bank[4][:, 0:T * E3].rearrange("p (t e) -> p t e", t=T)
            cnt = bank[5][:, 0:T * E3].rearrange("p (t e) -> p t e", t=T)
            dve.wait_ge(sem("logits3"), 1)
            then(dve.tensor_reduce(mx3[:, :], rows, AX.X, ALU.max))
            dve.tensor_tensor(d3[:, :, :], rows, per_expert(mx3[:, :]), ALU.subtract).then_inc(sem("d3"), 1)
            dve.wait_ge(sem("d3"), 1)
            rev = Cs[:, CST["rev"]].rearrange("p (t e) -> p t e", t=T)
            first = Cs[:, CST["first"]].rearrange("p (t e) -> p t e", t=T)
            then(dve.scalar_tensor_tensor(out=rv3[:, :, :], in0=d3[:, :, :], scalar=0.0, in1=rev,
                                          op0=ALU.is_equal, op1=ALU.mult))
            then(dve.tensor_reduce(mr3[:, :], rv3[:, :, :], AX.X, ALU.max))
            dve.tensor_tensor(ohb[:, :, :], rv3[:, :, :], per_expert(mr3[:, :]), ALU.is_equal) \
                .then_inc(sem("ohb"), 1)
            dve.wait_ge(sem("ohb"), 1)
            counted(dve.tensor_tensor(sel3[:, :, 1, :], ohb[:, :, :], first, ALU.mult))
            dve.wait_ge(sem("xh"), B)
            dve.tensor_tensor(XHL[:, :, 1, :], XN["d"][:, :, 0:C], XHL[:, :, 0, :].bitcast(F32), ALU.subtract) \
                .then_inc(sem("xl"), 1)
            dve.tensor_copy(twice[:, :], Cs[:, CST["twice"]]).then_inc(sem("xl"), 1)

            dve.wait_ge(sem("counts"), 1)
            then(dve.tensor_tensor(sel3[:, :, 0, :], ohb[:, :, :], cnt, ALU.mult))
            counted(dve.tensor_reduce(number[:, :], sel3[:, :, 0, :], AX.X, ALU.add))
            then(dve.tensor_reduce(sid[:, :], sel3[:, :, :, :].rearrange("p t k e -> p t (k e)"), AX.X, ALU.add))
            dve.scalar_tensor_tensor(out=sid[:, :], in0=number[:, :], scalar=float(CAP3), in1=sid[:, :],
                                     op0=ALU.is_le, op1=ALU.mult).then_inc(sem("sid"), 1)
            dve.wait_ge(sem("sid"), 1)
            dve.wait_ge(sem("later_const"), 8)
            for t in range(T):
                if t >= 3:
                    dve.wait_ge(sem("gathered"), t - 2)
                dve.tensor_scalar(G3[:, t % 3, :], iota_f[:, :], sid[:, t:t + 1], None, ALU.is_equal) \
                    .then_inc(sem("g3"), 1)
            dve.wait_ge(sem("ex3"), 1)
            then(dve.tensor_reduce(se3[:, :], ex3[:, :, :], AX.X, ALU.add))
            then(dve.reciprocal(prb[:, :], se3[:, :]))
            then(dve.scalar_tensor_tensor(out=gate3[:, :], in0=number[:, :], scalar=float(CAP3), in1=prb[:, :],
                                          op0=ALU.is_le, op1=ALU.mult))
            dve.wait_ge(sem("gathered"), T)
            dve.tensor_copy(XB[:, 512:1024], bank[1][:, :]).then_inc(sem("xb_v"), 1)
            dve.wait_ge(sem("sb"), 2)
            slot_no = Cs[:, CST["slot"]]

            def one_hot_slots(j):
                if j >= 4:
                    dve.wait_ge(sem("scattered"), j - 3)
                dve.tensor_scalar(GT[:, j % 4, :], SB[:, :], slot_no[:, j:j + 1], None, ALU.is_equal) \
                    .then_inc(sem("gt"), 1)

            def y_low(half):
                j = slice(half * HALF, (half + 1) * HALF)
                dve.wait_ge(sem("yh"), half + 1)
                dve.tensor_tensor(YHL[:, j, 1, :], TURN_Y[half][:, 0:HALF * C].rearrange("p (j c) -> p j c", j=HALF),
                                  YHL[:, j, 0, :].bitcast(F32), ALU.subtract).then_inc(sem("yl"), 1)

            for e in range(E3):
                dve.wait_ge(sem("up3"), e + 1)
                if e >= 3:
                    dve.wait_ge(sem("down3"), e - 2)
                dve.tensor_scalar(H3[:, e % 3, 1, :], UP3[1][e % 2][:, 0:CAP3],
                                  Cs[:, CST["fb1"]][:, 2 * e + 1:2 * e + 2], 0.0, ALU.add, ALU.max).then_inc(sem("h3_v"), 1)
                if e < 4:
                    one_hot_slots(e)
                if e == 5:
                    y_low(0)
            for j in range(4, 8):
                one_hot_slots(j)
            y_low(1)
            for j in range(8, 2 * HALF):
                one_hot_slots(j)
            dve.wait_ge(sem("scattered"), SLOTS // P)
            dve.tensor_copy(ZT[:, 512:1024], bank[7][:, :]).then_inc(sem("zt_v"), 1)
            halves = [slice(h * T // 2, (h + 1) * T // 2) for h in range(2)]
            for h, t in enumerate(halves):
                dve.wait_ge(sem("z_turned"), h + 1)
                dve.tensor_tensor(y3[:, t, :], bank[h][:, 0:T // 2 * C].rearrange("p (q c) -> p q c", q=T // 2),
                                  gate3[:, t].unsqueeze(2).to_broadcast([P, T // 2, C]), ALU.mult).then_inc(sem("y3"), 1)
            for h, t in enumerate(halves):
                dve.wait_ge(sem("y3"), h + 1)
                then(dve.tensor_tensor(nan3[:, t, :], y3[:, t, :], y3[:, t, :], ALU.is_equal))
                then(dve.scalar_tensor_tensor(out=sat3[:, t, :], in0=y3[:, t, :], scalar=1e4, in1=nan3[:, t, :],
                                              op0=ALU.min, op1=ALU.mult))
                then(dve.scalar_tensor_tensor(out=sat3[:, t, :], in0=sat3[:, t, :], scalar=-1e4, in1=X5[:, t, :],
                                              op0=ALU.max, op1=ALU.add))
                dve.wait_ge(sem("wild3"), h + 1)
                dve.wait_ge(sem("sum3"), h + 1)
                dve.copy_predicated(Y6[:, t, :], wild3[:, t, :].bitcast(I32), sat3[:, t, :]).then_inc(sem("y6"), TB)


def pack(pairs, where, rows, width):
    a = np.zeros((rows, width), np.float32)
    for name, value in pairs.items():
        a[:value.shape[0], where[name]] = value
    return a


def with_bias(w, b):
    return np.concatenate([w, b[None, :]], 0)


def feature_head(w):
    return w.reshape(*w.shape[:-1], NH, HD).swapaxes(-1, -2).reshape(w.shape)


def bias_tables(rpb):
    q = np.full((P, NH, TB, SPAN), MASKED, np.float32)
    k = np.full((P, NH, TB, SPAN), MASKED, np.float32)
    start = np.array([window_start(i) for i in range(HW)])
    n = np.arange(N)
    i, j = n // HW, n % HW
    ok = (i[None] >= start[i][:, None]) & (i[None] < start[i][:, None] + WIN) & \
         (j[None] >= start[j][:, None]) & (j[None] < start[j][:, None] + WIN)
    full = np.full((NH, N, N), MASKED, np.float32)
    qi, ki = np.nonzero(ok)
    full[:, qi, ki] = rpb[:, i[ki] - i[qi] + WIN - 1, j[ki] - j[qi] + WIN - 1]
    for s in range(TB):
        q[:, :, s, :] = full[:, s * P:s * P + P, OFF[s]:OFF[s] + SPAN].transpose(1, 0, 2)
        k[:, :, s, :] = full[:, OFF[s]:OFF[s] + SPAN, s * P:s * P + P].transpose(2, 0, 1)
    return q.reshape(P, NH, TB * SPAN), k.reshape(P, NH, TB * SPAN)


def kernel(**inputs):
    import concourse.bacc as bacc
    from concourse.bass_utils import run_bass_kernel_spmd

    a = {k: np.ascontiguousarray(np.asarray(v)) for k, v in inputs.items()}
    p = np.arange(P)
    pair = np.zeros((C, C), np.float32)
    for c in range(C):
        pair[c, c // 2 * 2:c // 2 * 2 + 2] = 0.5
    cst = pack({
        "ident": np.eye(P, dtype=np.float32),
        "prefix": (p[:, None] <= p[None]).astype(np.float32),
        "pair": pair,
        "rev": np.tile(np.arange(E3, 0, -1, dtype=np.float32), (P, T)),
        "first": np.tile(np.arange(E3, dtype=np.float32) * CAP3, (P, T)),
        "expert": np.tile(np.arange(E3, dtype=np.float32), (P, T)),
        "fb1": a["L3_ffn_b1"].reshape(E3, 2, P).transpose(2, 0, 1).reshape(P, E3 * 2),
        "twice": np.tile(np.eye(C, dtype=np.float32), (2, 1)),
        "slot": (1 + p[:, None] + P * np.arange(10)[None]).astype(np.float32),
    }, CST, P, CST_W)
    w8 = np.concatenate([with_bias(a["L0_conv_wq"], a["L0_conv_bq"]).T,
                         with_bias(a["L0_conv_wk"], a["L0_conv_bk"]).T], 1)
    wvT = np.zeros((C1, C1), np.float32)
    wvT[:C] = with_bias(a["L0_conv_wv"], a["L0_conv_bv"]).T
    wvT[C, C] = 1.0
    w0 = pack({
        "wvT": wvT, "wo": with_bias(a["L0_conv_wo"], a["L0_conv_bo"]),
        "wqk1": with_bias(np.concatenate([feature_head(a["L1_conv_wq"].T), feature_head(a["L1_conv_wk"].T)], 1),
                          np.concatenate([feature_head(a["L1_conv_bq"]), feature_head(a["L1_conv_bk"])])),
        "wv1": with_bias(a["L1_conv_wv"].T, a["L1_conv_bv"]),
    }, W0, C1, W0_W)
    bias_q, bias_k = bias_tables(a["L1_conv_rpb"])
    att = a["L3_attn_att_w"]
    y3 = np.zeros((C1, C1), np.float32)
    y3[np.arange(C), np.arange(C)] = att[2 * C:]
    y3[C, :C] = att[C:2 * C]
    y3[:C, C] = att[:C]
    gw = np.concatenate([a["L3_attn_z_w"], a["L3_attn_r_w"], a["L3_attn_f_w"]], 0)
    gbias = np.concatenate([a["L3_attn_z_b"], a["L3_attn_r_b"], a["L3_attn_f_b"]])
    wa = pack({
        "w1": np.concatenate([a["L2_ffn_W1"].transpose(1, 0, 2).reshape(C, E2 * F2),
                              a["L2_ffn_b1"].reshape(1, E2 * F2)]),
        "wr": with_bias(a["L2_ffn_Wr"], a["L2_ffn_br"]),
        "b2": a["L2_ffn_b2"].T,
        "y3": y3,
        "gx": with_bias(gw[:, :C].T, gbias),
        "ga": gw[:, C:].T,
        "gate": with_bias(a["L3_ffn_gate_w"], a["L3_ffn_gate_b"]),
        "fb2": a["L3_ffn_b2"].T,
    }, WA, C1, WA_W)
    arrays = {
        "x": a["x"].reshape(B, N, C), "w8": w8, "w0": w0, "wa": wa,
        "w3": np.tile(a["L3_ffn_w1"].transpose(1, 0, 2), (2, 1, 1)),
        "w2a": a["L2_ffn_W2"].transpose(1, 0, 2),
        "w2b": a["L3_ffn_w2"].reshape(E3, 2, P, C).transpose(2, 0, 1, 3),
        "cst": cst, "bias_q": bias_q, "bias_k": bias_k,
        "lnw": np.stack([a["L2_ffn_gamma"], a["L2_ffn_beta"]]),
    }
    arrays = {k: np.ascontiguousarray(v) for k, v in arrays.items()}
    nc = bacc.Bacc("TRN2", target_bir_lowering=False, num_devices=1)
    args = {n: nc.dram_tensor(n, v.shape, F32, kind="ExternalInput").ap() for n, v in arrays.items()}
    args["out"] = nc.dram_tensor("out", (B, N, C), F32, kind="ExternalOutput").ap()
    hybrid_kernel(nc, **args)
    r = run_bass_kernel_spmd(nc, [arrays], core_ids=[0])
    return r.results[0]["out"].reshape(B, HW, HW, C)
```
